# Optimizing a Trainium2 kernel written in Bass

```python
import numpy as np
import jax
import jax.numpy as jnp

def _softmax(x, axis=-1):
    return jax.nn.softmax(x, axis=axis)

def _gelu(x):
    return jax.nn.gelu(x, approximate=True)

def _silu(x):
    return jax.nn.silu(x)

def _sigmoid(x):
    return jax.nn.sigmoid(x)

def _layernorm(x, axis=-1, eps=1e-05):
    m = jnp.mean(x, axis=axis, keepdims=True)
    v = jnp.var(x, axis=axis, keepdims=True)
    return (x - m) / jnp.sqrt(v + eps)

def _scatter_add(tgt, idx, src, axis=0):
    return tgt.at[idx].add(src)

def _segment_sum(src, seg, n):
    return jax.ops.segment_sum(src, seg, n)
kernel_name = 'mk_prb_d2_jaxref_r4_2d12f4'

def setup_inputs(seed: int=0):
    np.random.seed(seed)
    _w = jnp.asarray

    def _L0_attn_setup():
        import jax, jax.numpy as jnp
        import numpy as np
        HIDDEN = 512
        NUM_HEADS = 16
        HEAD_SIZE = HIDDEN // NUM_HEADS
        SEQ = 512
        BATCH = 2

        def alibi_causal_bias(seq_len: int, num_heads: int) -> jnp.ndarray:
            i = jnp.arange(seq_len)[:, None]
            j = jnp.arange(seq_len)[None, :]
            dist = -(i - j).astype(jnp.float32)
            causal = jnp.where(j > i, -jnp.inf, 0.0)
            base = jnp.where(j > i, 0.0, dist) + causal
            if num_heads <= 8:
                slopes = jnp.asarray([1.0 / 2 ** k for k in range(num_heads)], jnp.float32)
            else:
                slopes = jnp.asarray([1.0 / 2 ** (k / 2) for k in range(num_heads)], jnp.float32)
            return slopes[None, :, None, None] * dist[None, None] * (j <= i)[None, None] + causal[None, None]
        key = jax.random.key(seed)
        ks = jax.random.split(key, 3)
        sd = 1.0 / np.sqrt(HIDDEN)
        return {'x': jax.random.normal(ks[0], (BATCH, SEQ, HIDDEN), jnp.float32), 'Wqkv': jax.random.normal(ks[1], (HIDDEN, 3 * HIDDEN), jnp.float32) * sd, 'bqkv': jnp.zeros((3 * HIDDEN,), jnp.float32), 'Wo': jax.random.normal(ks[2], (HIDDEN, HIDDEN), jnp.float32) * sd, 'bo': jnp.zeros((HIDDEN,), jnp.float32)}
    _L0_attn_in = _L0_attn_setup()

    def _L0_ffn_setup():
        import jax, jax.numpy as jnp
        import numpy as np
        H = 512
        key = jax.random.key(seed)
        ks = jax.random.split(key, 10)
        s = 1.0 / np.sqrt(H)
        x = jax.random.normal(ks[0], (4, 512, H), dtype=jnp.float32)
        Wg = jax.random.uniform(ks[1], (2, H), jnp.float32, -s, s)
        W0a = jax.random.uniform(ks[2], (2 * H, H), jnp.float32, -s, s)
        b0a = jax.random.uniform(ks[3], (2 * H,), jnp.float32, -s, s)
        W0b = jax.random.uniform(ks[4], (H, 2 * H), jnp.float32, -s, s)
        b0b = jax.random.uniform(ks[5], (H,), jnp.float32, -s, s)
        W1a = jax.random.uniform(ks[6], (2 * H, H), jnp.float32, -s, s)
        b1a = jax.random.uniform(ks[7], (2 * H,), jnp.float32, -s, s)
        W1b = jax.random.uniform(ks[8], (H, 2 * H), jnp.float32, -s, s)
        b1b = jax.random.uniform(ks[9], (H,), jnp.float32, -s, s)
        return {'x': x, 'Wg': Wg, 'W0a': W0a, 'b0a': b0a, 'W0b': W0b, 'b0b': b0b, 'W1a': W1a, 'b1a': b1a, 'W1b': W1b, 'b1b': b1b}
    _L0_ffn_in = _L0_ffn_setup()

    def _L1_attn_setup():
        import jax, jax.numpy as jnp
        import numpy as np
        EPS = 1e-05
        CHUNK = 128

        def lightning_attn(q, k, v, ld, chunk=CHUNK):
            b, n, h, d = q.shape
            nc = n // chunk
            idx = jnp.arange(chunk)
            diff = idx[:, None] - idx[None, :]
            mask = diff >= 0
            D = jnp.exp(ld[:, None, None] * jnp.where(mask, diff, 0)) * mask
            q_decay = jnp.exp(ld[None, :] * (idx + 1)[:, None])
            k_decay = jnp.exp(ld[None, :] * (chunk - 1 - idx)[:, None])
            chunk_decay = jnp.exp(ld * chunk)
            qc = jnp.moveaxis(q.reshape(b, nc, chunk, h, d), 1, 0)
            kc = jnp.moveaxis(k.reshape(b, nc, chunk, h, d), 1, 0)
            vc = jnp.moveaxis(v.reshape(b, nc, chunk, h, d), 1, 0)

            def step(S, inp):
                qb, kb, vb = inp
                scores = jnp.einsum('bchd,bshd->bhcs', qb, kb) * D[None]
                o_intra = jnp.einsum('bhcs,bshd->bchd', scores, vb)
                o_inter = jnp.einsum('bchd,bhde->bche', qb, S) * q_decay[None, :, :, None]
                S_new = chunk_decay[None, :, None, None] * S + jnp.einsum('bshd,bshe->bhde', kb * k_decay[None, :, :, None], vb)
                return (S_new, o_intra + o_inter)
            S0 = jnp.zeros((b, h, d, d), dtype=q.dtype)
            S_final, oc = jax.lax.scan(step, S0, (qc, kc, vc))
            out = jnp.moveaxis(oc, 0, 1).reshape(b, n, h, d)
            return (out, S_final)

        def group_rmsnorm_fused_gate(o, gate, w, num_heads):
            b, n, d = o.shape
            hd = d // num_heads
            o = o * jax.nn.sigmoid(gate)
            og = o.reshape(b, n, num_heads, hd)
            og = og * jax.lax.rsqrt(jnp.mean(og * og, axis=-1, keepdims=True) + EPS)
            return og.reshape(b, n, d) * w
        key = jax.random.key(seed)
        ks = jax.random.split(key, 10)
        B, N, D, H = (2, 1024, 512, 16)
        HD = D // H
        s = 1.0 / np.sqrt(D)
        x = jax.random.normal(ks[0], (B, N, D), dtype=jnp.float32)
        log_decay = -jax.random.uniform(ks[1], (H,), dtype=jnp.float32, minval=0.01, maxval=1.0)
        Wq = jax.random.normal(ks[2], (D, D), dtype=jnp.float32) * s
        Wk = jax.random.normal(ks[3], (D, D), dtype=jnp.float32) * s
        Wv = jax.random.normal(ks[4], (D, D), dtype=jnp.float32) * s
        Wo = jax.random.normal(ks[5], (D, D), dtype=jnp.float32) * s
        Wg1 = jax.random.normal(ks[6], (D, HD), dtype=jnp.float32) * s
        Wg2 = jax.random.normal(ks[7], (HD, D), dtype=jnp.float32) / np.sqrt(HD)
        norm_w = jnp.ones((D,), dtype=jnp.float32)
        return {'x': x, 'log_decay': log_decay, 'Wq': Wq, 'Wk': Wk, 'Wv': Wv, 'Wo': Wo, 'Wg1': Wg1, 'Wg2': Wg2, 'norm_w': norm_w}
    _L1_attn_in = _L1_attn_setup()

    def _L1_ffn_setup():
        import jax, jax.numpy as jnp
        import numpy as np
        EPS = 1e-08

        def _quantize(w):
            gamma = jnp.mean(jnp.abs(w))
            return jnp.clip(jnp.round(w / (gamma + EPS)), -1.0, 1.0)

        def _bitlinear(x, w):
            return jnp.matmul(x, _quantize(w).T)
        key = jax.random.key(seed)
        k1, k2, k3, k4 = jax.random.split(key, 4)
        d, h = (512, 1408)
        x = jax.random.normal(k1, (4, 512, d), dtype=jnp.float32)
        w1 = jax.random.normal(k2, (h, d), dtype=jnp.float32)
        w2 = jax.random.normal(k3, (h, d), dtype=jnp.float32)
        w3 = jax.random.normal(k4, (d, h), dtype=jnp.float32)
        return {'x': x, 'w1': w1, 'w2': w2, 'w3': w3}
    _L1_ffn_in = _L1_ffn_setup()
    _d = {'L0_attn_x': _L0_attn_in['x'], 'L0_attn_Wqkv': _L0_attn_in['Wqkv'], 'L0_attn_bqkv': _L0_attn_in['bqkv'], 'L0_attn_Wo': _L0_attn_in['Wo'], 'L0_attn_bo': _L0_attn_in['bo'], 'L0_ffn_Wg': _L0_ffn_in['Wg'], 'L0_ffn_W0a': _L0_ffn_in['W0a'], 'L0_ffn_b0a': _L0_ffn_in['b0a'], 'L0_ffn_W0b': _L0_ffn_in['W0b'], 'L0_ffn_b0b': _L0_ffn_in['b0b'], 'L0_ffn_W1a': _L0_ffn_in['W1a'], 'L0_ffn_b1a': _L0_ffn_in['b1a'], 'L0_ffn_W1b': _L0_ffn_in['W1b'], 'L0_ffn_b1b': _L0_ffn_in['b1b'], 'L1_attn_log_decay': _L1_attn_in['log_decay'], 'L1_attn_Wq': _L1_attn_in['Wq'], 'L1_attn_Wk': _L1_attn_in['Wk'], 'L1_attn_Wv': _L1_attn_in['Wv'], 'L1_attn_Wo': _L1_attn_in['Wo'], 'L1_attn_Wg1': _L1_attn_in['Wg1'], 'L1_attn_Wg2': _L1_attn_in['Wg2'], 'L1_attn_norm_w': _L1_attn_in['norm_w'], 'L1_ffn_w1': _L1_ffn_in['w1'], 'L1_ffn_w2': _L1_ffn_in['w2'], 'L1_ffn_w3': _L1_ffn_in['w3']}
    _x0 = _d['L0_attn_x']
    _d['L0_attn_x'] = jax.random.normal(jax.random.fold_in(jax.random.key(seed), 1), (1, 2048, 512), dtype=_x0.dtype)
    del _x0
    return _d

def reference(L0_attn_x, L0_attn_Wqkv, L0_attn_bqkv, L0_attn_Wo, L0_attn_bo, L0_ffn_Wg, L0_ffn_W0a, L0_ffn_b0a, L0_ffn_W0b, L0_ffn_b0b, L0_ffn_W1a, L0_ffn_b1a, L0_ffn_W1b, L0_ffn_b1b, L1_attn_log_decay, L1_attn_Wq, L1_attn_Wk, L1_attn_Wv, L1_attn_Wo, L1_attn_Wg1, L1_attn_Wg2, L1_attn_norm_w, L1_ffn_w1, L1_ffn_w2, L1_ffn_w3):

    def _L0_attn_ref(x, Wqkv, bqkv, Wo, bo):
        import jax, jax.numpy as jnp
        import numpy as np
        HIDDEN = 512
        NUM_HEADS = 16
        HEAD_SIZE = HIDDEN // NUM_HEADS
        SEQ = 512
        BATCH = 2

        def alibi_causal_bias(seq_len: int, num_heads: int) -> jnp.ndarray:
            i = jnp.arange(seq_len)[:, None]
            j = jnp.arange(seq_len)[None, :]
            dist = -(i - j).astype(jnp.float32)
            causal = jnp.where(j > i, -jnp.inf, 0.0)
            base = jnp.where(j > i, 0.0, dist) + causal
            if num_heads <= 8:
                slopes = jnp.asarray([1.0 / 2 ** k for k in range(num_heads)], jnp.float32)
            else:
                slopes = jnp.asarray([1.0 / 2 ** (k / 2) for k in range(num_heads)], jnp.float32)
            return slopes[None, :, None, None] * dist[None, None] * (j <= i)[None, None] + causal[None, None]
        b, s, h = x.shape
        scale = 1.0 / np.sqrt(HEAD_SIZE)
        qkv = x @ Wqkv + bqkv
        q, k, v = jnp.split(qkv, 3, axis=-1)

        def heads(t):
            return t.reshape(b, s, NUM_HEADS, HEAD_SIZE).transpose(0, 2, 1, 3)
        q, k, v = (heads(q), heads(k), heads(v))
        scores = jnp.einsum('bhid,bhjd->bhij', q, k) * scale
        scores = scores + alibi_causal_bias(s, NUM_HEADS)
        attn = jax.nn.softmax(scores, axis=-1)
        out = jnp.einsum('bhij,bhjd->bhid', attn, v)
        out = out.transpose(0, 2, 1, 3).reshape(b, s, NUM_HEADS * HEAD_SIZE)
        return out @ Wo + bo

    def _L0_ffn_ref(x, Wg, W0a, b0a, W0b, b0b, W1a, b1a, W1b, b1b):
        import jax, jax.numpy as jnp
        import numpy as np
        H = 512
        scores = jax.nn.softmax(jnp.einsum('bsh,eh->bse', x, Wg), axis=-1)
        top_expert = jnp.argmax(scores, axis=-1)
        h0 = jax.nn.gelu(jnp.einsum('bsh,fh->bsf', x, W0a) + b0a, approximate=False)
        out0 = jnp.einsum('bsf,hf->bsh', h0, W0b) + b0b
        h1 = jax.nn.relu(jnp.einsum('bsh,fh->bsf', x, W1a) + b1a)
        out1 = jnp.einsum('bsf,hf->bsh', h1, W1b) + b1b
        mask0 = (top_expert == 0).astype(x.dtype)[..., None]
        return out0 * mask0 + out1 * (1.0 - mask0)

    def _L1_attn_ref(x, log_decay, Wq, Wk, Wv, Wo, Wg1, Wg2, norm_w):
        import jax, jax.numpy as jnp
        import numpy as np
        EPS = 1e-05
        CHUNK = 128

        def lightning_attn(q, k, v, ld, chunk=CHUNK):
            b, n, h, d = q.shape
            nc = n // chunk
            idx = jnp.arange(chunk)
            diff = idx[:, None] - idx[None, :]
            mask = diff >= 0
            D = jnp.exp(ld[:, None, None] * jnp.where(mask, diff, 0)) * mask
            q_decay = jnp.exp(ld[None, :] * (idx + 1)[:, None])
            k_decay = jnp.exp(ld[None, :] * (chunk - 1 - idx)[:, None])
            chunk_decay = jnp.exp(ld * chunk)
            qc = jnp.moveaxis(q.reshape(b, nc, chunk, h, d), 1, 0)
            kc = jnp.moveaxis(k.reshape(b, nc, chunk, h, d), 1, 0)
            vc = jnp.moveaxis(v.reshape(b, nc, chunk, h, d), 1, 0)

            def step(S, inp):
                qb, kb, vb = inp
                scores = jnp.einsum('bchd,bshd->bhcs', qb, kb) * D[None]
                o_intra = jnp.einsum('bhcs,bshd->bchd', scores, vb)
                o_inter = jnp.einsum('bchd,bhde->bche', qb, S) * q_decay[None, :, :, None]
                S_new = chunk_decay[None, :, None, None] * S + jnp.einsum('bshd,bshe->bhde', kb * k_decay[None, :, :, None], vb)
                return (S_new, o_intra + o_inter)
            S0 = jnp.zeros((b, h, d, d), dtype=q.dtype)
            S_final, oc = jax.lax.scan(step, S0, (qc, kc, vc))
            out = jnp.moveaxis(oc, 0, 1).reshape(b, n, h, d)
            return (out, S_final)

        def group_rmsnorm_fused_gate(o, gate, w, num_heads):
            b, n, d = o.shape
            hd = d // num_heads
            o = o * jax.nn.sigmoid(gate)
            og = o.reshape(b, n, num_heads, hd)
            og = og * jax.lax.rsqrt(jnp.mean(og * og, axis=-1, keepdims=True) + EPS)
            return og.reshape(b, n, d) * w
        b, n, d = x.shape
        H = log_decay.shape[0]
        hd = d // H
        q = jax.nn.silu(jnp.einsum('bnd,de->bne', x, Wq).reshape(b, n, H, hd))
        k = jax.nn.silu(jnp.einsum('bnd,de->bne', x, Wk).reshape(b, n, H, hd))
        v = jax.nn.silu(jnp.einsum('bnd,de->bne', x, Wv).reshape(b, n, H, hd))
        o, _ = lightning_attn(q, k, v, log_decay)
        o = o.reshape(b, n, d)
        gate = jnp.einsum('bnk,kd->bnd', jnp.einsum('bnd,dk->bnk', x, Wg1), Wg2)
        o = group_rmsnorm_fused_gate(o, gate, norm_w, H)
        return jnp.einsum('bnd,de->bne', o, Wo)

    def _L1_ffn_ref(x, w1, w2, w3):
        import jax, jax.numpy as jnp
        import numpy as np
        EPS = 1e-08

        def _quantize(w):
            gamma = jnp.mean(jnp.abs(w))
            return jnp.clip(jnp.round(w / (gamma + EPS)), -1.0, 1.0)

        def _bitlinear(x, w):
            return jnp.matmul(x, _quantize(w).T)
        x1 = _bitlinear(x, w1)
        x2 = _bitlinear(x, w2)
        hidden = jax.nn.sigmoid(x1) * x2
        return _bitlinear(hidden, w3)
    x = L0_attn_x
    xn = _layernorm(x, axis=-1)
    x = x + _L0_attn_ref(xn, L0_attn_Wqkv, L0_attn_bqkv, L0_attn_Wo, L0_attn_bo) + _L0_ffn_ref(xn, L0_ffn_Wg, L0_ffn_W0a, L0_ffn_b0a, L0_ffn_W0b, L0_ffn_b0b, L0_ffn_W1a, L0_ffn_b1a, L0_ffn_W1b, L0_ffn_b1b)
    xn = _layernorm(x, axis=-1)
    x = x + _L1_attn_ref(xn, L1_attn_log_decay, L1_attn_Wq, L1_attn_Wk, L1_attn_Wv, L1_attn_Wo, L1_attn_Wg1, L1_attn_Wg2, L1_attn_norm_w) + _L1_ffn_ref(xn, L1_ffn_w1, L1_ffn_w2, L1_ffn_w3)
    return x

_drawn_inputs = setup_inputs


def setup_inputs(seed=0):
    import zlib

    import numpy as np

    out = dict(_drawn_inputs(seed))
    spreads = {'L0_attn_bqkv': (0.0, 0.1), 'L0_attn_bo': (0.0, 0.1), 'L1_attn_norm_w': (1.0, 0.6)}
    factors = {'L0_ffn_b0a': 3.993,
     'L0_ffn_b1a': 3.256,
     'L1_attn_log_decay': 54.142,
     'L1_attn_Wq': 64.0,
     'L1_attn_Wk': 64.0,
     'L1_attn_Wv': 21.368,
     'L1_attn_Wo': 8.0,
     'L1_attn_Wg1': 22.824,
     'L1_attn_Wg2': 23.052}
    for name, (base, spread) in spreads.items():
        noise = np.random.default_rng([zlib.crc32(name.encode()), seed]).standard_normal(out[name].shape)
        drawn = base * np.exp(spread * noise) if base else spread * noise
        out[name] = jnp.asarray(drawn.astype(out[name].dtype))
    for name, factor in factors.items():
        out[name] = (out[name] * factor).astype(out[name].dtype)
    return out
```

```python
from contextlib import ExitStack

import numpy as np

import concourse.bass as bass
from concourse import mybir

F32 = mybir.dt.float32
F32R = mybir.dt.float32r
BF16 = mybir.dt.bfloat16
ALU = mybir.AluOpType
ACT = mybir.ActivationFunctionType
AX = mybir.AxisListType

P = 128
T = 2048
D = 512
KT = D // P
CH = 512
NCH = T // CH
NH = 16
HD = D // NH
HPG = P // HD
TT = CH // P
QT = T // P
FH = 1024
FT = FH // P
GH = 1408
GT = GH // P
LN_EPS = 1e-5
NEG = -1e30


class Stage:

    def __init__(self, nc, name):
        self.nc, self.name, self.stack, self.sems = nc, name, ExitStack(), []

    def __enter__(self):
        return self

    def __exit__(self, *a):
        self.stack.__exit__(*a)
        self.nc.clear_and_free_semaphores(self.sems)
        self.nc.all_engine_barrier()

    def sb(self, name, shape, dt=F32):
        return self.stack.enter_context(self.nc.sbuf_tensor(f"{self.name}_{name}", shape, dt))

    def ps(self, name, shape):
        return self.stack.enter_context(self.nc.psum_tensor(f"{self.name}_{name}", shape, F32))

    def sem(self, name):
        self.sems.append(self.nc.alloc_semaphore(f"{self.name}_{name}"))
        return self.sems[-1]

    def block(self):
        return self.stack.enter_context(self.nc.Block())


class Chain:

    def __init__(self, eng, sem, base):
        self.eng, self.sem, self.base, self.n = eng, sem, base, 0

    def link(self, ins):
        self.n += 1
        ins.then_inc(self.sem, 1)
        self.eng.wait_ge(self.sem, self.base + self.n)


def wait_alone(pool, sem, value, passed):
    pool.wait_ge(sem, value)
    pool.sem_inc(passed, 1)


def chunk_loop(eng):
    with eng.Fori(0, NCH // 2) as r:
        for par in range(2):
            yield r, par, r * 2 + par


def feat(ap):
    return ap.rearrange("(k p) t -> p k t", p=P)


def tok(ap, c):
    return ap[:, :, bass.ds(c * CH, CH)]


class WeightSplit:

    def __init__(self, st, width, pieces):
        self.pieces = pieces
        self.stage = [st.sb(f"wstage{i}", [P, width]) for i in range(2)]
        self.loaded = [st.sem(f"w_loaded{i}") for i in range(2)]
        self.hi_done = st.sem("w_hi_done")
        self.lo_done = st.sem("w_lo_done")

    def load(self, sp):
        for j, (src, hi, lo) in enumerate(self.pieces):
            if j >= 2:
                sp.wait_ge(self.lo_done, j - 1)
            sp.dma_start(self.stage[j % 2][:, 0:src.shape[-1]], src).then_inc(self.loaded[j % 2], 16)

    def hi(self, act):
        for j, (src, hi, lo) in enumerate(self.pieces):
            act.wait_ge(self.loaded[j % 2], 16 * (j // 2 + 1))
            act.activation(hi, self.stage[j % 2][:, 0:src.shape[-1]], ACT.Copy).then_inc(self.hi_done, 1)

    def lo(self, dve):
        for j, (src, hi, lo) in enumerate(self.pieces):
            dve.wait_ge(self.hi_done, j + 1)
            dve.tensor_tensor(lo, self.stage[j % 2][:, 0:src.shape[-1]], hi.bitcast(F32),
                              ALU.subtract).then_inc(self.lo_done, 1)

    def wait(self, pe):
        pe.wait_ge(self.lo_done, len(self.pieces))


def three_passes(pe, out, wh, wl, xh, xl, first, last):
    pe.matmul(out, wh, xh, start=first, stop=False)
    pe.matmul(out, wh, xl, start=False, stop=False)
    return pe.matmul(out, wl, xh, start=False, stop=last)


def alibi_stage(nc, alibi_q, alibi_k, aq_d, ak_d):
    with Stage(nc, "alibi") as st:
        q, k = st.sb("q", [NH * 4, T]), st.sb("k", [NH * 6, T])
        qr, kr = st.sb("qr", [NH * 4, T], F32R), st.sb("kr", [NH * 6, T], F32R)
        loaded, rounded, stored = st.sem("loaded"), st.sem("rounded"), st.sem("stored")
        block = st.block()

        @block.sync
        def _(sp):
            sp.dma_start(q[:], alibi_q).then_inc(loaded, 16)
            sp.dma_start(k[:], alibi_k).then_inc(loaded, 16)
            sp.wait_ge(rounded, 2)
            sp.dma_start(aq_d, qr[:].bitcast(F32)).then_inc(stored, 16)
            sp.dma_start(ak_d, kr[:].bitcast(F32)).then_inc(stored, 16)
            sp.wait_ge(stored, 32)

        @block.vector
        def _(dve):
            dve.wait_ge(loaded, 32)
            dve.tensor_copy(qr[:], q[:]).then_inc(rounded, 1)
            dve.tensor_copy(kr[:], k[:]).then_inc(rounded, 1)


def rsqrt_newton(dve, chain, out, tmp, root, var, eps):
    chain.link(dve.reciprocal(out, root))
    chain.link(dve.tensor_tensor(tmp, out, out, ALU.mult))
    chain.link(dve.scalar_tensor_tensor(out=tmp, in0=var, scalar=eps, in1=tmp, op0=ALU.add, op1=ALU.mult))
    chain.link(dve.tensor_scalar(tmp, tmp, -0.5, 1.5, ALU.mult, ALU.add))
    chain.link(dve.tensor_tensor(out, out, tmp, ALU.mult))


def layernorm_stage(nc, name, x_d, xh_d, xl_d):
    with Stage(nc, name) as st:
        ones = st.sb("ones", [P, P])
        eps = st.sb("eps", [P, 1])
        x = [st.sb(f"x{i}", [P, KT, CH]) for i in range(2)]
        xc = [st.sb(f"xc{i}", [P, KT, CH]) for i in range(2)]
        sq = [st.sb(f"sq{i}", [P, KT, CH]) for i in range(2)]
        hi = [st.sb(f"hi{i}", [P, KT, CH], F32R) for i in range(2)]
        lo = [st.sb(f"lo{i}", [P, KT, CH], F32R) for i in range(2)]
        root, inv, tmp = st.sb("root", [P, CH]), st.sb("inv", [P, CH]), st.sb("tmp", [P, CH])
        mean, var = st.ps("mean", [P, 2, CH]), st.ps("var", [P, 2, CH])
        ones_set = st.sem("ones_set")
        x_in = [st.sem(f"x_in{i}") for i in range(2)]
        mean_ready, centered, squared = st.sem("mean_ready"), st.sem("centered"), st.sem("squared")
        var_ready, root_ready, newton = st.sem("var_ready"), st.sem("root_ready"), st.sem("newton")
        normed, hi_ready, lo_ready = st.sem("normed"), st.sem("hi_ready"), st.sem("lo_ready")
        stored, out_free = st.sem("stored"), st.sem("out_free")
        passed = st.sem("passed")
        block = st.block()
        LINKS = 5

        @block.sync
        def _(sp):
            for r, par, c in chunk_loop(sp):
                sp.wait_ge(centered, c + 1)
                sp.dma_start(x[par][:], tok(feat(x_d), c)).then_inc(x_in[par], 16)

        @block.tensor
        def _(pe):
            pe.wait_ge(ones_set, 2)
            for r, par, c in chunk_loop(pe):
                pe.wait_ge(x_in[par], r * 16 + 16)
                for k in range(KT):
                    last = pe.matmul(mean[:, par, :], ones[:], x[par][:, k, :], start=k == 0, stop=k == KT - 1)
                last.then_inc(mean_ready, 1)
                pe.wait_ge(squared, c + 1)
                for k in range(KT):
                    last = pe.matmul(var[:, par, :], ones[:], sq[par][:, k, :], start=k == 0, stop=k == KT - 1)
                last.then_inc(var_ready, 1)

        @block.scalar
        def _(act):
            act.wait_ge(ones_set, 2)
            for r, par, c in chunk_loop(act):
                act.wait_ge(centered, c + 3)
                act.activation(sq[par][:], xc[par][:], ACT.Square).then_inc(squared, 1)
                act.wait_ge(var_ready, c + 1)
                act.activation(root[:], var[:, par, :], ACT.Sqrt, bias=eps[:, 0:1]).then_inc(root_ready, 1)
                act.wait_ge(normed, c + 1)
                act.wait_ge(out_free, c + 1)
                act.activation(hi[par][:], xc[par][:], ACT.Copy).then_inc(hi_ready, 1)

        @block.vector
        def _(dve):
            dve.sem_inc(centered, 2)
            dve.memset(ones[:], 1.0 / D).then_inc(ones_set, 1)
            dve.memset(eps[:], LN_EPS).then_inc(ones_set, 1)
            for r, par, c in chunk_loop(dve):
                dve.wait_ge(mean_ready, c + 1)
                dve.tensor_tensor(xc[par][:], x[par][:], mean[:, par:par + 1, :].to_broadcast([P, KT, CH]),
                                  ALU.subtract).then_inc(centered, 1)
                dve.wait_ge(root_ready, c + 1)
                chain = Chain(dve, newton, c * LINKS)
                rsqrt_newton(dve, chain, inv[:], tmp[:], root[:], var[:, par, :], LN_EPS)
                assert chain.n == LINKS
                for k in range(KT):
                    last = dve.tensor_tensor(xc[par][:, k, :], xc[par][:, k, :], inv[:], ALU.mult)
                last.then_inc(normed, 1)
                dve.wait_ge(hi_ready, c + 1)
                dve.tensor_tensor(lo[par][:], xc[par][:], hi[par][:].bitcast(F32),
                                  ALU.subtract).then_inc(lo_ready, 1)

        @block.gpsimd
        def _(pool):
            pool.sem_inc(out_free, 2)
            for r, par, c in chunk_loop(pool):
                wait_alone(pool, lo_ready, c + 1, passed)
                pool.dma_start(tok(feat(xh_d), c), hi[par][:].bitcast(F32)).then_inc(stored, 16)
                pool.dma_start(tok(feat(xl_d), c), lo[par][:].bitcast(F32)).then_inc(stored, 16)
                pool.wait_ge(stored, c * 32 + 32)
                pool.sem_inc(out_free, 1)


def qkv_stage(nc, w_d, bqk_d, bv_d, xh_d, xl_d, qh_d, ql_d, kh_d, kl_d, v_d):
    NQK, NP = 2 * KT, 2 * KT + TT
    with Stage(nc, "qkv") as st:
        wh, wl = st.sb("wh", [P, KT, 3 * D], F32R), st.sb("wl", [P, KT, 3 * D], F32R)
        ws = WeightSplit(st, 3 * D, [(w_d[k * P:(k + 1) * P, :], wh[:, k, :], wl[:, k, :]) for k in range(KT)])
        bqk, bv = st.sb("bqk", [P, NQK]), st.sb("bv", [P, D])
        xh = [st.sb(f"xh{i}", [P, KT, CH], F32R) for i in range(2)]
        xl = [st.sb(f"xl{i}", [P, KT, CH], F32R) for i in range(2)]
        full = st.sb("full", [P, 4, CH])
        hi, lo = st.sb("hi", [P, 4, CH], F32R), st.sb("lo", [P, 4, CH], F32R)
        vb = st.sb("vb", [P, 2, D])
        acc = st.ps("acc", [P, 4, CH])
        b_in = st.sem("b_in")
        x_in = [st.sem(f"x_in{i}") for i in range(2)]
        made, taken = st.sem("made"), st.sem("taken")
        hi_ready, lo_ready = st.sem("hi_ready"), st.sem("lo_ready")
        qk_stored, v_stored = st.sem("qk_stored"), st.sem("v_stored")
        qk_free, v_free = st.sem("qk_free"), st.sem("v_free")
        passed = st.sem("passed")
        block = st.block()

        @block.sync
        def _(sp):
            sp.dma_start(bqk[:], bqk_d).then_inc(b_in, 16)
            sp.dma_start(bv[:], bv_d).then_inc(b_in, 16)
            ws.load(sp)
            for r, par, c in chunk_loop(sp):
                sp.wait_ge(made, c * NP + NP)
                sp.dma_start(xh[par][:].bitcast(F32), tok(feat(xh_d), c)).then_inc(x_in[par], 16)
                sp.dma_start(xl[par][:].bitcast(F32), tok(feat(xl_d), c)).then_inc(x_in[par], 16)

        @block.tensor
        def _(pe):
            pe.sem_inc(made, 2 * NP)
            ws.wait(pe)
            for r, par, c in chunk_loop(pe):
                pe.wait_ge(x_in[par], r * 32 + 32)
                for m in range(NP):
                    pe.wait_ge(taken, c * NP + m + 1)
                    for k in range(KT):
                        edge = (k == 0, k == KT - 1)
                        if m < NQK:
                            s = slice(m * P, (m + 1) * P)
                            last = three_passes(pe, acc[:, m % 4, :], wh[:, k, s], wl[:, k, s],
                                                xh[par][:, k, :], xl[par][:, k, :], *edge)
                        else:
                            s = slice((m - NQK) * P, (m - NQK + 1) * P)
                            last = three_passes(pe, acc[:, m % 4, :], xh[par][:, k, s], xl[par][:, k, s],
                                                wh[:, k, 2 * D:], wl[:, k, 2 * D:], *edge)
                    last.then_inc(made, 1)

        @block.scalar
        def _(act):
            ws.hi(act)
            for r, par, c in chunk_loop(act):
                for m in range(NQK):
                    act.wait_ge(taken, c * NP + m + 5)
                    act.wait_ge(qk_free, c * NQK + m + 1)
                    act.activation(hi[:, m % 4, :], full[:, m % 4, :], ACT.Copy).then_inc(hi_ready, 1)

        @block.vector
        def _(dve):
            dve.sem_inc(taken, 4)
            dve.sem_inc(lo_ready, 4)
            ws.lo(dve)
            dve.wait_ge(b_in, 32)
            for r, par, c in chunk_loop(dve):
                def low(m):
                    dve.wait_ge(hi_ready, c * NQK + m + 1)
                    dve.tensor_tensor(lo[:, m % 4, :], full[:, m % 4, :], hi[:, m % 4, :].bitcast(F32),
                                      ALU.subtract).then_inc(lo_ready, 1)

                for m in range(NP):
                    dve.wait_ge(made, c * NP + m + 1 + 2 * NP)
                    if m < NQK:
                        dve.wait_ge(lo_ready, c * NQK + m + 1)
                        dve.tensor_scalar(full[:, m % 4, :], acc[:, m % 4, :], bqk[:, m:m + 1],
                                          float(HD) ** -0.5 if m < KT else 1.0,
                                          ALU.add, ALU.mult).then_inc(taken, 1)
                        if m:
                            low(m - 1)
                    else:
                        t = m - NQK
                        if t == 0:
                            low(NQK - 1)
                        dve.wait_ge(v_free, c * TT + t + 1)
                        dve.tensor_tensor(vb[:, t % 2, :], acc[:, m % 4, :], bv[:], ALU.add).then_inc(taken, 1)

        @block.gpsimd
        def _(pool):
            pool.sem_inc(qk_free, 4)
            pool.sem_inc(v_free, 2)
            for r, par, c in chunk_loop(pool):
                for m in range(NQK):
                    wait_alone(pool, lo_ready, c * NQK + m + 5, passed)
                    f = slice(m % KT * P, (m % KT + 1) * P)
                    hi_d, lo_d = (qh_d, ql_d) if m < KT else (kh_d, kl_d)
                    pool.dma_start(hi_d[f, bass.ds(c * CH, CH)], hi[:, m % 4, :].bitcast(F32)).then_inc(qk_stored, 16)
                    pool.dma_start(lo_d[f, bass.ds(c * CH, CH)], lo[:, m % 4, :].bitcast(F32)).then_inc(qk_stored, 16)
                    pool.wait_ge(qk_stored, (c * NQK + m) * 32 + 32)
                    pool.sem_inc(qk_free, 1)
                for t in range(TT):
                    wait_alone(pool, taken, c * NP + NQK + t + 5, passed)
                    pool.dma_start(v_d[bass.ds(c * CH + t * P, P), :], vb[:, t % 2, :]).then_inc(v_stored, 16)
                    pool.wait_ge(v_stored, (c * TT + t) * 16 + 16)
                    pool.sem_inc(v_free, 1)


QROWS, SROWS, KROWS = 3 * HD, 3 * HD + 4, 3 * HD + 6
MAIN = [(c, kt) for c in range(NCH) for kt in range(TT * (c + 1))]
UNITS = [(t, g) for t in range(QT) for g in range(t // TT + 1)]
NS = len(MAIN)
LAST_UNIT_STEP = 30
UNITS_AT = [[u for u in range(NS) if u * LAST_UNIT_STEP // NS == s] for s in range(NS)]
ROW_STEP = LAST_UNIT_STEP + 3


def main_span(c, kt):
    off = max(kt - TT * c, 0) * P
    return off, min(off, CH - 2 * P)


def unit_span(t, g):
    width = CH if g < t // TT else (t % TT + 1) * P
    return width, max(width, 2 * P)


def attention_stage(nc, cst_d, aq_d, ak_d, qh_d, ql_d, kh_d, kl_d, v_d, att_d):
    with Stage(nc, "att") as st:
        cst = st.sb("cst", [P, 3, P])
        ident = st.sb("ident", [P, P], BF16)
        neg_q, neg_k = st.sb("neg_q", [P, P], BF16), st.sb("neg_k", [P, P], BF16)
        qs = [[st.sb(f"qs{i}{h}", [KROWS, T], F32R) for h in range(2)] for i in range(2)]
        ks = [[st.sb(f"ks{i}{h}", [KROWS, T], F32R) for h in range(2)] for i in range(2)]
        vs = [st.sb(f"vs{i}", [P, QT, 2, 2 * HD]) for i in range(2)]
        probs = st.sb("probs", [P, 4, 2, CH])
        maxes = st.sb("maxes", [P, 2, QT, NCH])
        negmax = st.sb("negmax", [P, 2, QT])
        turned = st.sb("turned", [P, P])
        split = turned[:, 0:2 * 2 * QT].rearrange("p (a h t) -> p a h t", a=2, h=2)
        rows = st.sb("rows", [2 * 2 * QT, P], F32R)
        rsum = st.sb("rsum", [P, CH])
        att = st.sb("att", [P, 2, CH])
        scores = st.ps("scores", [P, 2, 2, CH])
        unit = st.ps("unit", [P, 2, CH])
        outp = st.ps("outp", [P, 2, CH])
        cst_in, cst_ready = st.sem("cst_in"), st.sem("cst_ready")
        pair_in = [st.sem(f"pair_in{i}") for i in range(2)]
        row_in = [st.sem(f"row_in{i}") for i in range(2)]
        unit_made, unit_taken = st.sem("unit_made"), st.sem("unit_taken")
        max_step, rows_made, rows_ready = st.sem("max_step"), st.sem("rows_made"), st.sem("rows_ready")
        scored, exped, summed = st.sem("scored"), st.sem("exped"), st.sem("summed")
        recip, normed = st.sem("recip"), st.sem("normed")
        stored, att_free = st.sem("stored"), st.sem("att_free")
        passed = st.sem("passed")
        block = st.block()
        NPAIR = NH // 2
        LOADS = 2 * (3 + 1 + 3 + 1 + 1)
        MAX_LINKS = NCH + 2

        def pairs(eng, body):
            with eng.Fori(0, NPAIR // 2 - 1) as r:
                for par in range(2):
                    body(r * 2 + par, par, r, True)
            body(NPAIR - 2, 0, NPAIR // 2 - 1, True)
            body(NPAIR - 1, 1, NPAIR // 2 - 1, False)

        @block.sync
        def _(sp):
            sp.dma_start(cst[:], cst_d).then_inc(cst_in, 16)

            def load(p, par):
                for h in range(2):
                    f, sem = bass.ds(p * 2 * HD + h * HD, HD), pair_in[par]
                    q, k = qs[par][h], ks[par][h]
                    for b, (q_d, k_d) in enumerate(((qh_d, kh_d), (ql_d, kh_d), (qh_d, kl_d))):
                        s = slice(b * HD, (b + 1) * HD)
                        sp.dma_start(q[s, :].bitcast(F32), q_d[f, :]).then_inc(sem, 16)
                        sp.dma_start(k[s, :].bitcast(F32), k_d[f, :]).then_inc(sem, 16)
                    sp.dma_start(q[QROWS:SROWS, :].bitcast(F32), aq_d[bass.ds(p * 8 + h * 4, 4), :]).then_inc(sem, 16)
                    sp.dma_start(k[QROWS:KROWS, :].bitcast(F32), ak_d[bass.ds(p * 12 + h * 6, 6), :]).then_inc(sem, 16)
                    sp.dma_start(vs[par][:, :, h, 0:HD],
                                 v_d[:, f].rearrange("(t p) d -> p t d", p=P)).then_inc(sem, 16)

            def max_rows(p, par, r):
                sp.wait_ge(rows_ready, p + 1)
                for h in range(2):
                    for part in range(2):
                        src = rows[(part * 2 + h) * QT:(part * 2 + h + 1) * QT, :]
                        dst = qs[par][h][SROWS + part:SROWS + part + 1, :].rearrange("a (t q) -> a t q", q=P)
                        sp.dma_start(dst.bitcast(F32), src.bitcast(F32)).then_inc(row_in[par], 16)

            load(0, 0)
            max_rows(0, 0, 0)
            load(1, 1)

            def body(p, par, r, more):
                if not more:
                    return
                max_rows(p + 1, 1 - par, r)
                if isinstance(p, int) and p + 2 >= NPAIR:
                    return
                sp.wait_ge(summed, (p + 1) * NS + 4)
                load(p + 2, par)

            pairs(sp, body)

        @block.tensor
        def _(pe):
            def unit_product(p, par, u):
                t, g = UNITS[u]
                width, cover = unit_span(t, g)
                for h in range(2):
                    pe.wait_ge(unit_taken, (p * NS + u) * 2 + h + 1)
                    diag = g == t // TT
                    last = pe.matmul(unit[:, h, 0:cover], qs[par][h][0:SROWS, t * P:(t + 1) * P],
                                     ks[par][h][0:SROWS, g * CH:g * CH + cover], start=True, stop=not diag)
                    if diag:
                        last = pe.matmul(unit[:, h, width - P:width], ident[:], neg_q[:], start=False, stop=True)
                    last.then_inc(unit_made, 1)

            def turn(p):
                pe.wait_ge(max_step, (p + 1) * MAX_LINKS)
                pe.wait_ge(unit_taken, (p + 1) * NS * 2 + 2)
                pe.transpose(unit[:, 0, 0:P], turned[:], cst[:, 0, :]).then_inc(rows_made, 1)

            def sums(p, par, s):
                c, kt = MAIN[s]
                off, _ = main_span(c, kt)
                pe.wait_ge(exped, p * NS + s + 3)
                if kt == 0:
                    pe.wait_ge(normed, p * NCH + c + 1)
                for h in range(2):
                    last = pe.matmul(outp[h * 2 * HD:(h + 1) * 2 * HD, c % 2, off:CH], vs[par][:, kt, h, :],
                                     probs[:, s % 4, h, off:CH], start=kt == 0, stop=kt == TT * (c + 1) - 1,
                                     skip_group_check=True)
                last.then_inc(summed, 1)

            def body(p, par, r, more):
                for s, (c, kt) in enumerate(MAIN):
                    off, start = main_span(c, kt)
                    if s == 0:
                        pe.wait_ge(row_in[par], r * 64 + 64)
                    pe.wait_ge(exped, p * NS + s + 1)
                    for h in range(2):
                        diag = kt >= TT * c
                        last = pe.matmul(scores[:, s % 2, h, start:CH], ks[par][h][:, kt * P:(kt + 1) * P],
                                         qs[par][h][:, c * CH + start:(c + 1) * CH], start=True, stop=not diag)
                        if diag:
                            last = pe.matmul(scores[:, s % 2, h, off:off + P], ident[:], neg_k[:],
                                             start=False, stop=True)
                    last.then_inc(scored, 1)
                    if s > 0:
                        sums(p, par, s - 1)
                    if more:
                        if s == 0:
                            pe.wait_ge(pair_in[1 - par], (r + par) * LOADS * 16 + LOADS * 16)
                        for u in UNITS_AT[s]:
                            unit_product(p + 1, 1 - par, u)
                        if s == ROW_STEP:
                            turn(p + 1)
                sums(p, par, NS - 1)

            pe.sem_inc(summed, 4)
            pe.wait_ge(cst_ready, 6)
            pe.wait_ge(pair_in[0], LOADS * 16)
            for u in range(NS):
                unit_product(0, 0, u)
            turn(0)
            pairs(pe, body)

        @block.scalar
        def _(act):
            act.sem_inc(exped, 2)

            def body(p, par, r, more):
                for s, (c, kt) in enumerate(MAIN):
                    off, _ = main_span(c, kt)
                    act.wait_ge(scored, p * NS + s + 1)
                    act.wait_ge(summed, p * NS + s + 1)
                    act.activation(probs[:, s % 4, :, off:CH], scores[:, s % 2, :, off:CH], ACT.Exp).then_inc(exped, 1)
            pairs(act, body)

        @block.vector
        def _(dve):
            def take(p, u):
                t, g = UNITS[u]
                width, _ = unit_span(t, g)
                for h in range(2):
                    dve.wait_ge(unit_made, (p * NS + u) * 2 + h + 1)
                    dve.tensor_reduce(maxes[:, h, t, g:g + 1], unit[:, h, 0:width], AX.X, ALU.max).then_inc(unit_taken, 1)

            def finish_max(p):
                dve.wait_ge(unit_taken, (p + 1) * NS * 2 + 2)
                dve.wait_ge(rows_made, p + 1)
                chain = Chain(dve, max_step, p * MAX_LINKS)
                for g in range(NCH):
                    t = slice(g * TT, (g + 1) * TT)
                    chain.link(dve.tensor_reduce(negmax[:, :, t], maxes[:, :, t, 0:g + 1], AX.X, ALU.max, negate=True))
                chain.link(dve.tensor_copy(split[:, 0].bitcast(F32R), negmax[:]))
                chain.link(dve.tensor_tensor(split[:, 1].bitcast(F32R), negmax[:], split[:, 0], ALU.subtract))
                assert chain.n == MAX_LINKS
                dve.wait_ge(rows_made, p + 2)
                dve.tensor_copy(rows[:], unit[0:2 * 2 * QT, 0, 0:P]).then_inc(rows_ready, 1)

            def normalize(p, c):
                dve.wait_ge(summed, p * NS + len([1 for m in MAIN if m[0] <= c]) + 4)
                dve.wait_ge(normed, p * NCH + c + 2)
                for h in range(2):
                    o = h * 2 * HD
                    last = dve.reciprocal(rsum[o:o + HD, :], outp[o + HD:o + 2 * HD, c % 2, :])
                last.then_inc(recip, 1)
                dve.wait_ge(recip, p * NCH + c + 1)
                dve.wait_ge(att_free, p * NCH + c + 1)
                for h in range(2):
                    o = h * 2 * HD
                    last = dve.tensor_tensor(att[o:o + HD, c % 2, :], outp[o:o + HD, c % 2, :],
                                             rsum[o:o + HD, :], ALU.mult)
                last.then_inc(normed, 1)

            def body(p, par, r, more):
                for s, (c, kt) in enumerate(MAIN):
                    if more:
                        for u in UNITS_AT[s]:
                            take(p + 1, u)
                        if s == ROW_STEP - 1:
                            finish_max(p + 1)
                    if kt == 1 and c > 0:
                        normalize(p, c - 1)
                normalize(p, NCH - 1)

            dve.sem_inc(unit_taken, 2)
            dve.sem_inc(normed, 2)
            dve.sem_inc(rows_made, 1)
            dve.wait_ge(cst_in, 16)
            dve.tensor_copy(ident[:], cst[:, 0, :]).then_inc(cst_ready, 1)
            dve.tensor_copy(neg_q[:], cst[:, 1, :]).then_inc(cst_ready, 1)
            dve.tensor_copy(neg_k[:], cst[:, 2, :]).then_inc(cst_ready, 1)
            dve.memset(turned[:], 0.0).then_inc(cst_ready, 1)
            for i in range(2):
                dve.memset(vs[i][:, :, :, HD:], 1.0).then_inc(cst_ready, 1)
            dve.wait_ge(cst_ready, 6)
            for u in range(NS):
                take(0, u)
            finish_max(0)
            pairs(dve, body)

        @block.gpsimd
        def _(pool):
            pool.sem_inc(att_free, 2)

            def body(p, par, r, more):
                for c in range(NCH):
                    wait_alone(pool, normed, p * NCH + c + 3, passed)
                    for h in range(2):
                        pool.dma_start(att_d[bass.ds(p * 2 * HD + h * HD, HD), c * CH:(c + 1) * CH],
                                       att[h * 2 * HD:h * 2 * HD + HD, c % 2, :]).then_inc(stored, 16)
                    pool.wait_ge(stored, (p * NCH + c) * 32 + 32)
                    pool.sem_inc(att_free, 1)
            pairs(pool, body)


def attention_constants():
    i, j = np.arange(P)[:, None], np.arange(P)[None, :]
    cst = np.stack([np.eye(P), np.where(j > i, NEG, 0.0), np.where(i > j, NEG, 0.0)], axis=1).astype(np.float32)
    slope = np.float32([1.0 / 2 ** (h / 2) for h in range(NH)])
    hi = (slope.view(np.uint32) & np.uint32(0xFFFFF000)).view(np.float32)
    lo = slope - hi
    pos = np.arange(T, dtype=np.float32)
    one = np.ones(T, np.float32)
    q = np.stack([np.stack([-pos, hi[h] * one, -pos, lo[h] * one]) for h in range(NH)])
    k = np.stack([np.stack([hi[h] * one, pos, lo[h] * one, pos, one, one]) for h in range(NH)])
    return cst, q.reshape(NH * 4, T), k.reshape(NH * 6, T)


def expert_stage(nc, name, expert, act_fn, wg_d, wa_d, wb_d, bias_d, xh_d, xl_d, resid_d, out_d,
                 wo_d=None, att_d=None):
    proj = wo_d is not None
    with Stage(nc, name) as st:
        wah, wal = st.sb("wah", [P, KT, FH], F32R), st.sb("wal", [P, KT, FH], F32R)
        wbh, wbl = st.sb("wbh", [P, FT, D], F32R), st.sb("wbl", [P, FT, D], F32R)
        pieces = [(wa_d[k * P:(k + 1) * P, :], wah[:, k, :], wal[:, k, :]) for k in range(KT)]
        pieces += [(wb_d[f * P:(f + 1) * P, :], wbh[:, f, :], wbl[:, f, :]) for f in range(FT)]
        if proj:
            woh, wol = st.sb("woh", [P, KT, D], F32R), st.sb("wol", [P, KT, D], F32R)
            pieces += [(wo_d[k * P:(k + 1) * P, :], woh[:, k, :], wol[:, k, :]) for k in range(KT)]
            at = [st.sb(f"at{i}", [P, KT, CH]) for i in range(2)]
            ath, atl = st.sb("ath", [P, KT, CH], F32R), st.sb("atl", [P, KT, CH], F32R)
        ws = WeightSplit(st, FH, pieces)
        wg = st.sb("wg", [P, 2, KT])
        wd = st.sb("wd", [P, KT])
        wdw = st.sb("wdw", [P, KT, P])
        wdh, wdl = st.sb("wdh", [P, KT, P], F32R), st.sb("wdl", [P, KT, P], F32R)
        bias = st.sb("bias", [P, FT + 2 * KT])
        xh = [st.sb(f"xh{i}", [P, KT, CH], F32R) for i in range(2)]
        xl = [st.sb(f"xl{i}", [P, KT, CH], F32R) for i in range(2)]
        resid = st.sb("resid", [P, KT, CH])
        mask = st.sb("mask", [P, CH])
        hid = st.sb("hid", [P, 2, CH])
        masked = st.sb("masked", [P, 2, CH])
        hh, hl = st.sb("hh", [P, 2, CH], F32R), st.sb("hl", [P, 2, CH], F32R)
        y = st.sb("y", [P, KT, CH])
        gate, up, down = st.ps("gate", [P, CH]), st.ps("up", [P, 2, CH]), st.ps("down", [P, KT, CH])
        s_in, gate_w = st.sem("s_in"), st.sem("gate_w")
        x_in = [st.sem(f"x_in{i}") for i in range(2)]
        at_in, r_in = [st.sem(f"at_in{i}") for i in range(2)], st.sem("r_in")
        gated, masks = st.sem("gated"), st.sem("masks")
        upped, activated, hmasked = st.sem("upped"), st.sem("activated"), st.sem("hmasked")
        hi_ready, lo_ready, downed = st.sem("hi_ready"), st.sem("lo_ready"), st.sem("downed")
        at_hi, at_lo, at_used = st.sem("at_hi"), st.sem("at_lo"), st.sem("at_used")
        biased, added, y_ready = st.sem("biased"), st.sem("added"), st.sem("y_ready")
        stored, y_free = st.sem("stored"), st.sem("y_free")
        passed = st.sem("passed")
        block = st.block()
        LEAD = 2 * FT

        @block.sync
        def _(sp):
            sp.dma_start(wg[:], wg_d).then_inc(s_in, 16)
            sp.dma_start(bias[:], bias_d).then_inc(s_in, 16)
            ws.load(sp)
            for r, par, c in chunk_loop(sp):
                sp.wait_ge(downed, c * FT + FT)
                sp.dma_start(xh[par][:].bitcast(F32), tok(feat(xh_d), c)).then_inc(x_in[par], 16)
                sp.dma_start(xl[par][:].bitcast(F32), tok(feat(xl_d), c)).then_inc(x_in[par], 16)
                if proj:
                    sp.wait_ge(at_lo, c + 1)
                    sp.dma_start(at[par][:], tok(feat(att_d), c)).then_inc(at_in[par], 16)
                sp.wait_ge(y_ready, c + 1)
                sp.dma_start(resid[:], tok(feat(resid_d), c)).then_inc(r_in, 16)

        @block.tensor
        def _(pe):
            pe.sem_inc(downed, LEAD)
            if proj:
                pe.sem_inc(at_used, 1)
            ws.wait(pe)
            pe.wait_ge(gate_w, 4)
            for r, par, c in chunk_loop(pe):
                def up_product(f):
                    pe.wait_ge(activated, c * FT + f + 1)
                    for k in range(KT):
                        s = slice(f * P, (f + 1) * P)
                        last = three_passes(pe, up[:, f % 2, :], wah[:, k, s], wal[:, k, s],
                                            xh[par][:, k, :], xl[par][:, k, :], k == 0, k == KT - 1)
                    last.then_inc(upped, 1)

                def down_product(f):
                    pe.wait_ge(lo_ready, c * FT + f + 3)
                    for m in range(KT):
                        s = slice(m * P, (m + 1) * P)
                        last = three_passes(pe, down[:, m, :], wbh[:, f, s], wbl[:, f, s], hh[:, f % 2, :],
                                            hl[:, f % 2, :], f == 0 and not proj, f == FT - 1)
                    last.then_inc(downed, 1)

                pe.wait_ge(x_in[par], r * 32 + 32)
                pe.wait_ge(masks, c + 1)
                for k in range(KT):
                    last = three_passes(pe, gate[:], wdh[:, k, :], wdl[:, k, :], xh[par][:, k, :],
                                        xl[par][:, k, :], k == 0, k == KT - 1)
                last.then_inc(gated, 1)
                up_product(0)
                up_product(1)
                pe.wait_ge(added, c + 1)
                if proj:
                    pe.wait_ge(at_lo, c + 3)
                    for m in range(KT):
                        s = slice(m * P, (m + 1) * P)
                        for k in range(KT):
                            last = three_passes(pe, down[:, m, :], woh[:, k, s], wol[:, k, s],
                                                ath[:, k, :], atl[:, k, :], k == 0, False)
                    last.then_inc(at_used, 1)
                for f in range(FT):
                    down_product(f)
                    if f + 2 < FT:
                        up_product(f + 2)

        @block.scalar
        def _(act):
            act.sem_inc(activated, 2)
            ws.hi(act)
            for r, par, c in chunk_loop(act):
                def high(f):
                    act.wait_ge(hmasked, c * FT + f + 3)
                    act.wait_ge(downed, c * FT + f - 1 + LEAD)
                    act.activation(hh[:, f % 2, :], masked[:, f % 2, :], ACT.Copy).then_inc(hi_ready, 1)

                for f in range(FT):
                    act.wait_ge(upped, c * FT + f + 1)
                    act.wait_ge(hmasked, c * FT + f + 1)
                    act.activation(hid[:, f % 2, :], up[:, f % 2, :], act_fn,
                                   bias=bias[:, f:f + 1]).then_inc(activated, 1)
                    if f == 0 and proj:
                        act.wait_ge(at_in[par], r * 16 + 16)
                        act.wait_ge(at_used, c + 1)
                        act.activation(ath[:], at[par][:], ACT.Copy).then_inc(at_hi, 1)
                    if f:
                        high(f - 1)
                high(FT - 1)

        @block.vector
        def _(dve):
            dve.sem_inc(masks, 1)
            dve.sem_inc(hmasked, 2)
            dve.sem_inc(lo_ready, 2)
            dve.sem_inc(added, 1)
            dve.sem_inc(y_ready, 1)
            if proj:
                dve.sem_inc(at_lo, 2)
            dve.wait_ge(s_in, 32)
            dve.tensor_tensor(wd[:], wg[:, 0, :], wg[:, 1, :], ALU.subtract).then_inc(gate_w, 1)
            dve.wait_ge(gate_w, 1)
            dve.tensor_copy(wdw[:], wd[:].rearrange("p (k a) -> p k a", a=1).to_broadcast([P, KT, P])).then_inc(gate_w, 1)
            dve.wait_ge(gate_w, 2)
            dve.tensor_copy(wdh[:], wdw[:]).then_inc(gate_w, 1)
            dve.wait_ge(gate_w, 3)
            dve.tensor_tensor(wdl[:], wdw[:], wdh[:].bitcast(F32), ALU.subtract).then_inc(gate_w, 1)
            ws.lo(dve)
            for r, par, c in chunk_loop(dve):
                def low(f):
                    dve.wait_ge(hi_ready, c * FT + f + 1)
                    dve.tensor_tensor(hl[:, f % 2, :], masked[:, f % 2, :], hh[:, f % 2, :].bitcast(F32),
                                      ALU.subtract).then_inc(lo_ready, 1)

                dve.wait_ge(gated, c + 1)
                dve.wait_ge(biased, c * KT + KT)
                dve.tensor_scalar(mask[:], gate[:], 0.0, None,
                                  ALU.is_ge if expert == 0 else ALU.is_lt).then_inc(masks, 1)
                dve.wait_ge(masks, c + 2)
                for f in range(FT):
                    dve.wait_ge(activated, c * FT + f + 3)
                    dve.wait_ge(lo_ready, c * FT + f + 1)
                    dve.tensor_tensor(masked[:, f % 2, :], hid[:, f % 2, :], mask[:], ALU.mult).then_inc(hmasked, 1)
                    if f == 0 and proj:
                        dve.wait_ge(at_hi, c + 1)
                        dve.tensor_tensor(atl[:], at[par][:], ath[:].bitcast(F32), ALU.subtract).then_inc(at_lo, 1)
                    if f:
                        low(f - 1)
                low(FT - 1)
                dve.wait_ge(y_free, c + 1)
                for m in range(KT):
                    dve.tensor_scalar(y[:, m, :], mask[:], bias[:, FT + m:FT + m + 1],
                                      bias[:, FT + KT + m:FT + KT + m + 1], ALU.mult, ALU.add).then_inc(biased, 1)
                dve.wait_ge(r_in, c * 16 + 16)
                dve.wait_ge(biased, c * KT + 2 * KT)
                dve.wait_ge(downed, c * FT + FT + LEAD)
                dve.tensor_tensor(y[:], y[:], down[:], ALU.add).then_inc(added, 1)
                dve.wait_ge(added, c + 2)
                dve.tensor_tensor(y[:], y[:], resid[:], ALU.add).then_inc(y_ready, 1)

        @block.gpsimd
        def _(pool):
            pool.sem_inc(y_free, 1)
            pool.sem_inc(biased, KT)
            for r, par, c in chunk_loop(pool):
                wait_alone(pool, y_ready, c + 2, passed)
                pool.dma_start(tok(feat(out_d), c), y[:]).then_inc(stored, 16)
                pool.wait_ge(stored, c * 16 + 16)
                pool.sem_inc(y_free, 1)


def glu_stage(nc, w1_d, w2_d, w3_d, xh_d, xl_d, resid_d, out_d):
    with Stage(nc, "glu") as st:
        w1, w2 = st.sb("w1", [P, KT, GH], F32R), st.sb("w2", [P, KT, GH], F32R)
        w3 = st.sb("w3", [P, GT, D], F32R)
        raw = st.sb("raw", [P, KT, GH])
        below = st.sb("below", [P, GH])
        asum, gam = st.sb("asum", [P, 3]), st.sb("gam", [P, 3, 2])
        ones = st.sb("ones", [P, P])
        xh = [st.sb(f"xh{i}", [P, KT, CH], F32R) for i in range(2)]
        xl = [st.sb(f"xl{i}", [P, KT, CH], F32R) for i in range(2)]
        resid, y = st.sb("resid", [P, KT, CH]), st.sb("y", [P, KT, CH])
        sig, hid = st.sb("sig", [P, 2, CH]), st.sb("hid", [P, 2, CH])
        hh, hl = st.sb("hh", [P, 2, CH], F32R), st.sb("hl", [P, 2, CH], F32R)
        u1, u2, down = st.ps("u1", [P, 2, CH]), st.ps("u2", [P, 2, CH]), st.ps("down", [P, KT, CH])
        raw_in, abs_done, total = st.sem("raw_in"), st.sem("abs_done"), st.sem("total")
        thr, cut, ternary = st.sem("thr"), st.sem("cut"), st.sem("ternary")
        x_in, r_in = [st.sem(f"x_in{i}") for i in range(2)], st.sem("r_in")
        upped, sig_ready, hid_ready = st.sem("upped"), st.sem("sig_ready"), st.sem("hid_ready")
        hi_ready, lo_ready, downed = st.sem("hi_ready"), st.sem("lo_ready"), st.sem("downed")
        added, y_ready, stored, y_free = st.sem("added"), st.sem("y_ready"), st.sem("stored"), st.sem("y_free")
        passed = st.sem("passed")
        block = st.block()
        LEAD = 2 * GT
        weights = [(w1_d, w1[:].rearrange("p a b -> p (a b)")), (w2_d, w2[:].rearrange("p a b -> p (a b)")),
                   (w3_d, w3[:].rearrange("p a b -> p (a b)"))]
        flat = raw[:].rearrange("p a b -> p (a b)")

        @block.sync
        def _(sp):
            for j, (w_d, q) in enumerate(weights):
                if j:
                    sp.wait_ge(ternary, j * KT)
                sp.dma_start(raw[:] if j < 2 else flat.rearrange("p (a b) -> p a b", b=D),
                             w_d.rearrange("(k p) n -> p k n", p=P)).then_inc(raw_in, 16)
            for r, par, c in chunk_loop(sp):
                sp.wait_ge(downed, c * GT + GT)
                sp.dma_start(xh[par][:].bitcast(F32), tok(feat(xh_d), c)).then_inc(x_in[par], 16)
                sp.dma_start(xl[par][:].bitcast(F32), tok(feat(xl_d), c)).then_inc(x_in[par], 16)
                sp.wait_ge(y_ready, c + 1)
                sp.dma_start(resid[:], tok(feat(resid_d), c)).then_inc(r_in, 16)

        @block.tensor
        def _(pe):
            pe.sem_inc(downed, LEAD)
            for j in range(3):
                pe.wait_ge(abs_done, j + 2)
                pe.matmul(u1[:, 0, 0:1], ones[:], asum[:, j:j + 1], start=True, stop=True).then_inc(total, 1)
            pe.wait_ge(ternary, 3 * KT)
            for r, par, c in chunk_loop(pe):
                def up_product(f):
                    n = par * GT + f
                    s = slice(f * P, (f + 1) * P)
                    pe.wait_ge(hid_ready, c * GT + f + 1)
                    for w, u in ((w1, u1), (w2, u2)):
                        for k in range(KT):
                            pe.matmul(u[:, n % 2, :], w[:, k, s], xh[par][:, k, :], start=k == 0, stop=False)
                            last = pe.matmul(u[:, n % 2, :], w[:, k, s], xl[par][:, k, :], start=False, stop=k == KT - 1)
                    last.then_inc(upped, 1)

                def down_product(f):
                    n = par * GT + f
                    pe.wait_ge(lo_ready, c * GT + f + 3)
                    for m in range(KT):
                        w = w3[:, f, m * P:(m + 1) * P]
                        pe.matmul(down[:, m, :], w, hh[:, n % 2, :], start=f == 0, stop=False)
                        last = pe.matmul(down[:, m, :], w, hl[:, n % 2, :], start=False, stop=f == GT - 1)
                    last.then_inc(downed, 1)

                pe.wait_ge(x_in[par], r * 32 + 32)
                up_product(0)
                up_product(1)
                pe.wait_ge(added, c + 1)
                for f in range(GT):
                    down_product(f)
                    if f + 2 < GT:
                        up_product(f + 2)

        @block.scalar
        def _(act):
            for r, par, c in chunk_loop(act):
                def high(f):
                    n = par * GT + f
                    act.wait_ge(hid_ready, c * GT + f + 3)
                    act.wait_ge(downed, c * GT + f - 1 + LEAD)
                    act.activation(hh[:, n % 2, :], hid[:, n % 2, :], ACT.Copy).then_inc(hi_ready, 1)

                for f in range(GT):
                    n = par * GT + f
                    act.wait_ge(upped, c * GT + f + 1)
                    act.wait_ge(hid_ready, c * GT + f + 1)
                    act.activation(sig[:, n % 2, :], u1[:, n % 2, :], ACT.Sigmoid).then_inc(sig_ready, 1)
                    if f:
                        high(f - 1)
                high(GT - 1)

        @block.vector
        def _(dve):
            dve.sem_inc(hid_ready, 2)
            dve.sem_inc(lo_ready, 2)
            dve.sem_inc(added, 1)
            dve.sem_inc(y_ready, 1)
            dve.memset(ones[:], 1.0 / (D * GH)).then_inc(abs_done, 1)
            for j, (w_d, q) in enumerate(weights):
                dve.wait_ge(raw_in, j * 16 + 16)
                dve.tensor_reduce(asum[:, j:j + 1], flat, AX.X, ALU.add, apply_absolute_value=True).then_inc(abs_done, 1)
                dve.wait_ge(total, j + 1)
                dve.tensor_scalar(gam[:, j, 0:1], u1[:, 0, 0:1], 1e-8, 0.5, ALU.add, ALU.mult).then_inc(thr, 1)
                dve.tensor_scalar(gam[:, j, 1:2], u1[:, 0, 0:1], 1e-8, -0.5, ALU.add, ALU.mult).then_inc(thr, 1)
                dve.wait_ge(thr, 2 * j + 2)
                for k in range(KT):
                    s, i = slice(k * GH, (k + 1) * GH), j * KT + k
                    if i:
                        dve.wait_ge(ternary, i)
                    dve.tensor_scalar(below[:], flat[:, s], gam[:, j, 1:2], None, ALU.is_lt).then_inc(cut, 1)
                    dve.wait_ge(cut, i + 1)
                    dve.scalar_tensor_tensor(out=q[:, s], in0=flat[:, s], scalar=gam[:, j, 0:1], in1=below[:],
                                             op0=ALU.is_gt, op1=ALU.subtract).then_inc(ternary, 1)
            for r, par, c in chunk_loop(dve):
                def low(f):
                    n = par * GT + f
                    dve.wait_ge(hi_ready, c * GT + f + 1)
                    dve.tensor_tensor(hl[:, n % 2, :], hid[:, n % 2, :], hh[:, n % 2, :].bitcast(F32),
                                      ALU.subtract).then_inc(lo_ready, 1)

                for f in range(GT):
                    n = par * GT + f
                    dve.wait_ge(sig_ready, c * GT + f + 1)
                    dve.wait_ge(lo_ready, c * GT + f + 1)
                    dve.tensor_tensor(hid[:, n % 2, :], sig[:, n % 2, :], u2[:, n % 2, :], ALU.mult).then_inc(hid_ready, 1)
                    if f:
                        low(f - 1)
                low(GT - 1)
                dve.wait_ge(y_free, c + 1)
                dve.wait_ge(r_in, c * 16 + 16)
                dve.wait_ge(downed, c * GT + GT + LEAD)
                dve.tensor_tensor(y[:], resid[:], down[:], ALU.add).then_inc(added, 1)
                dve.wait_ge(added, c + 2)
                dve.sem_inc(y_ready, 1)

        @block.gpsimd
        def _(pool):
            pool.sem_inc(y_free, 1)
            for r, par, c in chunk_loop(pool):
                wait_alone(pool, added, c + 2, passed)
                pool.dma_start(tok(feat(out_d), c), y[:]).then_inc(stored, 16)
                pool.wait_ge(stored, c * 16 + 16)
                pool.sem_inc(y_free, 1)


RING = ["act"] * (2 * KT) + ["act"] * TT + ["act"] + ["act"] * KT + ["dve"] * KT + ["dve"] + ["dve"] * KT + ["dve"] * KT
R_Q, R_K, R_V, R_GK, R_GATE = 0, KT, 2 * KT, 2 * KT + TT, 2 * KT + TT + 1
R_TURN, R_MS, R_SPREAD, R_OUT = R_GATE + KT, R_GATE + 2 * KT, R_GATE + 2 * KT + 1, R_GATE + 3 * KT + 1
NR = len(RING)
READS = {e: RING.count(e) for e in ("act", "dve")}


def reads_to(n):
    return RING[:n + 1].count(RING[n])


def lightning_stage(nc, cst_d, w_d, wg1_d, wg2_d, decay_p_d, decay_f_d, norm_w_d, xh_d, xl_d, resid_d, out_d):
    with Stage(nc, "lin") as st:
        NC = 4 * P + HD + KT * P + P + 1
        cst = st.sb("cst", [P, NC])
        at = np.cumsum([0, P, P, P, P, HD, KT * P, P, 1])
        dist, causal, cpos, diag, msel, spread, ident, kpos = (cst[:, a:b] for a, b in zip(at[:-1], at[1:]))
        names = ("q", "k", "v", "o")
        wh = {n: st.sb(f"w{n}h", [P, KT, D], F32R) for n in names}
        wl = {n: st.sb(f"w{n}l", [P, KT, D], F32R) for n in names}
        g1h, g1l = st.sb("g1h", [P, KT, P], F32R), st.sb("g1l", [P, KT, P], F32R)
        g2 = st.sb("g2", [P, D])
        pieces = [(w_d[n][k * P:(k + 1) * P, :], wh[n][:, k, :], wl[n][:, k, :]) for n in names for k in range(KT)]
        pieces += [(wg1_d[k * P:(k + 1) * P, :], g1h[:, k, 0:HD], g1l[:, k, 0:HD]) for k in range(KT)]
        ws = WeightSplit(st, D, pieces)
        ld_p, ld_f, nw = st.sb("ld_p", [P, KT]), st.sb("ld_f", [P, NH]), st.sb("nw", [P, KT])
        eps = st.sb("eps", [P, 1])
        pair_decay = st.sb("pair_decay", [P, NH, P])
        q_decay = st.sb("q_decay", [P, KT, P])
        k_decay16, k_decay = st.sb("k_decay16", [P, NH]), st.sb("k_decay", [P, D])
        c_decay = st.sb("c_decay", [P, KT])
        xh, xl = st.sb("xh", [P, KT, CH], F32R), st.sb("xl", [P, KT, CH], F32R)
        qt, qd = st.sb("qt", [P, KT, CH]), st.sb("qd", [P, KT, CH])
        qblk = st.sb("qblk", [P, 2, KT, HPG, P])
        kt_, kd = st.sb("kt", [P, KT, CH]), st.sb("kd", [P, KT, TT, P])
        v = st.sb("v", [P, TT, D])
        gk, sig = st.sb("gk", [P, CH]), st.sb("sig", [P, KT, CH])
        dec = st.sb("dec", [P, 2, HPG, P])
        state, fresh = st.sb("state", [P, KT, P]), st.sb("fresh", [P, P])
        og = qt
        ogh, ogl = st.sb("ogh", [P, KT, CH], F32R), st.sb("ogl", [P, KT, CH], F32R)
        root, inv, tmp = gk, st.sb("inv", [P, CH]), st.sb("tmp", [P, CH])
        y = st.sb("y", [P, KT, CH])
        ring, pair, upd = st.ps("ring", [P, 2, CH]), st.ps("pair", [P, HPG, P]), st.ps("upd", [P, CH])
        o = st.ps("o", [P, KT, CH])
        s_in, zeroed, expd, masked = st.sem("s_in"), st.sem("zeroed"), st.sem("expd"), st.sem("masked")
        x_in, r_in = st.sem("x_in"), st.sem("r_in")
        made, taken = st.sem("made"), {e: st.sem(f"taken_{e}") for e in ("act", "dve")}
        qd_ready, qblk_ready = st.sem("qd_ready"), st.sem("qblk_ready")
        paired, decayed, o_made = st.sem("paired"), st.sem("decayed"), st.sem("o_made")
        updated, fresh_ready, state_ready = st.sem("updated"), st.sem("fresh_ready"), st.sem("state_ready")
        gated, squared, root_ready, newton = st.sem("gated"), st.sem("squared"), st.sem("root_ready"), st.sem("newton")
        normed, hi_ready, lo_ready = st.sem("normed"), st.sem("hi_ready"), st.sem("lo_ready")
        stored, y_free = st.sem("stored"), st.sem("y_free")
        passed = st.sem("passed")
        block = st.block()
        NI, LINKS = TT * KT, 5

        def wait_taken(eng, c, n):
            e = RING[n]
            eng.wait_ge(taken[e], (c + 1) * READS[e] + reads_to(n))

        @block.sync
        def _(sp):
            for dst, src in ((cst, cst_d), (ld_p, decay_p_d), (ld_f, decay_f_d), (nw, norm_w_d)):
                sp.dma_start(dst[:], src).then_inc(s_in, 16)
            ws.load(sp)
            sp.wait_ge(zeroed, 1)
            sp.dma_start(g2[0:HD, :], wg2_d).then_inc(s_in, 16)
            for r, par, c in chunk_loop(sp):
                sp.wait_ge(made, c * NR + R_GATE)
                sp.dma_start(xh[:].bitcast(F32), tok(feat(xh_d), c)).then_inc(x_in, 16)
                sp.dma_start(xl[:].bitcast(F32), tok(feat(xl_d), c)).then_inc(x_in, 16)
                sp.wait_ge(y_free, c + 1)
                sp.dma_start(y[:], tok(feat(resid_d), c)).then_inc(r_in, 16)

        @block.tensor
        def _(pe):
            pe.sem_inc(made, NR)
            pe.sem_inc(paired, 2 * KT)
            pe.sem_inc(o_made, 2)
            pe.sem_inc(updated, 1)
            ws.wait(pe)
            pe.wait_ge(s_in, 5 * 16)
            pe.wait_ge(zeroed, 5)
            for r, par, c in chunk_loop(pe):
                def slot(n):
                    m = n - 2
                    wait_taken(pe, *((c, m) if m >= 0 else (c - 1, m + NR)))
                    return ring[:, n % 2, :]

                def projected(n, w, m, lhs_is_x=False):
                    out, s = slot(n), slice(m * P, (m + 1) * P)
                    for k in range(KT):
                        edge = (k == 0, k == KT - 1)
                        if lhs_is_x:
                            last = three_passes(pe, out, xh[:, k, s], xl[:, k, s], wh[w][:, k, :], wl[w][:, k, :], *edge)
                        else:
                            last = three_passes(pe, out, wh[w][:, k, s], wl[w][:, k, s], xh[:, k, :], xl[:, k, :], *edge)
                    last.then_inc(made, 1)

                pe.wait_ge(x_in, c * 32 + 32)
                for m in range(KT):
                    projected(R_Q + m, "q", m)
                for m in range(KT):
                    projected(R_K + m, "k", m)
                for t in range(TT):
                    projected(R_V + t, "v", t, True)
                out = slot(R_GK)
                for k in range(KT):
                    last = three_passes(pe, out, g1h[:, k, :], g1l[:, k, :], xh[:, k, :], xl[:, k, :], k == 0, k == KT - 1)
                last.then_inc(made, 1)
                for g in range(KT):
                    out = slot(R_GATE + g)
                    if g == 0:
                        wait_taken(pe, c, R_GK)
                    pe.matmul(out, g2[:, g * P:(g + 1) * P], gk[:], start=True, stop=True).then_inc(made, 1)
                for g in range(KT):
                    out = slot(R_TURN + g)
                    wait_taken(pe, c, R_K + g)
                    for t in range(TT):
                        last = pe.transpose(out[:, t * P:(t + 1) * P], kt_[:, g, t * P:(t + 1) * P], ident)
                    last.then_inc(made, 1)

                def score(i):
                    t, g = divmod(i, KT)
                    pe.wait_ge(decayed, c * NI + i + 1)
                    pe.wait_ge(qblk_ready, c * NI + i + 2)
                    pe.matmul(pair[:].rearrange("p h c -> p (h c)"), kt_[:, g, t * P:(t + 1) * P],
                              qblk[:, t % 2, g].rearrange("p h c -> p (h c)"), start=True, stop=True).then_inc(paired, 1)

                def attend(i):
                    t, g = divmod(i, KT)
                    s = slice(t * P, (t + 1) * P)
                    pe.wait_ge(state_ready, c * NI + i + 1)
                    pe.wait_ge(decayed, c * NI + i + 2)
                    if i == 0:
                        pe.wait_ge(qd_ready, c * KT + 2 * KT)
                        pe.wait_ge(gated, c + 1)
                        wait_taken(pe, c, R_V + TT - 1)
                    pe.matmul(o[:, g, s], state[:, g, :], qd[:, g, s], start=True, stop=False, skip_group_check=True)
                    for h in range(HPG):
                        f = (g * HPG + h) * HD
                        last = pe.matmul(o[h * HD:(h + 1) * HD, g, s], v[:, t, f:f + HD], dec[:, i % 2, h, :],
                                         start=False, stop=True, skip_group_check=True)
                    last.then_inc(o_made, 1)
                    if t == 0:
                        wait_taken(pe, c, R_TURN + g)
                    pe.wait_ge(fresh_ready, c * NI + i + 1)
                    pe.matmul(upd[:, 0:P], kd[:, g, t, :], v[:, t, g * P:(g + 1) * P], start=True,
                              stop=True).then_inc(updated, 1)

                for i in range(NI):
                    score(i)
                    if i:
                        attend(i - 1)
                attend(NI - 1)
                out = slot(R_MS)
                pe.wait_ge(squared, c + 1)
                for g in range(KT):
                    last = pe.matmul(ring[g * HD:(g + 1) * HD, R_MS % 2, :], msel, sig[:, g, :], start=True, stop=True,
                                     skip_group_check=True)
                last.then_inc(made, 1)
                for g in range(KT):
                    slot(R_SPREAD + g)
                    if g == 0:
                        pe.wait_ge(newton, (c + 1) * LINKS + 1)
                    pe.matmul(ring[:, (R_SPREAD + g) % 2, :], spread[:, g * P:(g + 1) * P], inv[:], start=True,
                              stop=True).then_inc(made, 1)
                for m in range(KT):
                    out, s = slot(R_OUT + m), slice(m * P, (m + 1) * P)
                    pe.wait_ge(lo_ready, c * KT + 2 * KT)
                    for k in range(KT):
                        last = three_passes(pe, out, wh["o"][:, k, s], wl["o"][:, k, s], ogh[:, k, :], ogl[:, k, :],
                                            k == 0, k == KT - 1)
                    last.then_inc(made, 1)

        @block.scalar
        def _(act):
            act.sem_inc(taken["act"], READS["act"])
            act.wait_ge(s_in, 4 * 16)
            for h in range(NH):
                act.activation(pair_decay[:, h, :], dist, ACT.Exp, scale=ld_f[:, h:h + 1]).then_inc(expd, 1)
            for g in range(KT):
                act.activation(q_decay[:, g, :], cpos, ACT.Exp, scale=ld_p[:, g:g + 1]).then_inc(expd, 1)
            act.activation(k_decay16[:], ld_f[:], ACT.Exp, scale=kpos).then_inc(expd, 1)
            act.activation(c_decay[:], ld_p[:], ACT.Exp, scale=float(P)).then_inc(expd, 1)
            ws.hi(act)
            for r, par, c in chunk_loop(act):
                def arrived(n):
                    act.wait_ge(made, (c + 1) * NR + n + 1)
                    return ring[:, n % 2, :]

                act.wait_ge(qblk_ready, c * NI + 1)
                act.wait_ge(qd_ready, c * KT + KT)
                act.wait_ge(lo_ready, c * KT + KT)
                for g in range(KT):
                    act.activation(qt[:, g, :], arrived(R_Q + g), ACT.Silu).then_inc(taken["act"], 1)
                act.wait_ge(paired, c * NI + 2 * KT)
                for g in range(KT):
                    act.activation(kt_[:, g, :], arrived(R_K + g), ACT.Silu).then_inc(taken["act"], 1)
                act.wait_ge(updated, c * NI + 1)
                for t in range(TT):
                    act.activation(v[:, t, :], arrived(R_V + t), ACT.Silu).then_inc(taken["act"], 1)
                act.wait_ge(newton, c * LINKS + 1)
                act.activation(gk[:], arrived(R_GK), ACT.Copy).then_inc(taken["act"], 1)
                act.wait_ge(made, (c + 1) * NR + R_MS + 1 - NR)
                for g in range(KT):
                    act.activation(sig[:, g, :], arrived(R_GATE + g), ACT.Sigmoid).then_inc(taken["act"], 1)
                act.wait_ge(gated, c + 2)
                act.activation(sig[:], og[:], ACT.Square).then_inc(squared, 1)
                act.activation(root[:], arrived(R_MS), ACT.Sqrt, bias=eps[:, 0:1]).then_inc(root_ready, 1)
                act.wait_ge(made, (c + 1) * NR)
                for g in range(KT):
                    act.wait_ge(normed, c * KT + g + 1)
                    act.activation(ogh[:, g, :], og[:, g, :], ACT.Copy).then_inc(hi_ready, 1)

        @block.vector
        def _(dve):
            dve.sem_inc(taken["dve"], READS["dve"])
            dve.sem_inc(qd_ready, KT)
            dve.sem_inc(decayed, 1)
            dve.sem_inc(fresh_ready, 1)
            dve.sem_inc(state_ready, KT)
            dve.sem_inc(gated, 1)
            dve.sem_inc(lo_ready, KT)
            dve.sem_inc(newton, 1)
            dve.memset(g2[:], 0.0).then_inc(zeroed, 1)
            dve.memset(g1h[:].bitcast(F32), 0.0).then_inc(zeroed, 1)
            dve.memset(g1l[:].bitcast(F32), 0.0).then_inc(zeroed, 1)
            dve.memset(state[:], 0.0).then_inc(zeroed, 1)
            dve.memset(eps[:], LN_EPS).then_inc(zeroed, 1)
            dve.wait_ge(expd, NH + KT + 2)
            for g in range(KT):
                s = slice(g * HPG, (g + 1) * HPG)
                dve.tensor_tensor(pair_decay[:, s, :], pair_decay[:, s, :],
                                  causal.rearrange("p (a c) -> p a c", a=1).to_broadcast([P, HPG, P]),
                                  ALU.mult).then_inc(masked, 1)
            dve.tensor_copy(k_decay[:].rearrange("p (h d) -> p h d", d=HD),
                            k_decay16[:].rearrange("p (h a) -> p h a", a=1).to_broadcast([P, NH, HD])).then_inc(masked, 1)
            ws.lo(dve)
            dve.wait_ge(masked, KT + 1)
            for r, par, c in chunk_loop(dve):
                def arrived(n):
                    dve.wait_ge(made, (c + 1) * NR + n + 1)
                    return ring[:, n % 2, :]

                for g in range(KT):
                    wait_taken(dve, c, R_Q + g)
                    dve.wait_ge(o_made, c * NI + 2)
                    dve.tensor_tensor(qd[:, g, :].rearrange("p (t c) -> p t c", c=P),
                                      qt[:, g, :].rearrange("p (t c) -> p t c", c=P),
                                      q_decay[:, g:g + 1, :].to_broadcast([P, TT, P]), ALU.mult).then_inc(qd_ready, 1)
                dve.wait_ge(updated, c * NI + 1)
                for g in range(KT):
                    dve.tensor_tensor(kd[:, g, :, :], arrived(R_TURN + g).rearrange("p (t f) -> p t f", f=P),
                                      k_decay[:, g * P:(g + 1) * P].rearrange("p (a f) -> p a f", a=1).to_broadcast([P, TT, P]),
                                      ALU.mult).then_inc(taken["dve"], 1)

                def decay(i):
                    t, g = divmod(i, KT)
                    dve.wait_ge(paired, c * NI + i + 1 + 2 * KT)
                    dve.wait_ge(o_made, c * NI + i + 1)
                    dve.tensor_tensor(dec[:, i % 2], pair[:], pair_decay[:, g * HPG:(g + 1) * HPG, :],
                                      ALU.mult).then_inc(decayed, 1)

                def advance(i):
                    t, g = divmod(i, KT)
                    dve.wait_ge(updated, c * NI + i + 2)
                    dve.wait_ge(state_ready, c * NI + i + KT)
                    dve.tensor_tensor(fresh[:], upd[:, 0:P], diag, ALU.mult).then_inc(fresh_ready, 1)
                    dve.wait_ge(fresh_ready, c * NI + i + 2)
                    dve.wait_ge(o_made, c * NI + i + 3)
                    dve.scalar_tensor_tensor(out=state[:, g, :], in0=state[:, g, :], scalar=c_decay[:, g:g + 1],
                                             in1=fresh[:], op0=ALU.mult, op1=ALU.add).then_inc(state_ready, 1)

                for i in range(NI):
                    decay(i)
                    if i:
                        advance(i - 1)
                advance(NI - 1)
                wait_taken(dve, c, R_GATE + KT - 1)
                dve.wait_ge(qd_ready, (c + 1) * KT + KT)
                dve.wait_ge(qblk_ready, (c + 1) * NI + 1)
                dve.tensor_tensor(og[:], o[:], sig[:], ALU.mult).then_inc(gated, 1)
                dve.wait_ge(root_ready, c + 1)
                chain = Chain(dve, newton, c * LINKS + 1)
                rsqrt_newton(dve, chain, inv[:], tmp[:], root[:], ring[:, R_MS % 2, :], LN_EPS)
                dve.sem_inc(taken["dve"], 1)
                assert chain.n == LINKS
                for g in range(KT):
                    dve.scalar_tensor_tensor(out=og[:, g, :], in0=og[:, g, :], scalar=nw[:, g:g + 1],
                                             in1=arrived(R_SPREAD + g), op0=ALU.mult, op1=ALU.mult).then_inc(normed, 1)
                    dve.wait_ge(normed, c * KT + g + 1)
                    dve.sem_inc(taken["dve"], 1)
                for g in range(KT):
                    dve.wait_ge(hi_ready, c * KT + g + 1)
                    dve.tensor_tensor(ogl[:, g, :], og[:, g, :], ogh[:, g, :].bitcast(F32),
                                      ALU.subtract).then_inc(lo_ready, 1)
                dve.wait_ge(r_in, c * 16 + 16)
                for m in range(KT):
                    dve.tensor_tensor(y[:, m, :], y[:, m, :], arrived(R_OUT + m), ALU.add).then_inc(taken["dve"], 1)

        @block.gpsimd
        def _(pool):
            pool.sem_inc(qblk_ready, 1)
            pool.sem_inc(y_free, 1)
            pool.memset(qblk[:], 0.0).then_inc(masked, 1)
            pool.wait_ge(masked, KT + 2)
            for r, par, c in chunk_loop(pool):
                for i in range(NI):
                    t, g = divmod(i, KT)
                    if t == 0:
                        wait_taken(pool, c, R_Q + g)
                    wait_alone(pool, paired, c * NI + i + 1, passed)
                    for h in range(HPG):
                        s = slice(h * HD, (h + 1) * HD)
                        last = pool.tensor_copy(qblk[s, t % 2, g, h, :], qt[s, g, t * P:(t + 1) * P])
                    last.then_inc(qblk_ready, 1)
                wait_taken(pool, c, R_OUT + KT - 1)
                pool.dma_start(tok(feat(out_d), c), y[:]).then_inc(stored, 16)
                pool.wait_ge(stored, c * 16 + 16)
                pool.sem_inc(y_free, 1)


def lightning_constants():
    s, c = np.arange(P)[:, None], np.arange(P)[None, :]
    p = np.arange(P)[:, None]
    parts = [np.maximum(c - s, 0), c >= s, np.broadcast_to(c + 1, (P, P)), p // HD == c // HD,
             (p // HD == np.arange(HD)[None, :] % HPG) / HD]
    parts += [p == g * HD + c // HD for g in range(KT)]
    parts += [p == c, P - 1 - p]
    return np.concatenate([np.asarray(a, np.float32) for a in parts], axis=1)


def build(nc, i, out):
    def dram(name, shape):
        return nc.dram_tensor(name, shape, F32).ap()

    aq_d, ak_d = dram("alibi_q_rounded", [NH * 4, T]), dram("alibi_k_rounded", [NH * 6, T])
    xh_d, xl_d = dram("xn_hi", [D, T]), dram("xn_lo", [D, T])
    qh_d, ql_d, kh_d, kl_d = (dram(n, [D, T]) for n in ("q_hi", "q_lo", "k_hi", "k_lo"))
    v_d, att_d = dram("v", [T, D]), dram("att", [D, T])
    y0_d, x1_d, y1_d = dram("y0", [D, T]), dram("x1", [D, T]), dram("y1", [D, T])
    zh_d, zl_d = dram("zn_hi", [D, T]), dram("zn_lo", [D, T])

    alibi_stage(nc, i["alibi_q"], i["alibi_k"], aq_d, ak_d)
    layernorm_stage(nc, "ln0", i["x"], xh_d, xl_d)
    qkv_stage(nc, i["Wqkv"], i["bqk"], i["bv"], xh_d, xl_d, qh_d, ql_d, kh_d, kl_d, v_d)
    attention_stage(nc, i["att_cst"], aq_d, ak_d, qh_d, ql_d, kh_d, kl_d, v_d, att_d)
    expert_stage(nc, "exp0", 0, ACT.Gelu, i["Wg"], i["W0a"], i["W0b"], i["bias0"], xh_d, xl_d, i["x"], y0_d,
                 i["L0_Wo"], att_d)
    expert_stage(nc, "exp1", 1, ACT.Relu, i["Wg"], i["W1a"], i["W1b"], i["bias1"], xh_d, xl_d, y0_d, x1_d)
    layernorm_stage(nc, "ln1", x1_d, zh_d, zl_d)
    lightning_stage(nc, i["lin_cst"], {n: i[f"W{n}"] for n in "qkvo"}, i["Wg1"], i["Wg2"], i["decay_p"], i["decay_f"],
                    i["norm_w"], zh_d, zl_d, x1_d, y1_d)
    glu_stage(nc, i["w1"], i["w2"], i["w3"], zh_d, zl_d, y1_d, out)


def kernel(**inputs):
    import numpy as _np
    import concourse.bacc as _bacc
    from concourse import mybir as _mybir
    from concourse.bass_utils import run_bass_kernel_spmd as _run

    a = {n: _np.asarray(v) for n, v in inputs.items()}

    def by_partition(v):
        return v.reshape(-1, P).T

    att_cst, alibi_q, alibi_k = attention_constants()
    bqkv, ld = a["L0_attn_bqkv"], a["L1_attn_log_decay"]
    none = _np.zeros(D, _np.float32)
    arrays = {
        "x": a["L0_attn_x"][0].T, "Wqkv": a["L0_attn_Wqkv"], "bqk": by_partition(bqkv[:2 * D]),
        "bv": _np.broadcast_to(bqkv[2 * D:], (P, D)), "L0_Wo": a["L0_attn_Wo"],
        "Wg": a["L0_ffn_Wg"].reshape(2, KT, P).transpose(2, 0, 1),
        "W0a": a["L0_ffn_W0a"].T, "W0b": a["L0_ffn_W0b"].T, "W1a": a["L0_ffn_W1a"].T, "W1b": a["L0_ffn_W1b"].T,
        "bias0": _np.concatenate([by_partition(a[n]) for n in ("L0_ffn_b0a", "L0_ffn_b0b", "L0_attn_bo")], 1),
        "bias1": _np.concatenate([by_partition(v) for v in (a["L0_ffn_b1a"], a["L0_ffn_b1b"], none)], 1),
        "Wq": a["L1_attn_Wq"], "Wk": a["L1_attn_Wk"], "Wv": a["L1_attn_Wv"], "Wo": a["L1_attn_Wo"],
        "Wg1": a["L1_attn_Wg1"], "Wg2": a["L1_attn_Wg2"], "norm_w": by_partition(a["L1_attn_norm_w"]),
        "decay_p": _np.repeat(ld.reshape(KT, HPG).T, HD, axis=0), "decay_f": _np.broadcast_to(ld, (P, NH)),
        "w1": a["L1_ffn_w1"].T, "w2": a["L1_ffn_w2"].T, "w3": a["L1_ffn_w3"].T,
        "att_cst": att_cst, "alibi_q": alibi_q, "alibi_k": alibi_k, "lin_cst": lightning_constants(),
    }
    nc = _bacc.Bacc("TRN2", target_bir_lowering=False, num_devices=1)
    given, aps = {}, {}
    for name, v in arrays.items():
        given[f"in_{name}"] = _np.ascontiguousarray(v)
        aps[name] = nc.dram_tensor(f"in_{name}", v.shape, _mybir.dt.from_np(v.dtype), kind="ExternalInput").ap()
    out = nc.dram_tensor("out", (D, T), F32, kind="ExternalOutput").ap()
    build(nc, aps, out)
    r = _run(nc, [given], core_ids=[0])
    return r.results[0]["out"].T.reshape(1, T, D)
```

```python
from contextlib import ExitStack

import numpy as np

import concourse.bass as bass
from concourse import mybir

F32 = mybir.dt.float32
F32R = mybir.dt.float32r
BF16 = mybir.dt.bfloat16
ALU = mybir.AluOpType
ACT = mybir.ActivationFunctionType
AX = mybir.AxisListType

P = 128
T = 2048
D = 512
KT = D // P
CH = 512
NCH = T // CH
NH = 16
HD = D // NH
HPG = P // HD
TT = CH // P
QT = T // P
FH = 1024
FT = FH // P
GH = 1408
GT = GH // P
LN_EPS = 1e-5
NEG = -1e30


class Stage:

    def __init__(self, nc, name):
        self.nc, self.name, self.stack, self.sems = nc, name, ExitStack(), []

    def __enter__(self):
        return self

    def __exit__(self, *a):
        self.stack.__exit__(*a)
        self.nc.clear_and_free_semaphores(self.sems)
        self.nc.all_engine_barrier()

    def sb(self, name, shape, dt=F32):
        return self.stack.enter_context(self.nc.sbuf_tensor(f"{self.name}_{name}", shape, dt))

    def ps(self, name, shape):
        return self.stack.enter_context(self.nc.psum_tensor(f"{self.name}_{name}", shape, F32))

    def sem(self, name):
        self.sems.append(self.nc.alloc_semaphore(f"{self.name}_{name}"))
        return self.sems[-1]

    def block(self):
        return self.stack.enter_context(self.nc.Block())


class Chain:

    def __init__(self, eng, sem, base):
        self.eng, self.sem, self.base, self.n = eng, sem, base, 0

    def link(self, ins):
        self.n += 1
        ins.then_inc(self.sem, 1)
        self.eng.wait_ge(self.sem, self.base + self.n)


def wait_alone(pool, sem, value, passed):
    pool.wait_ge(sem, value)
    pool.sem_inc(passed, 1)


def chunk_loop(eng):
    with eng.Fori(0, NCH // 2) as r:
        for par in range(2):
            yield r, par, r * 2 + par


def feat(ap):
    return ap.rearrange("(k p) t -> p k t", p=P)


def tok(ap, c):
    return ap[:, :, bass.ds(c * CH, CH)]


class WeightSplit:

    def __init__(self, st, width, pieces, depth=4):
        self.pieces, self.depth = pieces, depth
        self.stage = [st.sb(f"wstage{i}", [P, width]) for i in range(depth)]
        self.loaded = [st.sem(f"w_loaded{i}") for i in range(depth)]
        self.hi_done = st.sem("w_hi_done")
        self.lo_done = st.sem("w_lo_done")

    def load(self, eng, j):
        src, hi, lo = self.pieces[j]
        if j >= self.depth:
            eng.wait_ge(self.lo_done, j - self.depth + 1)
        eng.dma_start(self.stage[j % self.depth][:, 0:src.shape[-1]], src).then_inc(self.loaded[j % self.depth], 16)

    def load_all(self, eng):
        for j in range(len(self.pieces)):
            self.load(eng, j)

    def hi(self, act, j):
        src, hi, lo = self.pieces[j]
        act.wait_ge(self.loaded[j % self.depth], 16 * (j // self.depth + 1))
        act.activation(hi, self.stage[j % self.depth][:, 0:src.shape[-1]], ACT.Copy).then_inc(self.hi_done, 1)

    def hi_all(self, act):
        for j in range(len(self.pieces)):
            self.hi(act, j)

    def lo(self, eng, j):
        src, hi, lo = self.pieces[j]
        eng.wait_ge(self.hi_done, j + 1)
        eng.tensor_tensor(lo, self.stage[j % self.depth][:, 0:src.shape[-1]], hi.bitcast(F32),
                          ALU.subtract).then_inc(self.lo_done, 1)

    def lo_all(self, eng):
        for j in range(len(self.pieces)):
            self.lo(eng, j)

    def wait(self, pe, n=None):
        pe.wait_ge(self.lo_done, len(self.pieces) if n is None else n)


class Quantizer:
    WIDTH = GH // 2
    PIECES = D * GH // P // WIDTH

    def __init__(self, st, weights):
        self.weights = weights
        self.raw = [st.sb(f"q_raw{i}", [P, self.WIDTH]) for i in range(2)]
        self.below, self.above = st.sb("q_below", [P, self.WIDTH]), st.sb("q_above", [P, self.WIDTH])
        self.out = st.sb("q_out", [P, self.WIDTH], F32R)
        self.total, self.thr = st.sb("q_total", [P, P]), st.sb("q_thr", [P, 2])
        self.loaded = [st.sem(f"q_loaded{i}") for i in range(2)]
        self.summed, self.moved, self.thr_set = st.sem("q_summed"), st.sem("q_moved"), st.sem("q_thr_set")
        self.cut, self.made, self.stored = st.sem("q_cut"), st.sem("q_made"), st.sem("q_stored")

    def run(self, pool):
        pieces = [0, 0]
        adds = [0]

        def step(ins):
            ins.then_inc(self.summed, 1)
            adds[0] += 1
            pool.wait_ge(self.summed, adds[0])

        def magnitude(out, x):
            step(pool.tensor_scalar(self.above[:], x, 0.0, 2.0, ALU.max, ALU.mult))
            step(pool.tensor_tensor(out, self.above[:], x, ALU.subtract))

        def add(acc, x):
            step(pool.tensor_tensor(acc, acc, x, ALU.add))

        def fold(buf, n):
            while n > 1:
                add(buf[:, 0:n // 2], buf[:, n - n // 2:n])
                n -= n // 2

        def pieces_of(d):
            return d.rearrange("r n -> (r n)").rearrange("(k p n) -> k p n", p=P, n=self.WIDTH)

        def load(src, k):
            pool.dma_start(self.raw[k % 2][:], pieces_of(src)[k]).then_inc(self.loaded[k % 2], 16)
            pieces[k % 2] += 1

        for j, (w_d, q_d, sums_d) in enumerate(self.weights):
            load(w_d, 0)
            load(w_d, 1)
            for k in range(self.PIECES):
                pool.wait_ge(self.loaded[k % 2], pieces[k % 2] * 16)
                if k == 0:
                    magnitude(self.below[:], self.raw[0][:])
                else:
                    magnitude(self.raw[k % 2][:], self.raw[k % 2][:])
                    add(self.below[:], self.raw[k % 2][:])
                if k + 2 < self.PIECES:
                    load(w_d, k + 2)
            load(w_d, 0)
            load(w_d, 1)
            fold(self.below, self.WIDTH)
            pool.dma_start(sums_d.rearrange("(p a) -> p a", a=1), self.below[:, 0:1]).then_inc(self.moved, 16)
            pool.wait_ge(self.moved, 32 * j + 16)
            pool.dma_start(self.total[:], sums_d.rearrange("(a p) -> a p", a=1).to_broadcast([P, P])
                           ).then_inc(self.moved, 16)
            pool.wait_ge(self.moved, 32 * j + 32)
            fold(self.total, P)
            for i, half in enumerate((0.5, -0.5)):
                pool.tensor_scalar(self.thr[:, i:i + 1], self.total[:, 0:1], 1.0 / (D * GH), 1e-8, ALU.mult, ALU.add
                                   ).then_inc(self.thr_set, 1)
                pool.wait_ge(self.thr_set, 4 * j + 2 * i + 1)
                pool.tensor_scalar(self.thr[:, i:i + 1], self.thr[:, i:i + 1], half, None, ALU.mult
                                   ).then_inc(self.thr_set, 1)
                pool.wait_ge(self.thr_set, 4 * j + 2 * i + 2)
            for k in range(self.PIECES):
                n = j * self.PIECES + k
                pool.wait_ge(self.loaded[k % 2], pieces[k % 2] * 16)
                if n:
                    pool.wait_ge(self.made, n)
                pool.tensor_scalar(self.below[:], self.raw[k % 2][:], self.thr[:, 1:2], None, ALU.is_lt
                                   ).then_inc(self.cut, 1)
                pool.tensor_scalar(self.above[:], self.raw[k % 2][:], self.thr[:, 0:1], None, ALU.is_gt
                                   ).then_inc(self.cut, 1)
                pool.wait_ge(self.cut, 2 * n + 2)
                if n:
                    pool.wait_ge(self.stored, n * 16)
                pool.tensor_tensor(self.out[:], self.above[:], self.below[:], ALU.subtract).then_inc(self.made, 1)
                pool.wait_ge(self.made, n + 1)
                pool.dma_start(pieces_of(q_d)[k], self.out[:].bitcast(F32)).then_inc(self.stored, 16)
                if k + 2 < self.PIECES:
                    load(w_d, k + 2)
        pool.wait_ge(self.stored, len(self.weights) * self.PIECES * 16)


def three_passes(pe, out, wh, wl, xh, xl, first, last):
    pe.matmul(out, wh, xh, start=first, stop=False)
    pe.matmul(out, wh, xl, start=False, stop=False)
    return pe.matmul(out, wl, xh, start=False, stop=last)


def rsqrt_newton(dve, chain, out, tmp, root, var, eps):
    chain.link(dve.reciprocal(out, root))
    newton_step(dve, chain, out, tmp, var, eps)


def newton_step(dve, chain, out, tmp, var, eps):
    chain.link(dve.tensor_tensor(tmp, out, out, ALU.mult))
    chain.link(dve.scalar_tensor_tensor(out=tmp, in0=var, scalar=eps, in1=tmp, op0=ALU.add, op1=ALU.mult))
    chain.link(dve.tensor_scalar(tmp, tmp, -0.5, 1.5, ALU.mult, ALU.add))
    chain.link(dve.tensor_tensor(out, out, tmp, ALU.mult))


def normed_qkv_stage(nc, w_d, bqk_d, bv_d, x_d, xh_d, xl_d, qh_d, ql_d, kh_d, kl_d, v_d, alibi):
    NQK, NP = 2 * KT, 2 * KT + TT
    MEAN_AT, CENTER_AT, SQUARE_AT, VAR_AT, ROOT_AT, NORM_AT, LOW_AT = 0, 1, 1, 3, 3, 5, 8
    with Stage(nc, "qkv") as st:
        wh, wl = st.sb("wh", [P, KT, 3 * D], F32R), st.sb("wl", [P, KT, 3 * D], F32R)
        ws = WeightSplit(st, 3 * D, [(w_d[k * P:(k + 1) * P, :], wh[:, k, :], wl[:, k, :]) for k in range(KT)])
        bqk, bv = st.sb("bqk", [P, NQK]), st.sb("bv", [P, D])
        ones, eps = st.sb("ones", [P, P]), st.sb("eps", [P, 1])
        x = [st.sb(f"x{i}", [P, KT, CH]) for i in range(2)]
        xc, sq = st.sb("xc", [P, KT, CH]), st.sb("sq", [P, KT, CH])
        root, inv, tmp = st.sb("root", [P, CH]), st.sb("inv", [P, CH]), st.sb("tmp", [P, CH])
        xh = [st.sb(f"xh{i}", [P, KT, CH], F32R) for i in range(2)]
        xl = [st.sb(f"xl{i}", [P, KT, CH], F32R) for i in range(2)]
        full = st.sb("full", [P, 4, CH])
        hi, lo = st.sb("hi", [P, 4, CH], F32R), st.sb("lo", [P, 4, CH], F32R)
        vb = st.sb("vb", [P, TT, D])
        rounded = st.sb("rounded", [P, T], F32R)
        al_in, al_rounded, al_stored = st.sem("al_in"), st.sem("al_rounded"), st.sem("al_stored")
        acc = st.ps("acc", [P, 4, CH])
        mean, var = st.ps("mean", [P, 2, CH]), st.ps("var", [P, 2, CH])
        b_in, ones_set = st.sem("b_in"), st.sem("ones_set")
        x_in = [st.sem(f"x_in{i}") for i in range(2)]
        mean_ready, centered, squared = st.sem("mean_ready"), st.sem("centered"), st.sem("squared")
        var_ready, root_ready, newton = st.sem("var_ready"), st.sem("root_ready"), st.sem("newton")
        normed, xh_ready, xl_ready = st.sem("normed"), st.sem("xh_ready"), st.sem("xl_ready")
        made, taken = st.sem("made"), st.sem("taken")
        hi_ready, lo_ready = st.sem("hi_ready"), st.sem("lo_ready")
        xn_stored = [st.sem(f"xn_stored{i}") for i in range(2)]
        qk_stored = [st.sem(f"qk_stored{i}") for i in range(4)]
        v_stored = st.sem("v_stored")
        block = st.block()
        LINKS = 5

        @block.sync
        def _(sp):
            def load_x(c):
                if c >= 2:
                    sp.wait_ge(centered, c - 1)
                sp.dma_start(x[c % 2][:], tok(feat(x_d), c)).then_inc(x_in[c % 2], 16)

            load_x(0)
            sp.dma_start(bqk[:], bqk_d).then_inc(b_in, 16)
            sp.dma_start(bv[:], bv_d).then_inc(b_in, 16)
            ws.load_all(sp)
            load_x(1)
            for c in range(NCH):
                sp.wait_ge(xl_ready, c + 1)
                for dst, src in ((xh_d, xh), (xl_d, xl)):
                    sp.dma_start(tok(feat(dst), c), src[c % 2][:].bitcast(F32)).then_inc(xn_stored[c % 2], 16)
                if c + 2 < NCH:
                    load_x(c + 2)
                for m in range(NQK):
                    sp.wait_ge(lo_ready, c * NQK + m + 1)
                    f = slice(m % KT * P, (m % KT + 1) * P)
                    for dst, src in ((qh_d, hi), (ql_d, lo)) if m < KT else ((kh_d, hi), (kl_d, lo)):
                        sp.dma_start(dst[f, c * CH:(c + 1) * CH], src[:, m % 4, :].bitcast(F32)
                                     ).then_inc(qk_stored[m % 4], 16)
                sp.wait_ge(taken, (c + 1) * NP)
                sp.dma_start(v_d[c * CH:(c + 1) * CH, :].rearrange("(t p) d -> p t d", p=P), vb[:]).then_inc(v_stored, 16)
            for sem, n in [(xn_stored[i], NCH // 2 * 2) for i in range(2)] + [
                    (qk_stored[i], NCH * 2 * NQK // 4) for i in range(4)] + [(v_stored, NCH)]:
                sp.wait_ge(sem, n * 16)

        @block.tensor
        def _(pe):
            def mean_of(c):
                pe.wait_ge(x_in[c % 2], (c // 2 + 1) * 16)
                for k in range(KT):
                    last = pe.matmul(mean[:, c % 2, :], ones[:], x[c % 2][:, k, :], start=k == 0, stop=k == KT - 1)
                last.then_inc(mean_ready, 1)

            def var_of(c):
                pe.wait_ge(squared, c + 1)
                for k in range(KT):
                    last = pe.matmul(var[:, c % 2, :], ones[:], sq[:, k, :], start=k == 0, stop=k == KT - 1)
                last.then_inc(var_ready, 1)

            pe.wait_ge(ones_set, 2)
            mean_of(0)
            var_of(0)
            ws.wait(pe)
            for c in range(NCH):
                pe.wait_ge(xl_ready, c + 1)
                for m in range(NP):
                    n = c * NP + m
                    if n >= 4:
                        pe.wait_ge(taken, n - 3)
                    for k in range(KT):
                        edge = (k == 0, k == KT - 1)
                        if m < NQK:
                            s = slice(m * P, (m + 1) * P)
                            last = three_passes(pe, acc[:, m % 4, :], wh[:, k, s], wl[:, k, s],
                                                xh[c % 2][:, k, :], xl[c % 2][:, k, :], *edge)
                        else:
                            s = slice((m - NQK) * P, (m - NQK + 1) * P)
                            last = three_passes(pe, acc[:, m % 4, :], xh[c % 2][:, k, s], xl[c % 2][:, k, s],
                                                wh[:, k, 2 * D:], wl[:, k, 2 * D:], *edge)
                    last.then_inc(made, 1)
                    if c + 1 < NCH and m == MEAN_AT:
                        mean_of(c + 1)
                    if c + 1 < NCH and m == VAR_AT:
                        var_of(c + 1)

        @block.scalar
        def _(act):
            def square(c):
                act.wait_ge(centered, c + 1)
                if c:
                    act.wait_ge(var_ready, c)
                act.activation(sq[:], xc[:], ACT.Square).then_inc(squared, 1)

            def take_root(c):
                act.wait_ge(var_ready, c + 1)
                if c:
                    act.wait_ge(normed, c)
                act.activation(root[:], var[:, c % 2, :], ACT.Sqrt, bias=eps[:, 0:1]).then_inc(root_ready, 1)

            def xn_high(c):
                act.wait_ge(normed, c + 1)
                if c >= 2:
                    act.wait_ge(made, (c - 1) * NP)
                    act.wait_ge(xn_stored[c % 2], 32)
                act.activation(xh[c % 2][:], xc[:], ACT.Copy).then_inc(xh_ready, 1)

            act.wait_ge(ones_set, 2)
            square(0)
            ws.hi(act, 0)
            take_root(0)
            ws.hi(act, 1)
            xn_high(0)
            ws.hi(act, 2)
            ws.hi(act, 3)
            for c in range(NCH):
                for m in range(NQK):
                    n = c * NQK + m
                    act.wait_ge(taken, c * NP + m + 1)
                    if n >= 4:
                        act.wait_ge(qk_stored[m % 4], n // 4 * 32)
                    act.activation(hi[:, m % 4, :], full[:, m % 4, :], ACT.Copy).then_inc(hi_ready, 1)
                    if c + 1 < NCH:
                        if m == SQUARE_AT:
                            square(c + 1)
                        if m == ROOT_AT:
                            take_root(c + 1)
                if c + 1 < NCH:
                    xn_high(c + 1)

        @block.vector
        def _(dve):
            def center(c):
                dve.wait_ge(mean_ready, c + 1)
                if c:
                    dve.wait_ge(xl_ready, c)
                dve.tensor_tensor(xc[:], x[c % 2][:], mean[:, c % 2:c % 2 + 1, :].to_broadcast([P, KT, CH]),
                                  ALU.subtract).then_inc(centered, 1)

            def normalize(c):
                dve.wait_ge(root_ready, c + 1)
                chain = Chain(dve, newton, c * LINKS)
                rsqrt_newton(dve, chain, inv[:], tmp[:], root[:], var[:, c % 2, :], LN_EPS)
                assert chain.n == LINKS
                for k in range(KT):
                    last = dve.tensor_tensor(xc[:, k, :], xc[:, k, :], inv[:], ALU.mult)
                last.then_inc(normed, 1)

            def xn_low(c):
                dve.wait_ge(xh_ready, c + 1)
                dve.tensor_tensor(xl[c % 2][:], xc[:], xh[c % 2][:].bitcast(F32), ALU.subtract).then_inc(xl_ready, 1)

            def low(n):
                dve.wait_ge(hi_ready, n + 1)
                dve.tensor_tensor(lo[:, n % 4, :], full[:, n % 4, :], hi[:, n % 4, :].bitcast(F32),
                                  ALU.subtract).then_inc(lo_ready, 1)

            dve.memset(ones[:], 1.0 / D).then_inc(ones_set, 1)
            dve.memset(eps[:], LN_EPS).then_inc(ones_set, 1)
            center(0)
            normalize(0)
            xn_low(0)
            ws.lo(dve, 2)
            ws.lo(dve, 3)
            dve.wait_ge(b_in, 32)
            for c in range(NCH):
                for m in range(NP):
                    dve.wait_ge(made, c * NP + m + 1)
                    if m < NQK:
                        n = c * NQK + m
                        if n >= 4:
                            dve.wait_ge(lo_ready, n - 3)
                        dve.tensor_scalar(full[:, m % 4, :], acc[:, m % 4, :], bqk[:, m:m + 1],
                                          float(HD) ** -0.5 if m < KT else 1.0,
                                          ALU.add, ALU.mult).then_inc(taken, 1)
                        if m:
                            low(n - 1)
                    else:
                        t = m - NQK
                        if t == 0:
                            low(c * NQK + NQK - 1)
                            if c:
                                dve.wait_ge(v_stored, c * 16)
                        dve.tensor_tensor(vb[:, t, :], acc[:, m % 4, :], bv[:], ALU.add).then_inc(taken, 1)
                    if c + 1 < NCH:
                        if m == CENTER_AT:
                            center(c + 1)
                        if m == NORM_AT:
                            normalize(c + 1)
                        if m == LOW_AT:
                            xn_low(c + 1)

        @block.gpsimd
        def _(pool):
            ws.lo(pool, 0)
            ws.lo(pool, 1)
            for j, (src, dst) in enumerate(alibi):
                rows = rounded[0:src.shape[0], :]
                pool.dma_start(rows.bitcast(F32), src).then_inc(al_in, 16)
                pool.wait_ge(al_in, 16 * j + 16)
                pool.tensor_copy(rows, rows.bitcast(F32)).then_inc(al_rounded, 1)
                pool.wait_ge(al_rounded, j + 1)
                pool.dma_start(dst, rows.bitcast(F32)).then_inc(al_stored, 16)
                pool.wait_ge(al_stored, 16 * j + 16)


QROWS, SROWS, KROWS = 3 * HD, 3 * HD + 4, 3 * HD + 6
MAIN = [(c, kt) for c in range(NCH) for kt in range(TT * (c + 1))]
UNITS = [(t, g) for t in range(QT) for g in range(t // TT + 1)]
NS = len(MAIN)
FIRST_UNIT_STEP, LAST_UNIT_STEP = 12, 35
UNITS_AT = [[u for u in range(NS) if FIRST_UNIT_STEP + u * (LAST_UNIT_STEP - FIRST_UNIT_STEP) // NS == s]
            for s in range(NS)]
ROW_STEP = LAST_UNIT_STEP + 1



def main_span(c, kt):
    off = max(kt - TT * c, 0) * P
    return off, min(off, CH - 2 * P)


def unit_span(t, g):
    width = CH if g < t // TT else (t % TT + 1) * P
    return width, max(width, 2 * P)


def attention_stage(nc, cst_d, aq_d, ak_d, qh_d, ql_d, kh_d, kl_d, v_d, att_d, sum_d, ahead, ternary):
    with Stage(nc, "att") as st:
        cst = st.sb("cst", [P, 3, P])
        ident = st.sb("ident", [P, P], BF16)
        neg_q, neg_k = st.sb("neg_q", [P, P], BF16), st.sb("neg_k", [P, P], BF16)
        qs = [[st.sb(f"qs{i}{h}", [KROWS, T], F32R) for h in range(2)] for i in range(2)]
        ks = [[st.sb(f"ks{i}{h}", [KROWS, T], F32R) for h in range(2)] for i in range(2)]
        vs = [st.sb(f"vs{i}", [P, QT, 2, 2 * HD]) for i in range(2)]
        probs = st.sb("probs", [P, 4, 2, CH])
        maxes = st.sb("maxes", [P, 2, QT, NCH])
        negmax = st.sb("negmax", [P, 2, QT])
        turned = st.sb("turned", [P, P])
        split = turned[:, 0:2 * 2 * QT].rearrange("p (a h t) -> p a h t", a=2, h=2)
        rows = st.sb("rows", [2 * 2 * QT, P], F32R)
        att = st.sb("att", [P, 2, CH])
        scores = st.ps("scores", [P, 2, 2, CH])
        unit = st.ps("unit", [P, 2, CH])
        outp = st.ps("outp", [P, 2, CH])
        cst_in, cst_ready = st.sem("cst_in"), st.sem("cst_ready")
        pair_in = [st.sem(f"pair_in{i}") for i in range(2)]
        row_in = [st.sem(f"row_in{i}") for i in range(2)]
        unit_made, unit_taken = st.sem("unit_made"), st.sem("unit_taken")
        max_step, rows_made, rows_ready = st.sem("max_step"), st.sem("rows_made"), st.sem("rows_ready")
        scored, exped, summed = st.sem("scored"), st.sem("exped"), st.sem("summed")
        copied, stored = st.sem("copied"), [st.sem(f"stored{i}") for i in range(2)]
        block = st.block()
        NPAIR = NH // 2
        LOADS = 2 * (3 + 1 + 3 + 1 + 1)
        MAX_LINKS = NCH + 2
        ws = WeightSplit(st, FH, ahead, 2)
        quantizer = Quantizer(st, ternary)

        def pairs(eng, body):
            with eng.Fori(0, NPAIR // 2 - 1) as r:
                for par in range(2):
                    body(r * 2 + par, par, r, True)
            body(NPAIR - 2, 0, NPAIR // 2 - 1, True)
            body(NPAIR - 1, 1, NPAIR // 2 - 1, False)

        @block.sync
        def _(sp):
            sp.dma_start(cst[:], cst_d).then_inc(cst_in, 16)

            def load(p, par):
                for h in range(2):
                    f, sem = bass.ds(p * 2 * HD + h * HD, HD), pair_in[par]
                    q, k = qs[par][h], ks[par][h]
                    for b, (q_d, k_d) in enumerate(((qh_d, kh_d), (ql_d, kh_d), (qh_d, kl_d))):
                        s = slice(b * HD, (b + 1) * HD)
                        sp.dma_start(q[s, :].bitcast(F32), q_d[f, :]).then_inc(sem, 16)
                        sp.dma_start(k[s, :].bitcast(F32), k_d[f, :]).then_inc(sem, 16)
                    sp.dma_start(q[QROWS:SROWS, :].bitcast(F32), aq_d[bass.ds(p * 8 + h * 4, 4), :]).then_inc(sem, 16)
                    sp.dma_start(k[QROWS:KROWS, :].bitcast(F32), ak_d[bass.ds(p * 12 + h * 6, 6), :]).then_inc(sem, 16)
                    sp.dma_start(vs[par][:, :, h, 0:HD],
                                 v_d[:, f].rearrange("(t p) d -> p t d", p=P)).then_inc(sem, 16)

            def store(p, c):
                sp.wait_ge(copied, p * NCH + c + 3)
                for h in range(2):
                    o = h * 2 * HD
                    sp.dma_start(att_d[bass.ds((p * 2 + h) * HD, HD), c * CH:(c + 1) * CH], att[o:o + HD, c % 2, :]
                                 ).then_inc(stored[c % 2], 16)
                    sp.dma_start(sum_d[bass.ds(p * 2 + h, 1), c * CH:(c + 1) * CH], att[o + HD:o + HD + 1, c % 2, :]
                                 ).then_inc(stored[c % 2], 16)

            def max_rows(p, par, r):
                sp.wait_ge(rows_ready, p + 1)
                for h in range(2):
                    for part in range(2):
                        src = rows[(part * 2 + h) * QT:(part * 2 + h + 1) * QT, :]
                        dst = qs[par][h][SROWS + part:SROWS + part + 1, :].rearrange("a (t q) -> a t q", q=P)
                        sp.dma_start(dst.bitcast(F32), src.bitcast(F32)).then_inc(row_in[par], 16)

            load(0, 0)
            max_rows(0, 0, 0)
            load(1, 1)

            def body(p, par, r, more):
                for c in range(NCH - 1):
                    store(p, c)
                if more:
                    max_rows(p + 1, 1 - par, r)
                if not isinstance(p, int) or p + 2 < NPAIR:
                    sp.wait_ge(summed, (p + 1) * NS + 4)
                    load(p + 2, par)
                store(p, NCH - 1)

            pairs(sp, body)

        @block.tensor
        def _(pe):
            def unit_product(p, par, u, heads=(0, 1)):
                t, g = UNITS[u]
                width, cover = unit_span(t, g)
                for h in heads:
                    pe.wait_ge(unit_taken, (p * NS + u) * 2 + h + 1)
                    diag = g == t // TT
                    last = pe.matmul(unit[:, h, 0:cover], qs[par][h][0:SROWS, t * P:(t + 1) * P],
                                     ks[par][h][0:SROWS, g * CH:g * CH + cover], start=True, stop=not diag)
                    if diag:
                        last = pe.matmul(unit[:, h, width - P:width], ident[:], neg_q[:], start=False, stop=True)
                    last.then_inc(unit_made, 1)

            def turn(p):
                pe.wait_ge(max_step, (p + 1) * MAX_LINKS)
                pe.wait_ge(unit_taken, (p + 1) * NS * 2 + 2)
                pe.transpose(unit[:, 0, 0:P], turned[:], cst[:, 0, :]).then_inc(rows_made, 1)

            def sums(p, par, s):
                c, kt = MAIN[s]
                off, _ = main_span(c, kt)
                pe.wait_ge(exped, p * NS + s + 3)
                if kt == 0:
                    pe.wait_ge(copied, p * NCH + c + 1)
                for h in range(2):
                    last = pe.matmul(outp[h * 2 * HD:(h + 1) * 2 * HD, c % 2, off:CH], vs[par][:, kt, h, :],
                                     probs[:, s % 4, h, off:CH], start=kt == 0, stop=kt == TT * (c + 1) - 1,
                                     skip_group_check=True)
                last.then_inc(summed, 1)

            def body(p, par, r, more):
                for s, (c, kt) in enumerate(MAIN):
                    off, start = main_span(c, kt)
                    if s == 0:
                        pe.wait_ge(row_in[par], r * 64 + 64)
                    pe.wait_ge(exped, p * NS + s + 1)
                    for h in range(2):
                        diag = kt >= TT * c
                        last = pe.matmul(scores[:, s % 2, h, start:CH], ks[par][h][:, kt * P:(kt + 1) * P],
                                         qs[par][h][:, c * CH + start:(c + 1) * CH], start=True, stop=not diag)
                        if diag:
                            last = pe.matmul(scores[:, s % 2, h, off:off + P], ident[:], neg_k[:],
                                             start=False, stop=True)
                    last.then_inc(scored, 1)
                    if more:
                        if s == FIRST_UNIT_STEP:
                            pe.wait_ge(pair_in[1 - par], (r + par) * LOADS * 16 + LOADS * 16)
                        for u in UNITS_AT[s][:1]:
                            unit_product(p + 1, 1 - par, u)
                    if s > 1:
                        sums(p, par, s - 2)
                    if more:
                        for u in UNITS_AT[s][1:]:
                            unit_product(p + 1, 1 - par, u)
                        if s == ROW_STEP:
                            turn(p + 1)
                sums(p, par, NS - 2)
                sums(p, par, NS - 1)

            pe.sem_inc(summed, 4)
            pe.wait_ge(cst_ready, 6)
            pe.wait_ge(pair_in[0], LOADS * 16)
            for u in range(NS):
                unit_product(0, 0, u)
            turn(0)
            pairs(pe, body)

        @block.scalar
        def _(act):
            act.sem_inc(exped, 2)
            act.sem_inc(copied, 2)
            for i in range(2):
                act.sem_inc(stored[i], 4 * 16)
            ws.hi_all(act)

            def copy_out(p, c):
                act.wait_ge(summed, p * NS + len([1 for m in MAIN if m[0] <= c]) + 4)
                act.wait_ge(stored[c % 2], (p * (NCH // 2) + c // 2) * 4 * 16 + 4 * 16)
                act.activation(att[:, c % 2, :], outp[:, c % 2, :], ACT.Copy).then_inc(copied, 1)

            def body(p, par, r, more):
                for s, (c, kt) in enumerate(MAIN):
                    off, _ = main_span(c, kt)
                    act.wait_ge(scored, p * NS + s + 1)
                    act.wait_ge(summed, p * NS + s + 1)
                    act.activation(probs[:, s % 4, :, off:CH], scores[:, s % 2, :, off:CH], ACT.Exp).then_inc(exped, 1)
                    if kt == 2 and c > 0:
                        copy_out(p, c - 1)
                copy_out(p, NCH - 1)
            pairs(act, body)
            for i in range(2):
                act.wait_ge(stored[i], (NPAIR * NCH // 2 + 1) * 4 * 16)

        @block.vector
        def _(dve):
            def take(p, u):
                t, g = UNITS[u]
                width, _ = unit_span(t, g)
                for h in range(2):
                    dve.wait_ge(unit_made, (p * NS + u) * 2 + h + 1)
                    dve.tensor_reduce(maxes[:, h, t, g:g + 1], unit[:, h, 0:width], AX.X, ALU.max).then_inc(unit_taken, 1)

            def finish_max(p):
                dve.wait_ge(unit_taken, (p + 1) * NS * 2 + 2)
                dve.wait_ge(rows_made, p + 1)
                chain = Chain(dve, max_step, p * MAX_LINKS)
                for g in range(NCH):
                    t = slice(g * TT, (g + 1) * TT)
                    chain.link(dve.tensor_reduce(negmax[:, :, t], maxes[:, :, t, 0:g + 1], AX.X, ALU.max, negate=True))
                chain.link(dve.tensor_copy(split[:, 0].bitcast(F32R), negmax[:]))
                chain.link(dve.tensor_tensor(split[:, 1].bitcast(F32R), negmax[:], split[:, 0], ALU.subtract))
                assert chain.n == MAX_LINKS
                dve.wait_ge(rows_made, p + 2)
                dve.tensor_copy(rows[:], unit[0:2 * 2 * QT, 0, 0:P]).then_inc(rows_ready, 1)

            def body(p, par, r, more):
                for s, (c, kt) in enumerate(MAIN):
                    if more:
                        for u in UNITS_AT[s]:
                            take(p + 1, u)
                        if s == ROW_STEP - 1:
                            finish_max(p + 1)

            dve.sem_inc(unit_taken, 2)
            dve.sem_inc(rows_made, 1)
            dve.wait_ge(cst_in, 16)
            dve.tensor_copy(ident[:], cst[:, 0, :]).then_inc(cst_ready, 1)
            dve.tensor_copy(neg_q[:], cst[:, 1, :]).then_inc(cst_ready, 1)
            dve.tensor_copy(neg_k[:], cst[:, 2, :]).then_inc(cst_ready, 1)
            dve.memset(turned[:], 0.0).then_inc(cst_ready, 1)
            for i in range(2):
                dve.memset(vs[i][:, :, :, HD:], 1.0).then_inc(cst_ready, 1)
            dve.wait_ge(cst_ready, 6)
            for u in range(NS):
                take(0, u)
            finish_max(0)
            pairs(dve, body)

        @block.gpsimd
        def _(pool):
            for j in range(len(ahead)):
                ws.load(pool, j)
                if j:
                    ws.lo(pool, j - 1)
            ws.lo(pool, len(ahead) - 1)
            quantizer.run(pool)


def attention_constants():
    i, j = np.arange(P)[:, None], np.arange(P)[None, :]
    cst = np.stack([np.eye(P), np.where(j > i, NEG, 0.0), np.where(i > j, NEG, 0.0)], axis=1).astype(np.float32)
    slope = np.float32([1.0 / 2 ** (h / 2) for h in range(NH)])
    hi = (slope.view(np.uint32) & np.uint32(0xFFFFF000)).view(np.float32)
    lo = slope - hi
    pos = np.arange(T, dtype=np.float32)
    one = np.ones(T, np.float32)
    q = np.stack([np.stack([-pos, hi[h] * one, -pos, lo[h] * one]) for h in range(NH)])
    k = np.stack([np.stack([hi[h] * one, pos, lo[h] * one, pos, one, one]) for h in range(NH)])
    return cst, q.reshape(NH * 4, T), k.reshape(NH * 6, T)


class ExpertWeights:

    def __init__(self, st, wa_d, wb_d, wo_d=None):
        self.wah, self.wal = st.sb("wah", [P, KT, FH], F32R), st.sb("wal", [P, KT, FH], F32R)
        self.wbh, self.wbl = st.sb("wbh", [P, FT, D], F32R), st.sb("wbl", [P, FT, D], F32R)
        self.pieces = [(wa_d[k * P:(k + 1) * P, :], self.wah[:, k, :], self.wal[:, k, :]) for k in range(KT)]
        self.pieces += [(wb_d[f * P:(f + 1) * P, :], self.wbh[:, f, :], self.wbl[:, f, :]) for f in range(FT)]
        if wo_d is not None:
            self.woh, self.wol = st.sb("woh", [P, KT, D], F32R), st.sb("wol", [P, KT, D], F32R)
            self.pieces += [(wo_d[k * P:(k + 1) * P, :], self.woh[:, k, :], self.wol[:, k, :]) for k in range(KT)]


def expert_stage(nc, name, expert, act_fn, w, split, wg_d, bias_d, xh_d, xl_d, resid_d, out_d,
                 att_d=None, sum_d=None, inv_d=None, zh_d=None, zl_d=None):
    proj, norm = att_d is not None, zh_d is not None
    wah, wal, wbh, wbl = w.wah, w.wal, w.wbh, w.wbl
    MEAN_AT, CENTER_AT, SQUARE_AT, VAR_AT, ROOT_AT, INVERT_AT = 1, 2, 3, 3, 5, 5
    BIAS_AT, RESID_AT = 3, 4
    with Stage(nc, name) as st:
        if proj:
            woh, wol = w.woh, w.wol
            at = [st.sb(f"at{i}", [P, KT, CH]) for i in range(2)]
            ath, atl = st.sb("ath", [P, KT, CH], F32R), st.sb("atl", [P, KT, CH], F32R)
            inv = st.sb("inv", [P, KT, CH])
            sums = st.sb("sums", [P, NH * T // P])
            sum_in, inverted, inv_out = st.sem("sum_in"), st.sem("inverted"), st.sem("inv_out")
            inv_in, at_normed = st.sem("inv_in"), st.sem("at_normed")
            by_rows = [d.rearrange("h (a b) -> (h a) b", b=NH * T // P) for d in (sum_d, inv_d)]
        if split:
            ws = WeightSplit(st, FH, w.pieces)
        if norm:
            ones, eps = st.sb("ones", [P, P]), st.sb("eps", [P, 1])
            yc, sq = st.sb("yc", [P, KT, CH]), st.sb("sq", [P, KT, CH])
            zh, zl = st.sb("zh", [P, KT, CH], F32R), st.sb("zl", [P, KT, CH], F32R)
            root, rinv, tmp = st.sb("root", [P, CH]), st.sb("rinv", [P, CH]), st.sb("tmp", [P, CH])
            stat = st.ps("stat", [P, CH])
            ones_set, mean_ready, centered = st.sem("ones_set"), st.sem("mean_ready"), st.sem("centered")
            squared, var_ready, root_ready = st.sem("squared"), st.sem("var_ready"), st.sem("root_ready")
            newton, normed = st.sem("newton"), st.sem("normed")
            zh_ready, zl_ready, z_stored = st.sem("zh_ready"), st.sem("zl_ready"), st.sem("z_stored")
            LINKS = 5
        wg = st.sb("wg", [P, 2, KT])
        wd = st.sb("wd", [P, KT])
        wdw = st.sb("wdw", [P, KT, P])
        wdh, wdl = st.sb("wdh", [P, KT, P], F32R), st.sb("wdl", [P, KT, P], F32R)
        bias = st.sb("bias", [P, FT + 2 * KT])
        xh = [st.sb(f"xh{i}", [P, KT, CH], F32R) for i in range(2)]
        xl = [st.sb(f"xl{i}", [P, KT, CH], F32R) for i in range(2)]
        resid = st.sb("resid", [P, KT, CH])
        mask = st.sb("mask", [P, CH])
        hid = st.sb("hid", [P, 2, CH])
        masked = st.sb("masked", [P, 2, CH])
        hh, hl = st.sb("hh", [P, 2, CH], F32R), st.sb("hl", [P, 2, CH], F32R)
        y = st.sb("y", [P, KT, CH])
        gate, up, down = st.ps("gate", [P, CH]), st.ps("up", [P, 2, CH]), st.ps("down", [P, KT, CH])
        s_in, gate_w = st.sem("s_in"), st.sem("gate_w")
        x_in = [st.sem(f"x_in{i}") for i in range(2)]
        at_in, r_in = [st.sem(f"at_in{i}") for i in range(2)], st.sem("r_in")
        gated, masks = st.sem("gated"), st.sem("masks")
        upped, activated, hmasked = st.sem("upped"), st.sem("activated"), st.sem("hmasked")
        hi_ready, lo_ready, downed = st.sem("hi_ready"), st.sem("lo_ready"), st.sem("downed")
        at_hi, at_lo, at_used = st.sem("at_hi"), st.sem("at_lo"), st.sem("at_used")
        biased, resided, added = st.sem("biased"), st.sem("resided"), st.sem("added")
        stored, y_free = st.sem("stored"), st.sem("y_free")
        passed = st.sem("passed")
        block = st.block()
        LEAD = 2 * FT

        def chunks(eng):
            return ((c // 2, c % 2, c) for c in range(NCH)) if norm else chunk_loop(eng)

        @block.sync
        def _(sp):
            sp.dma_start(wg[:], wg_d).then_inc(s_in, 16)
            sp.dma_start(bias[:], bias_d).then_inc(s_in, 16)
            if proj:
                sp.dma_start(sums[:], by_rows[0]).then_inc(sum_in, 16)
                sp.wait_ge(inverted, 1)
                sp.dma_start(by_rows[1], sums[:]).then_inc(inv_out, 16)
            if split:
                ws.load_all(sp)
            if proj:
                sp.wait_ge(inv_out, 16)
            for r, par, c in chunks(sp):
                sp.wait_ge(downed, c * FT + FT)
                sp.dma_start(xh[par][:].bitcast(F32), tok(feat(xh_d), c)).then_inc(x_in[par], 16)
                sp.dma_start(xl[par][:].bitcast(F32), tok(feat(xl_d), c)).then_inc(x_in[par], 16)
                if proj:
                    sp.wait_ge(at_normed, c + 1)
                    for h in range(NH):
                        s = slice(h % HPG * HD, (h % HPG + 1) * HD)
                        sp.dma_start(inv[s, h // HPG, :], inv_d[h:h + 1, bass.ds(c * CH, CH)].to_broadcast([HD, CH])
                                     ).then_inc(inv_in, 16)
                    sp.wait_ge(at_lo, c + 1)
                    sp.dma_start(at[par][:], tok(feat(att_d), c)).then_inc(at_in[par], 16)
                sp.wait_ge(resided, c + 1)
                sp.dma_start(resid[:], tok(feat(resid_d), c)).then_inc(r_in, 16)

        @block.tensor
        def _(pe):
            def mean_of(c):
                pe.wait_ge(added, c + 2)
                for k in range(KT):
                    last = pe.matmul(stat[:], ones[:], y[:, k, :], start=k == 0, stop=k == KT - 1)
                last.then_inc(mean_ready, 1)

            def var_of(c):
                pe.wait_ge(squared, c + 1)
                for k in range(KT):
                    last = pe.matmul(stat[:], ones[:], sq[:, k, :], start=k == 0, stop=k == KT - 1)
                last.then_inc(var_ready, 1)

            pe.sem_inc(downed, LEAD)
            if proj:
                pe.sem_inc(at_used, 1)
            if norm:
                pe.wait_ge(ones_set, 2)
            pe.wait_ge(gate_w, 4)
            if split:
                ws.wait(pe)
            for r, par, c in chunks(pe):
                def up_product(f):
                    pe.wait_ge(activated, c * FT + f + 1)
                    for k in range(KT):
                        s = slice(f * P, (f + 1) * P)
                        last = three_passes(pe, up[:, f % 2, :], wah[:, k, s], wal[:, k, s],
                                            xh[par][:, k, :], xl[par][:, k, :], k == 0, k == KT - 1)
                    last.then_inc(upped, 1)

                def down_product(f):
                    pe.wait_ge(lo_ready, c * FT + f + 3)
                    for m in range(KT):
                        s = slice(m * P, (m + 1) * P)
                        last = three_passes(pe, down[:, m, :], wbh[:, f, s], wbl[:, f, s], hh[:, f % 2, :],
                                            hl[:, f % 2, :], f == 0 and not proj, f == FT - 1)
                    last.then_inc(downed, 1)

                pe.wait_ge(x_in[par], r * 32 + 32)
                pe.wait_ge(masks, c + 1)
                for k in range(KT):
                    last = three_passes(pe, gate[:], wdh[:, k, :], wdl[:, k, :], xh[par][:, k, :],
                                        xl[par][:, k, :], k == 0, k == KT - 1)
                last.then_inc(gated, 1)
                up_product(0)
                up_product(1)
                pe.wait_ge(added, c + 1)
                if proj:
                    pe.wait_ge(at_lo, c + 3)
                    for m in range(KT):
                        s = slice(m * P, (m + 1) * P)
                        for k in range(KT):
                            last = three_passes(pe, down[:, m, :], woh[:, k, s], wol[:, k, s],
                                                ath[:, k, :], atl[:, k, :], k == 0, False)
                    last.then_inc(at_used, 1)
                for f in range(FT):
                    down_product(f)
                    if f + 2 < FT:
                        up_product(f + 2)
                    if norm and c and f == MEAN_AT:
                        mean_of(c - 1)
                    if norm and c and f == VAR_AT:
                        var_of(c - 1)
            if norm:
                mean_of(NCH - 1)
                var_of(NCH - 1)

        @block.scalar
        def _(act):
            def square(c):
                act.wait_ge(centered, c + 1)
                act.activation(sq[:], yc[:], ACT.Square).then_inc(squared, 1)

            def take_root(c):
                act.wait_ge(var_ready, c + 1)
                act.activation(root[:], stat[:], ACT.Sqrt, bias=eps[:, 0:1]).then_inc(root_ready, 1)

            def z_high(c):
                act.wait_ge(normed, c + 1)
                if c:
                    act.wait_ge(z_stored, c * 32)
                act.activation(zh[:], yc[:], ACT.Copy).then_inc(zh_ready, 1)

            act.sem_inc(activated, 2)
            if proj:
                act.sem_inc(stored, 16)
            if split:
                ws.hi_all(act)
            if norm:
                act.wait_ge(ones_set, 2)
            for r, par, c in chunks(act):
                def high(f):
                    act.wait_ge(hmasked, c * FT + f + 3)
                    act.wait_ge(downed, c * FT + f - 1 + LEAD)
                    act.activation(hh[:, f % 2, :], masked[:, f % 2, :], ACT.Copy).then_inc(hi_ready, 1)

                if proj:
                    act.wait_ge(at_normed, c + 2)
                    act.wait_ge(at_used, c + 1)
                    act.activation(ath[:], at[par][:], ACT.Copy).then_inc(at_hi, 1)
                for f in range(FT):
                    act.wait_ge(upped, c * FT + f + 1)
                    act.wait_ge(hmasked, c * FT + f + 1)
                    act.activation(hid[:, f % 2, :], up[:, f % 2, :], act_fn,
                                   bias=bias[:, f:f + 1]).then_inc(activated, 1)
                    high(f)
                    if norm and c and f == SQUARE_AT:
                        square(c - 1)
                    if norm and c and f == ROOT_AT:
                        take_root(c - 1)
                if norm and c:
                    z_high(c - 1)
                if proj:
                    act.wait_ge(added, c + 2)
                    act.dma_start(tok(feat(out_d), c), y[:]).then_inc(stored, 16)
            if norm:
                square(NCH - 1)
                take_root(NCH - 1)
                z_high(NCH - 1)

        @block.vector
        def _(dve):
            def center(c):
                dve.wait_ge(mean_ready, c + 1)
                if c:
                    dve.wait_ge(zl_ready, c)
                dve.tensor_tensor(yc[:], y[:], stat[:].rearrange("p (a t) -> p a t", a=1).to_broadcast([P, KT, CH]),
                                  ALU.subtract).then_inc(centered, 1)

            def invert(c):
                dve.wait_ge(root_ready, c + 1)
                if c:
                    dve.wait_ge(normed, c)
                chain = Chain(dve, newton, c * LINKS)
                chain.link(dve.reciprocal(rinv[:], root[:]))
                return chain

            def refine(chain):
                newton_step(dve, chain, rinv[:], tmp[:], stat[:], LN_EPS)
                assert chain.n == LINKS

            dve.sem_inc(masks, 1)
            dve.sem_inc(hmasked, 2)
            dve.sem_inc(lo_ready, 2)
            dve.sem_inc(added, 1)
            dve.sem_inc(resided, 1)
            if norm:
                dve.memset(ones[:], 1.0 / D).then_inc(ones_set, 1)
                dve.memset(eps[:], LN_EPS).then_inc(ones_set, 1)
            if proj:
                dve.sem_inc(at_lo, 2)
                dve.wait_ge(sum_in, 16)
                dve.reciprocal(sums[:], sums[:]).then_inc(inverted, 1)
            dve.wait_ge(s_in, 32)
            dve.tensor_tensor(wd[:], wg[:, 0, :], wg[:, 1, :], ALU.subtract).then_inc(gate_w, 1)
            dve.wait_ge(gate_w, 1)
            dve.tensor_copy(wdw[:], wd[:].rearrange("p (k a) -> p k a", a=1).to_broadcast([P, KT, P])).then_inc(gate_w, 1)
            dve.wait_ge(gate_w, 2)
            dve.tensor_copy(wdh[:], wdw[:]).then_inc(gate_w, 1)
            dve.wait_ge(gate_w, 3)
            dve.tensor_tensor(wdl[:], wdw[:], wdh[:].bitcast(F32), ALU.subtract).then_inc(gate_w, 1)
            if split:
                ws.lo_all(dve)
            for r, par, c in chunks(dve):
                def low(f):
                    dve.wait_ge(hi_ready, c * FT + f + 1)
                    dve.tensor_tensor(hl[:, f % 2, :], masked[:, f % 2, :], hh[:, f % 2, :].bitcast(F32),
                                      ALU.subtract).then_inc(lo_ready, 1)

                if proj:
                    dve.wait_ge(at_hi, c + 1)
                    dve.tensor_tensor(atl[:], at[par][:], ath[:].bitcast(F32), ALU.subtract).then_inc(at_lo, 1)
                dve.wait_ge(gated, c + 1)
                dve.wait_ge(biased, c * KT + KT)
                dve.tensor_scalar(mask[:], gate[:], 0.0, None,
                                  ALU.is_ge if expert == 0 else ALU.is_lt).then_inc(masks, 1)
                dve.wait_ge(masks, c + 2)
                for f in range(FT):
                    dve.wait_ge(activated, c * FT + f + 3)
                    dve.wait_ge(lo_ready, c * FT + f + 1)
                    dve.tensor_tensor(masked[:, f % 2, :], hid[:, f % 2, :], mask[:], ALU.mult).then_inc(hmasked, 1)
                    low(f)
                    if norm and c and f == CENTER_AT:
                        center(c - 1)
                    if f == BIAS_AT:
                        if proj:
                            dve.wait_ge(stored, c * 16 + 16)
                        else:
                            dve.wait_ge(y_free, c + 1)
                        if norm and c:
                            dve.wait_ge(centered, c)
                        for m in range(KT):
                            dve.tensor_scalar(y[:, m, :], mask[:], bias[:, FT + m:FT + m + 1],
                                              bias[:, FT + KT + m:FT + KT + m + 1], ALU.mult, ALU.add).then_inc(biased, 1)
                    if f == RESID_AT:
                        dve.wait_ge(r_in, c * 16 + 16)
                        dve.wait_ge(biased, c * KT + 2 * KT)
                        dve.tensor_tensor(y[:], y[:], resid[:], ALU.add).then_inc(resided, 1)
                    if norm and c and f == INVERT_AT:
                        chain = invert(c - 1)
                    if norm and c and f == INVERT_AT + 1:
                        refine(chain)
                dve.wait_ge(resided, c + 2)
                dve.wait_ge(downed, c * FT + FT + LEAD)
                dve.tensor_tensor(y[:], y[:], down[:], ALU.add).then_inc(added, 1)
            if norm:
                center(NCH - 1)
                refine(invert(NCH - 1))

        @block.gpsimd
        def _(pool):
            def z_rest(c):
                pool.wait_ge(newton, (c + 1) * LINKS)
                pool.wait_ge(squared, c + 1)
                pool.tensor_tensor(yc[:], yc[:], rinv[:].rearrange("p (a t) -> p a t", a=1).to_broadcast([P, KT, CH]),
                                   ALU.mult).then_inc(normed, 1)
                pool.wait_ge(zh_ready, c + 1)
                pool.tensor_tensor(zl[:], yc[:], zh[:].bitcast(F32), ALU.subtract).then_inc(zl_ready, 1)
                pool.wait_ge(zl_ready, c + 1)
                pool.dma_start(tok(feat(zh_d), c), zh[:].bitcast(F32)).then_inc(z_stored, 16)
                pool.dma_start(tok(feat(zl_d), c), zl[:].bitcast(F32)).then_inc(z_stored, 16)

            pool.sem_inc(biased, KT)
            if proj:
                pool.sem_inc(at_normed, 1)
                for r, par, c in chunks(pool):
                    wait_alone(pool, at_in[par], r * 16 + 16, passed)
                    wait_alone(pool, inv_in, (c + 1) * NH * 16, passed)
                    pool.tensor_tensor(at[par][:], at[par][:], inv[:], ALU.mult).then_inc(at_normed, 1)
                pool.wait_ge(stored, NCH * 16 + 16)
                return
            pool.sem_inc(y_free, 1)
            for r, par, c in chunks(pool):
                if norm and c:
                    z_rest(c - 1)
                wait_alone(pool, added, c + 2, passed)
                pool.dma_start(tok(feat(out_d), c), y[:]).then_inc(stored, 16)
                pool.wait_ge(stored, c * 16 + 16)
                if norm and c:
                    pool.wait_ge(z_stored, c * 32)
                pool.sem_inc(y_free, 1)
            if norm:
                z_rest(NCH - 1)
                pool.wait_ge(z_stored, NCH * 32)


def glu_stage(nc, w1_d, w2_d, w3_d, xh_d, xl_d, resid_d, out_d):
    LOAD = 4
    with Stage(nc, "glu") as st:
        w1, w2 = st.sb("w1", [P, KT, GH], F32R), st.sb("w2", [P, KT, GH], F32R)
        w3 = st.sb("w3", [P, GT, D], F32R)
        xh = [st.sb(f"xh{i}", [P, KT, CH], F32R) for i in range(2)]
        xl = [st.sb(f"xl{i}", [P, KT, CH], F32R) for i in range(2)]
        resid, y = st.sb("resid", [P, KT, CH]), st.sb("y", [P, KT, CH])
        sig, hid = st.sb("sig", [P, 2, CH]), st.sb("hid", [P, 2, CH])
        hh, hl = st.sb("hh", [P, 2, CH], F32R), st.sb("hl", [P, 2, CH], F32R)
        u1, u2, down = st.ps("u1", [P, 2, CH]), st.ps("u2", [P, 2, CH]), st.ps("down", [P, KT, CH])
        loads = [range(f, min(f + LOAD, GT)) for f in range(0, GT, LOAD)]
        up_in, down_in = [st.sem(f"up_in{i}") for i in range(len(loads))], [st.sem(f"down_in{i}") for i in range(len(loads))]
        x_in, r_in = [st.sem(f"x_in{i}") for i in range(2)], st.sem("r_in")
        upped, sig_ready, hid_ready = st.sem("upped"), st.sem("sig_ready"), st.sem("hid_ready")
        hi_ready, lo_ready, downed = st.sem("hi_ready"), st.sem("lo_ready"), st.sem("downed")
        added, y_ready, stored, y_free = st.sem("added"), st.sem("y_ready"), st.sem("stored"), st.sem("y_free")
        passed = st.sem("passed")
        block = st.block()
        LEAD = 2 * GT

        def load_weights(eng, i):
            fs = slice(loads[i][0] * P, (loads[i][-1] + 1) * P)
            for w, w_d in ((w1, w1_d), (w2, w2_d)):
                eng.dma_start(w[:, :, fs].bitcast(F32), w_d[:, fs].rearrange("(k p) n -> p k n", p=P)).then_inc(up_in[i], 16)
            eng.dma_start(w3[:, loads[i][0]:loads[i][-1] + 1, :].bitcast(F32),
                          w3_d[fs, :].rearrange("(f p) n -> p f n", p=P)).then_inc(down_in[i], 16)

        @block.sync
        def _(sp):
            load_weights(sp, 0)
            for r, par, c in chunk_loop(sp):
                sp.wait_ge(downed, c * GT + GT)
                sp.dma_start(xh[par][:].bitcast(F32), tok(feat(xh_d), c)).then_inc(x_in[par], 16)
                sp.dma_start(xl[par][:].bitcast(F32), tok(feat(xl_d), c)).then_inc(x_in[par], 16)
                sp.wait_ge(y_ready, c + 1)
                sp.dma_start(resid[:], tok(feat(resid_d), c)).then_inc(r_in, 16)

        @block.tensor
        def _(pe):
            pe.sem_inc(downed, LEAD)
            for r, par, c in chunk_loop(pe):
                def up_product(f):
                    n = par * GT + f
                    s = slice(f * P, (f + 1) * P)
                    pe.wait_ge(up_in[f // LOAD], 32)
                    pe.wait_ge(hid_ready, c * GT + f + 1)
                    for w, u in ((w1, u1), (w2, u2)):
                        for k in range(KT):
                            pe.matmul(u[:, n % 2, :], w[:, k, s], xh[par][:, k, :], start=k == 0, stop=False)
                            last = pe.matmul(u[:, n % 2, :], w[:, k, s], xl[par][:, k, :], start=False, stop=k == KT - 1)
                    last.then_inc(upped, 1)

                def down_product(f):
                    n = par * GT + f
                    pe.wait_ge(down_in[f // LOAD], 16)
                    pe.wait_ge(lo_ready, c * GT + f + 3)
                    for m in range(KT):
                        w = w3[:, f, m * P:(m + 1) * P]
                        pe.matmul(down[:, m, :], w, hh[:, n % 2, :], start=f == 0, stop=False)
                        last = pe.matmul(down[:, m, :], w, hl[:, n % 2, :], start=False, stop=f == GT - 1)
                    last.then_inc(downed, 1)

                pe.wait_ge(x_in[par], r * 32 + 32)
                up_product(0)
                up_product(1)
                pe.wait_ge(added, c + 1)
                for f in range(GT):
                    down_product(f)
                    if f + 2 < GT:
                        up_product(f + 2)

        @block.scalar
        def _(act):
            for i in range(1, len(loads)):
                load_weights(act, i)
            for r, par, c in chunk_loop(act):
                def high(f):
                    n = par * GT + f
                    act.wait_ge(hid_ready, c * GT + f + 3)
                    act.wait_ge(downed, c * GT + f - 1 + LEAD)
                    act.activation(hh[:, n % 2, :], hid[:, n % 2, :], ACT.Copy).then_inc(hi_ready, 1)

                for f in range(GT):
                    n = par * GT + f
                    act.wait_ge(upped, c * GT + f + 1)
                    act.wait_ge(hid_ready, c * GT + f + 1)
                    act.activation(sig[:, n % 2, :], u1[:, n % 2, :], ACT.Sigmoid).then_inc(sig_ready, 1)
                    high(f)

        @block.vector
        def _(dve):
            dve.sem_inc(hid_ready, 2)
            dve.sem_inc(lo_ready, 2)
            dve.sem_inc(added, 1)
            dve.sem_inc(y_ready, 1)
            for r, par, c in chunk_loop(dve):
                def low(f):
                    n = par * GT + f
                    dve.wait_ge(hi_ready, c * GT + f + 1)
                    dve.tensor_tensor(hl[:, n % 2, :], hid[:, n % 2, :], hh[:, n % 2, :].bitcast(F32),
                                      ALU.subtract).then_inc(lo_ready, 1)

                for f in range(GT):
                    n = par * GT + f
                    dve.wait_ge(sig_ready, c * GT + f + 1)
                    dve.wait_ge(lo_ready, c * GT + f + 1)
                    dve.tensor_tensor(hid[:, n % 2, :], sig[:, n % 2, :], u2[:, n % 2, :], ALU.mult).then_inc(hid_ready, 1)
                    low(f)
                dve.wait_ge(y_free, c + 1)
                dve.wait_ge(r_in, c * 16 + 16)
                dve.wait_ge(downed, c * GT + GT + LEAD)
                dve.tensor_tensor(y[:], resid[:], down[:], ALU.add).then_inc(added, 1)
                dve.wait_ge(added, c + 2)
                dve.sem_inc(y_ready, 1)

        @block.gpsimd
        def _(pool):
            pool.sem_inc(y_free, 1)
            for r, par, c in chunk_loop(pool):
                wait_alone(pool, added, c + 2, passed)
                pool.dma_start(tok(feat(out_d), c), y[:]).then_inc(stored, 16)
                pool.wait_ge(stored, c * 16 + 16)
                pool.sem_inc(y_free, 1)


RING = ["act"] * (2 * KT) + ["act"] * TT + ["act"] + ["act"] * KT + ["dve"] * KT + ["dve"] + ["dve"] * KT + ["dve"] * KT
R_Q, R_K, R_V, R_GK, R_GATE = 0, KT, 2 * KT, 2 * KT + TT, 2 * KT + TT + 1
R_TURN, R_MS, R_SPREAD, R_OUT = R_GATE + KT, R_GATE + 2 * KT, R_GATE + 2 * KT + 1, R_GATE + 3 * KT + 1
NR = len(RING)
READS = {e: RING.count(e) for e in ("act", "dve")}


def reads_to(n):
    return RING[:n + 1].count(RING[n])


def lightning_stage(nc, cst_d, w_d, wg1_d, wg2_d, decay_p_d, decay_f_d, norm_w_d, xh_d, xl_d, resid_d, out_d):
    with Stage(nc, "lin") as st:
        NC = 4 * P + HD + KT * P + P + 1
        cst = st.sb("cst", [P, NC])
        at = np.cumsum([0, P, P, P, P, HD, KT * P, P, 1])
        dist, causal, cpos, diag, msel, spread, ident, kpos = (cst[:, a:b] for a, b in zip(at[:-1], at[1:]))
        names = ("q", "k", "v", "o")
        wh = {n: st.sb(f"w{n}h", [P, KT, D], F32R) for n in names}
        wl = {n: st.sb(f"w{n}l", [P, KT, D], F32R) for n in names}
        g1h, g1l = st.sb("g1h", [P, KT, P], F32R), st.sb("g1l", [P, KT, P], F32R)
        g2 = st.sb("g2", [P, D])
        pieces = [(w_d[n][k * P:(k + 1) * P, :], wh[n][:, k, :], wl[n][:, k, :]) for n in names for k in range(KT)]
        pieces += [(wg1_d[k * P:(k + 1) * P, :], g1h[:, k, 0:HD], g1l[:, k, 0:HD]) for k in range(KT)]
        ws = WeightSplit(st, D, pieces, 2)
        ld_p, ld_f, nw = st.sb("ld_p", [P, KT]), st.sb("ld_f", [P, NH]), st.sb("nw", [P, KT])
        eps = st.sb("eps", [P, 1])
        pair_decay = st.sb("pair_decay", [P, NH, P])
        q_decay = st.sb("q_decay", [P, KT, P])
        k_decay16, k_decay = st.sb("k_decay16", [P, NH]), st.sb("k_decay", [P, D])
        c_decay = st.sb("c_decay", [P, KT])
        xh, xl = st.sb("xh", [P, KT, CH], F32R), st.sb("xl", [P, KT, CH], F32R)
        qt, qd = st.sb("qt", [P, KT, CH]), st.sb("qd", [P, KT, CH])
        qblk = st.sb("qblk", [P, 2, KT, HPG, P])
        kt_, kd = st.sb("kt", [P, KT, CH]), st.sb("kd", [P, KT, TT, P])
        v = st.sb("v", [P, TT, D])
        gk, sig = st.sb("gk", [P, CH]), st.sb("sig", [P, KT, CH])
        dec = st.sb("dec", [P, 2, HPG, P])
        state, fresh = st.sb("state", [P, KT, P]), st.sb("fresh", [P, P])
        og = qt
        ogh, ogl = st.sb("ogh", [P, KT, CH], F32R), st.sb("ogl", [P, KT, CH], F32R)
        root, inv, tmp = gk, st.sb("inv", [P, CH]), st.sb("tmp", [P, CH])
        y = st.sb("y", [P, KT, CH])
        ring, pair, upd = st.ps("ring", [P, 2, CH]), st.ps("pair", [P, HPG, P]), st.ps("upd", [P, CH])
        o = st.ps("o", [P, KT, CH])
        s_in, zeroed, expd, masked = st.sem("s_in"), st.sem("zeroed"), st.sem("expd"), st.sem("masked")
        x_in, r_in = st.sem("x_in"), st.sem("r_in")
        made, taken = st.sem("made"), {e: st.sem(f"taken_{e}") for e in ("act", "dve")}
        qd_ready, qblk_ready = st.sem("qd_ready"), st.sem("qblk_ready")
        paired, decayed, o_made = st.sem("paired"), st.sem("decayed"), st.sem("o_made")
        updated, fresh_ready, state_ready = st.sem("updated"), st.sem("fresh_ready"), st.sem("state_ready")
        gated, squared, root_ready, newton = st.sem("gated"), st.sem("squared"), st.sem("root_ready"), st.sem("newton")
        normed, hi_ready, lo_ready = st.sem("normed"), st.sem("hi_ready"), st.sem("lo_ready")
        stored, y_free = st.sem("stored"), st.sem("y_free")
        passed = st.sem("passed")
        block = st.block()
        NI, LINKS = TT * KT, 5

        def wait_taken(eng, c, n):
            e = RING[n]
            eng.wait_ge(taken[e], (c + 1) * READS[e] + reads_to(n))

        @block.sync
        def _(sp):
            for dst, src in ((cst, cst_d), (ld_p, decay_p_d), (ld_f, decay_f_d), (nw, norm_w_d)):
                sp.dma_start(dst[:], src).then_inc(s_in, 16)
            ws.load_all(sp)
            sp.wait_ge(zeroed, 1)
            sp.dma_start(g2[0:HD, :], wg2_d).then_inc(s_in, 16)
            for r, par, c in chunk_loop(sp):
                sp.wait_ge(made, c * NR + R_GATE)
                sp.dma_start(xh[:].bitcast(F32), tok(feat(xh_d), c)).then_inc(x_in, 16)
                sp.dma_start(xl[:].bitcast(F32), tok(feat(xl_d), c)).then_inc(x_in, 16)
                sp.wait_ge(y_free, c + 1)
                sp.dma_start(y[:], tok(feat(resid_d), c)).then_inc(r_in, 16)

        @block.tensor
        def _(pe):
            pe.sem_inc(made, NR)
            pe.sem_inc(paired, 2 * KT)
            pe.sem_inc(o_made, 2)
            pe.sem_inc(updated, 1)
            ws.wait(pe)
            pe.wait_ge(s_in, 5 * 16)
            pe.wait_ge(zeroed, 5)
            for r, par, c in chunk_loop(pe):
                def slot(n):
                    m = n - 2
                    wait_taken(pe, *((c, m) if m >= 0 else (c - 1, m + NR)))
                    return ring[:, n % 2, :]

                def projected(n, w, m, lhs_is_x=False):
                    out, s = slot(n), slice(m * P, (m + 1) * P)
                    for k in range(KT):
                        edge = (k == 0, k == KT - 1)
                        if lhs_is_x:
                            last = three_passes(pe, out, xh[:, k, s], xl[:, k, s], wh[w][:, k, :], wl[w][:, k, :], *edge)
                        else:
                            last = three_passes(pe, out, wh[w][:, k, s], wl[w][:, k, s], xh[:, k, :], xl[:, k, :], *edge)
                    last.then_inc(made, 1)

                pe.wait_ge(x_in, c * 32 + 32)
                for m in range(KT):
                    projected(R_Q + m, "q", m)
                for m in range(KT):
                    projected(R_K + m, "k", m)
                for t in range(TT):
                    projected(R_V + t, "v", t, True)
                out = slot(R_GK)
                for k in range(KT):
                    last = three_passes(pe, out, g1h[:, k, :], g1l[:, k, :], xh[:, k, :], xl[:, k, :], k == 0, k == KT - 1)
                last.then_inc(made, 1)
                for g in range(KT):
                    out = slot(R_GATE + g)
                    if g == 0:
                        wait_taken(pe, c, R_GK)
                    pe.matmul(out, g2[:, g * P:(g + 1) * P], gk[:], start=True, stop=True).then_inc(made, 1)
                for g in range(KT):
                    out = slot(R_TURN + g)
                    wait_taken(pe, c, R_K + g)
                    for t in range(TT):
                        last = pe.transpose(out[:, t * P:(t + 1) * P], kt_[:, g, t * P:(t + 1) * P], ident)
                    last.then_inc(made, 1)

                def score(i):
                    t, g = divmod(i, KT)
                    pe.wait_ge(decayed, c * NI + i + 1)
                    pe.wait_ge(qblk_ready, c * NI + i + 2)
                    pe.matmul(pair[:].rearrange("p h c -> p (h c)"), kt_[:, g, t * P:(t + 1) * P],
                              qblk[:, t % 2, g].rearrange("p h c -> p (h c)"), start=True, stop=True).then_inc(paired, 1)

                def attend(i):
                    t, g = divmod(i, KT)
                    s = slice(t * P, (t + 1) * P)
                    pe.wait_ge(state_ready, c * NI + i + 1)
                    pe.wait_ge(decayed, c * NI + i + 2)
                    if i == 0:
                        pe.wait_ge(qd_ready, c * KT + 2 * KT)
                        pe.wait_ge(gated, c + 1)
                        wait_taken(pe, c, R_V + TT - 1)
                    pe.matmul(o[:, g, s], state[:, g, :], qd[:, g, s], start=True, stop=False, skip_group_check=True)
                    for h in range(HPG):
                        f = (g * HPG + h) * HD
                        last = pe.matmul(o[h * HD:(h + 1) * HD, g, s], v[:, t, f:f + HD], dec[:, i % 2, h, :],
                                         start=False, stop=True, skip_group_check=True)
                    last.then_inc(o_made, 1)
                    if t == 0:
                        wait_taken(pe, c, R_TURN + g)
                    pe.wait_ge(fresh_ready, c * NI + i + 1)
                    pe.matmul(upd[:, 0:P], kd[:, g, t, :], v[:, t, g * P:(g + 1) * P], start=True,
                              stop=True).then_inc(updated, 1)

                for i in range(NI):
                    score(i)
                    if i:
                        attend(i - 1)
                attend(NI - 1)
                out = slot(R_MS)
                pe.wait_ge(squared, c + 1)
                for g in range(KT):
                    last = pe.matmul(ring[g * HD:(g + 1) * HD, R_MS % 2, :], msel, sig[:, g, :], start=True, stop=True,
                                     skip_group_check=True)
                last.then_inc(made, 1)
                for g in range(KT):
                    slot(R_SPREAD + g)
                    if g == 0:
                        pe.wait_ge(newton, (c + 1) * LINKS + 1)
                    pe.matmul(ring[:, (R_SPREAD + g) % 2, :], spread[:, g * P:(g + 1) * P], inv[:], start=True,
                              stop=True).then_inc(made, 1)
                for m in range(KT):
                    out, s = slot(R_OUT + m), slice(m * P, (m + 1) * P)
                    pe.wait_ge(lo_ready, c * KT + 2 * KT)
                    for k in range(KT):
                        last = three_passes(pe, out, wh["o"][:, k, s], wl["o"][:, k, s], ogh[:, k, :], ogl[:, k, :],
                                            k == 0, k == KT - 1)
                    last.then_inc(made, 1)

        @block.scalar
        def _(act):
            act.sem_inc(taken["act"], READS["act"])
            act.wait_ge(s_in, 4 * 16)
            for h in range(NH):
                act.activation(pair_decay[:, h, :], dist, ACT.Exp, scale=ld_f[:, h:h + 1]).then_inc(expd, 1)
            for g in range(KT):
                act.activation(q_decay[:, g, :], cpos, ACT.Exp, scale=ld_p[:, g:g + 1]).then_inc(expd, 1)
            act.activation(k_decay16[:], ld_f[:], ACT.Exp, scale=kpos).then_inc(expd, 1)
            act.activation(c_decay[:], ld_p[:], ACT.Exp, scale=float(P)).then_inc(expd, 1)
            ws.hi_all(act)
            for r, par, c in chunk_loop(act):
                def arrived(n):
                    act.wait_ge(made, (c + 1) * NR + n + 1)
                    return ring[:, n % 2, :]

                act.wait_ge(qblk_ready, c * NI + 1)
                act.wait_ge(qd_ready, c * KT + KT)
                act.wait_ge(lo_ready, c * KT + KT)
                for g in range(KT):
                    act.activation(qt[:, g, :], arrived(R_Q + g), ACT.Silu).then_inc(taken["act"], 1)
                act.wait_ge(paired, c * NI + 2 * KT)
                for g in range(KT):
                    act.activation(kt_[:, g, :], arrived(R_K + g), ACT.Silu).then_inc(taken["act"], 1)
                act.wait_ge(updated, c * NI + 1)
                for t in range(TT):
                    act.activation(v[:, t, :], arrived(R_V + t), ACT.Silu).then_inc(taken["act"], 1)
                act.wait_ge(newton, c * LINKS + 1)
                act.activation(gk[:], arrived(R_GK), ACT.Copy).then_inc(taken["act"], 1)
                act.wait_ge(made, (c + 1) * NR + R_MS + 1 - NR)
                for g in range(KT):
                    act.activation(sig[:, g, :], arrived(R_GATE + g), ACT.Sigmoid).then_inc(taken["act"], 1)
                act.wait_ge(gated, c + 2)
                act.activation(sig[:], og[:], ACT.Square).then_inc(squared, 1)
                act.activation(root[:], arrived(R_MS), ACT.Sqrt, bias=eps[:, 0:1]).then_inc(root_ready, 1)
                act.wait_ge(made, (c + 1) * NR)
                for g in range(KT):
                    act.wait_ge(normed, c * KT + g + 1)
                    act.activation(ogh[:, g, :], og[:, g, :], ACT.Copy).then_inc(hi_ready, 1)

        @block.vector
        def _(dve):
            dve.sem_inc(taken["dve"], READS["dve"])
            dve.sem_inc(qd_ready, KT)
            dve.sem_inc(decayed, 1)
            dve.sem_inc(fresh_ready, 1)
            dve.sem_inc(state_ready, KT)
            dve.sem_inc(gated, 1)
            dve.sem_inc(lo_ready, KT)
            dve.sem_inc(newton, 1)
            dve.memset(g2[:], 0.0).then_inc(zeroed, 1)
            dve.memset(g1h[:].bitcast(F32), 0.0).then_inc(zeroed, 1)
            dve.memset(g1l[:].bitcast(F32), 0.0).then_inc(zeroed, 1)
            dve.memset(state[:], 0.0).then_inc(zeroed, 1)
            dve.memset(eps[:], LN_EPS).then_inc(zeroed, 1)
            dve.wait_ge(expd, NH + KT + 2)
            for g in range(KT):
                s = slice(g * HPG, (g + 1) * HPG)
                dve.tensor_tensor(pair_decay[:, s, :], pair_decay[:, s, :],
                                  causal.rearrange("p (a c) -> p a c", a=1).to_broadcast([P, HPG, P]),
                                  ALU.mult).then_inc(masked, 1)
            dve.tensor_copy(k_decay[:].rearrange("p (h d) -> p h d", d=HD),
                            k_decay16[:].rearrange("p (h a) -> p h a", a=1).to_broadcast([P, NH, HD])).then_inc(masked, 1)
            ws.lo_all(dve)
            dve.wait_ge(masked, KT + 1)
            for r, par, c in chunk_loop(dve):
                def arrived(n):
                    dve.wait_ge(made, (c + 1) * NR + n + 1)
                    return ring[:, n % 2, :]

                for g in range(KT):
                    wait_taken(dve, c, R_Q + g)
                    dve.wait_ge(o_made, c * NI + 2)
                    dve.tensor_tensor(qd[:, g, :].rearrange("p (t c) -> p t c", c=P),
                                      qt[:, g, :].rearrange("p (t c) -> p t c", c=P),
                                      q_decay[:, g:g + 1, :].to_broadcast([P, TT, P]), ALU.mult).then_inc(qd_ready, 1)
                dve.wait_ge(updated, c * NI + 1)
                for g in range(KT):
                    dve.tensor_tensor(kd[:, g, :, :], arrived(R_TURN + g).rearrange("p (t f) -> p t f", f=P),
                                      k_decay[:, g * P:(g + 1) * P].rearrange("p (a f) -> p a f", a=1).to_broadcast([P, TT, P]),
                                      ALU.mult).then_inc(taken["dve"], 1)

                def decay(i):
                    t, g = divmod(i, KT)
                    dve.wait_ge(paired, c * NI + i + 1 + 2 * KT)
                    dve.wait_ge(o_made, c * NI + i + 1)
                    dve.tensor_tensor(dec[:, i % 2], pair[:], pair_decay[:, g * HPG:(g + 1) * HPG, :],
                                      ALU.mult).then_inc(decayed, 1)

                def advance(i):
                    t, g = divmod(i, KT)
                    dve.wait_ge(updated, c * NI + i + 2)
                    dve.wait_ge(state_ready, c * NI + i + KT)
                    dve.tensor_tensor(fresh[:], upd[:, 0:P], diag, ALU.mult).then_inc(fresh_ready, 1)
                    dve.wait_ge(fresh_ready, c * NI + i + 2)
                    dve.wait_ge(o_made, c * NI + i + 3)
                    dve.scalar_tensor_tensor(out=state[:, g, :], in0=state[:, g, :], scalar=c_decay[:, g:g + 1],
                                             in1=fresh[:], op0=ALU.mult, op1=ALU.add).then_inc(state_ready, 1)

                for i in range(NI):
                    decay(i)
                    if i:
                        advance(i - 1)
                advance(NI - 1)
                wait_taken(dve, c, R_GATE + KT - 1)
                dve.wait_ge(qd_ready, (c + 1) * KT + KT)
                dve.wait_ge(qblk_ready, (c + 1) * NI + 1)
                dve.tensor_tensor(og[:], o[:], sig[:], ALU.mult).then_inc(gated, 1)
                dve.wait_ge(root_ready, c + 1)
                chain = Chain(dve, newton, c * LINKS + 1)
                rsqrt_newton(dve, chain, inv[:], tmp[:], root[:], ring[:, R_MS % 2, :], LN_EPS)
                dve.sem_inc(taken["dve"], 1)
                assert chain.n == LINKS
                for g in range(KT):
                    dve.scalar_tensor_tensor(out=og[:, g, :], in0=og[:, g, :], scalar=nw[:, g:g + 1],
                                             in1=arrived(R_SPREAD + g), op0=ALU.mult, op1=ALU.mult).then_inc(normed, 1)
                    dve.wait_ge(normed, c * KT + g + 1)
                    dve.sem_inc(taken["dve"], 1)
                for g in range(KT):
                    dve.wait_ge(hi_ready, c * KT + g + 1)
                    dve.tensor_tensor(ogl[:, g, :], og[:, g, :], ogh[:, g, :].bitcast(F32),
                                      ALU.subtract).then_inc(lo_ready, 1)
                dve.wait_ge(r_in, c * 16 + 16)
                for m in range(KT):
                    dve.tensor_tensor(y[:, m, :], y[:, m, :], arrived(R_OUT + m), ALU.add).then_inc(taken["dve"], 1)

        @block.gpsimd
        def _(pool):
            pool.sem_inc(qblk_ready, 1)
            pool.sem_inc(y_free, 1)
            pool.memset(qblk[:], 0.0).then_inc(masked, 1)
            pool.wait_ge(masked, KT + 2)
            for r, par, c in chunk_loop(pool):
                for i in range(NI):
                    t, g = divmod(i, KT)
                    if t == 0:
                        wait_taken(pool, c, R_Q + g)
                    wait_alone(pool, paired, c * NI + i + 1, passed)
                    for h in range(HPG):
                        s = slice(h * HD, (h + 1) * HD)
                        last = pool.tensor_copy(qblk[s, t % 2, g, h, :], qt[s, g, t * P:(t + 1) * P])
                    last.then_inc(qblk_ready, 1)
                wait_taken(pool, c, R_OUT + KT - 1)
                pool.dma_start(tok(feat(out_d), c), y[:]).then_inc(stored, 16)
                pool.wait_ge(stored, c * 16 + 16)
                pool.sem_inc(y_free, 1)


def lightning_constants():
    s, c = np.arange(P)[:, None], np.arange(P)[None, :]
    p = np.arange(P)[:, None]
    parts = [np.maximum(c - s, 0), c >= s, np.broadcast_to(c + 1, (P, P)), p // HD == c // HD,
             (p // HD == np.arange(HD)[None, :] % HPG) / HD]
    parts += [p == g * HD + c // HD for g in range(KT)]
    parts += [p == c, P - 1 - p]
    return np.concatenate([np.asarray(a, np.float32) for a in parts], axis=1)


def build(nc, i, out):
    def dram(name, shape):
        return nc.dram_tensor(name, shape, F32).ap()

    xh_d, xl_d = dram("xn_hi", [D, T]), dram("xn_lo", [D, T])
    qh_d, ql_d, kh_d, kl_d = (dram(n, [D, T]) for n in ("q_hi", "q_lo", "k_hi", "k_lo"))
    v_d, att_d = dram("v", [T, D]), dram("att", [D, T])
    sum_d, inv_d = dram("softmax_sums", [NH, T]), dram("softmax_inverses", [NH, T])
    ternary = [(i[n], dram(f"{n}_ternary", list(i[n].shape)), dram(f"{n}_sums", [P])) for n in ("w1", "w2", "w3")]
    y0_d, x1_d, y1_d = dram("y0", [D, T]), dram("x1", [D, T]), dram("y1", [D, T])
    zh_d, zl_d = dram("zn_hi", [D, T]), dram("zn_lo", [D, T])

    aq_d, ak_d = dram("alibi_q_rounded", [NH * 4, T]), dram("alibi_k_rounded", [NH * 6, T])
    normed_qkv_stage(nc, i["Wqkv"], i["bqk"], i["bv"], i["x"], xh_d, xl_d, qh_d, ql_d, kh_d, kl_d, v_d,
                     ((i["alibi_q"], aq_d), (i["alibi_k"], ak_d)))
    with Stage(nc, "exp0w") as st:
        w = ExpertWeights(st, i["W0a"], i["W0b"], i["L0_Wo"])
        attention_stage(nc, i["att_cst"], aq_d, ak_d, qh_d, ql_d, kh_d, kl_d, v_d, att_d, sum_d,
                        w.pieces, ternary)
        expert_stage(nc, "exp0", 0, ACT.Gelu, w, False, i["Wg"], i["bias0"], xh_d, xl_d, i["x"], y0_d,
                     att_d, sum_d, inv_d)
    with Stage(nc, "exp1w") as st:
        w = ExpertWeights(st, i["W1a"], i["W1b"])
        expert_stage(nc, "exp1", 1, ACT.Relu, w, True, i["Wg"], i["bias1"], xh_d, xl_d, y0_d, x1_d,
                     zh_d=zh_d, zl_d=zl_d)
    lightning_stage(nc, i["lin_cst"], {n: i[f"W{n}"] for n in "qkvo"}, i["Wg1"], i["Wg2"], i["decay_p"], i["decay_f"],
                    i["norm_w"], zh_d, zl_d, x1_d, y1_d)
    glu_stage(nc, *(q for _, q, _ in ternary), zh_d, zl_d, y1_d, out)


def kernel(**inputs):
    import numpy as _np
    import concourse.bacc as _bacc
    from concourse import mybir as _mybir
    from concourse.bass_utils import run_bass_kernel_spmd as _run

    a = {n: _np.asarray(v) for n, v in inputs.items()}

    def by_partition(v):
        return v.reshape(-1, P).T

    att_cst, alibi_q, alibi_k = attention_constants()
    bqkv, ld = a["L0_attn_bqkv"], a["L1_attn_log_decay"]
    none = _np.zeros(D, _np.float32)
    arrays = {
        "x": a["L0_attn_x"][0].T, "Wqkv": a["L0_attn_Wqkv"], "bqk": by_partition(bqkv[:2 * D]),
        "bv": _np.broadcast_to(bqkv[2 * D:], (P, D)), "L0_Wo": a["L0_attn_Wo"],
        "Wg": a["L0_ffn_Wg"].reshape(2, KT, P).transpose(2, 0, 1),
        "W0a": a["L0_ffn_W0a"].T, "W0b": a["L0_ffn_W0b"].T, "W1a": a["L0_ffn_W1a"].T, "W1b": a["L0_ffn_W1b"].T,
        "bias0": _np.concatenate([by_partition(a[n]) for n in ("L0_ffn_b0a", "L0_ffn_b0b", "L0_attn_bo")], 1),
        "bias1": _np.concatenate([by_partition(v) for v in (a["L0_ffn_b1a"], a["L0_ffn_b1b"], none)], 1),
        "Wq": a["L1_attn_Wq"], "Wk": a["L1_attn_Wk"], "Wv": a["L1_attn_Wv"], "Wo": a["L1_attn_Wo"],
        "Wg1": a["L1_attn_Wg1"], "Wg2": a["L1_attn_Wg2"], "norm_w": by_partition(a["L1_attn_norm_w"]),
        "decay_p": _np.repeat(ld.reshape(KT, HPG).T, HD, axis=0), "decay_f": _np.broadcast_to(ld, (P, NH)),
        "w1": a["L1_ffn_w1"].T, "w2": a["L1_ffn_w2"].T, "w3": a["L1_ffn_w3"].T,
        "att_cst": att_cst, "alibi_q": alibi_q, "alibi_k": alibi_k, "lin_cst": lightning_constants(),
    }
    nc = _bacc.Bacc("TRN2", target_bir_lowering=False, num_devices=1)
    given, aps = {}, {}
    for name, v in arrays.items():
        given[f"in_{name}"] = _np.ascontiguousarray(v)
        aps[name] = nc.dram_tensor(f"in_{name}", v.shape, _mybir.dt.from_np(v.dtype), kind="ExternalInput").ap()
    out = nc.dram_tensor("out", (D, T), F32, kind="ExternalOutput").ap()
    build(nc, aps, out)
    r = _run(nc, [given], core_ids=[0])
    return r.results[0]["out"].T.reshape(1, T, D)
```

```python
from contextlib import ExitStack

import numpy as np

import concourse.bass as bass
from concourse import mybir

F32 = mybir.dt.float32
F32R = mybir.dt.float32r
BF16 = mybir.dt.bfloat16
ALU = mybir.AluOpType
ACT = mybir.ActivationFunctionType
AX = mybir.AxisListType

P = 128
T = 2048
D = 512
KT = D // P
CH = 512
NCH = T // CH
NH = 16
HD = D // NH
HPG = P // HD
TT = CH // P
QT = T // P
FH = 1024
FT = FH // P
GH = 1408
GT = GH // P
LN_EPS = 1e-5
NEG = -1e30


class Stage:

    def __init__(self, nc, name):
        self.nc, self.name, self.stack, self.sems = nc, name, ExitStack(), []

    def __enter__(self):
        return self

    def __exit__(self, *a):
        self.stack.__exit__(*a)
        self.nc.clear_and_free_semaphores(self.sems)
        self.nc.all_engine_barrier()

    def sb(self, name, shape, dt=F32):
        return self.stack.enter_context(self.nc.sbuf_tensor(f"{self.name}_{name}", shape, dt))

    def ps(self, name, shape):
        return self.stack.enter_context(self.nc.psum_tensor(f"{self.name}_{name}", shape, F32))

    def sem(self, name):
        self.sems.append(self.nc.alloc_semaphore(f"{self.name}_{name}"))
        return self.sems[-1]

    def block(self):
        return self.stack.enter_context(self.nc.Block())


class Chain:

    def __init__(self, eng, sem, base):
        self.eng, self.sem, self.base, self.n = eng, sem, base, 0

    def link(self, ins):
        self.n += 1
        ins.then_inc(self.sem, 1)
        self.eng.wait_ge(self.sem, self.base + self.n)


def wait_alone(pool, sem, value, passed):
    pool.wait_ge(sem, value)
    pool.sem_inc(passed, 1)


def chunk_loop(eng):
    with eng.Fori(0, NCH // 2) as r:
        for par in range(2):
            yield r, par, r * 2 + par


def feat(ap):
    return ap.rearrange("(k p) t -> p k t", p=P)


def tok(ap, c):
    return ap[:, :, bass.ds(c * CH, CH)]


class WeightSplit:

    def __init__(self, st, width, pieces, depth=4, stage=None):
        if stage is None:
            stage = [st.sb(f"wstage{i}", [P, width])[:] for i in range(depth)]
        self.pieces, self.stage, self.depth = pieces, stage, len(stage)
        self.loaded = [st.sem(f"w_loaded{i}") for i in range(self.depth)]
        self.hi_done = st.sem("w_hi_done")
        self.lo_done = st.sem("w_lo_done")

    def load(self, eng, j):
        src, hi, lo = self.pieces[j]
        if j >= self.depth:
            eng.wait_ge(self.lo_done, j - self.depth + 1)
        eng.dma_start(self.stage[j % self.depth][:, 0:src.shape[-1]], src).then_inc(self.loaded[j % self.depth], 16)

    def load_all(self, eng):
        for j in range(len(self.pieces)):
            self.load(eng, j)

    def hi(self, act, j):
        src, hi, lo = self.pieces[j]
        act.wait_ge(self.loaded[j % self.depth], 16 * (j // self.depth + 1))
        act.activation(hi, self.stage[j % self.depth][:, 0:src.shape[-1]], ACT.Copy).then_inc(self.hi_done, 1)

    def hi_all(self, act):
        for j in range(len(self.pieces)):
            self.hi(act, j)

    def lo(self, eng, j):
        src, hi, lo = self.pieces[j]
        eng.wait_ge(self.hi_done, j + 1)
        eng.tensor_tensor(lo, self.stage[j % self.depth][:, 0:src.shape[-1]], hi.bitcast(F32),
                          ALU.subtract).then_inc(self.lo_done, 1)

    def lo_all(self, eng):
        for j in range(len(self.pieces)):
            self.lo(eng, j)

    def wait(self, pe, n=None):
        pe.wait_ge(self.lo_done, len(self.pieces) if n is None else n)


class Quantizer:
    WIDTH = GH // 2
    PIECES = D * GH // P // WIDTH

    def __init__(self, st, weights):
        self.weights = weights
        self.raw = [st.sb(f"q_raw{i}", [P, self.WIDTH]) for i in range(2)]
        self.below, self.above = st.sb("q_below", [P, self.WIDTH]), st.sb("q_above", [P, self.WIDTH])
        self.out = st.sb("q_out", [P, self.WIDTH], F32R)
        self.total, self.thr = st.sb("q_total", [P, P]), st.sb("q_thr", [P, 2])
        self.loaded = [st.sem(f"q_loaded{i}") for i in range(2)]
        self.summed, self.moved, self.thr_set = st.sem("q_summed"), st.sem("q_moved"), st.sem("q_thr_set")
        self.cut, self.made, self.stored = st.sem("q_cut"), st.sem("q_made"), st.sem("q_stored")

    def run(self, pool):
        pieces = [0, 0]
        adds = [0]

        def step(ins):
            ins.then_inc(self.summed, 1)
            adds[0] += 1
            pool.wait_ge(self.summed, adds[0])

        def magnitude(out, x):
            step(pool.tensor_scalar(self.above[:], x, 0.0, 2.0, ALU.max, ALU.mult))
            step(pool.tensor_tensor(out, self.above[:], x, ALU.subtract))

        def add(acc, x):
            step(pool.tensor_tensor(acc, acc, x, ALU.add))

        def fold(buf, n):
            while n > 1:
                add(buf[:, 0:n // 2], buf[:, n - n // 2:n])
                n -= n // 2

        def pieces_of(d):
            return d.rearrange("r n -> (r n)").rearrange("(k p n) -> k p n", p=P, n=self.WIDTH)

        def load(src, k):
            pool.dma_start(self.raw[k % 2][:], pieces_of(src)[k]).then_inc(self.loaded[k % 2], 16)
            pieces[k % 2] += 1

        for j, (w_d, q_d, sums_d) in enumerate(self.weights):
            load(w_d, 0)
            load(w_d, 1)
            for k in range(self.PIECES):
                pool.wait_ge(self.loaded[k % 2], pieces[k % 2] * 16)
                if k == 0:
                    magnitude(self.below[:], self.raw[0][:])
                else:
                    magnitude(self.raw[k % 2][:], self.raw[k % 2][:])
                    add(self.below[:], self.raw[k % 2][:])
                if k + 2 < self.PIECES:
                    load(w_d, k + 2)
            load(w_d, 0)
            load(w_d, 1)
            fold(self.below, self.WIDTH)
            pool.dma_start(sums_d.rearrange("(p a) -> p a", a=1), self.below[:, 0:1]).then_inc(self.moved, 16)
            pool.wait_ge(self.moved, 32 * j + 16)
            pool.dma_start(self.total[:], sums_d.rearrange("(a p) -> a p", a=1).to_broadcast([P, P])
                           ).then_inc(self.moved, 16)
            pool.wait_ge(self.moved, 32 * j + 32)
            fold(self.total, P)
            for i, half in enumerate((0.5, -0.5)):
                pool.tensor_scalar(self.thr[:, i:i + 1], self.total[:, 0:1], 1.0 / (D * GH), 1e-8, ALU.mult, ALU.add
                                   ).then_inc(self.thr_set, 1)
                pool.wait_ge(self.thr_set, 4 * j + 2 * i + 1)
                pool.tensor_scalar(self.thr[:, i:i + 1], self.thr[:, i:i + 1], half, None, ALU.mult
                                   ).then_inc(self.thr_set, 1)
                pool.wait_ge(self.thr_set, 4 * j + 2 * i + 2)
            for k in range(self.PIECES):
                n = j * self.PIECES + k
                pool.wait_ge(self.loaded[k % 2], pieces[k % 2] * 16)
                if n:
                    pool.wait_ge(self.made, n)
                pool.tensor_scalar(self.below[:], self.raw[k % 2][:], self.thr[:, 1:2], None, ALU.is_lt
                                   ).then_inc(self.cut, 1)
                pool.tensor_scalar(self.above[:], self.raw[k % 2][:], self.thr[:, 0:1], None, ALU.is_gt
                                   ).then_inc(self.cut, 1)
                pool.wait_ge(self.cut, 2 * n + 2)
                if n:
                    pool.wait_ge(self.stored, n * 16)
                pool.tensor_tensor(self.out[:], self.above[:], self.below[:], ALU.subtract).then_inc(self.made, 1)
                pool.wait_ge(self.made, n + 1)
                pool.dma_start(pieces_of(q_d)[k], self.out[:].bitcast(F32)).then_inc(self.stored, 16)
                if k + 2 < self.PIECES:
                    load(w_d, k + 2)
        pool.wait_ge(self.stored, len(self.weights) * self.PIECES * 16)


def three_passes(pe, out, wh, wl, xh, xl, first, last):
    pe.matmul(out, wh, xh, start=first, stop=False)
    pe.matmul(out, wh, xl, start=False, stop=False)
    return pe.matmul(out, wl, xh, start=False, stop=last)


def rsqrt_newton(dve, chain, out, tmp, root, var, eps):
    chain.link(dve.reciprocal(out, root))
    newton_step(dve, chain, out, tmp, var, eps)


def newton_step(dve, chain, out, tmp, var, eps):
    chain.link(dve.tensor_tensor(tmp, out, out, ALU.mult))
    chain.link(dve.scalar_tensor_tensor(out=tmp, in0=var, scalar=eps, in1=tmp, op0=ALU.add, op1=ALU.mult))
    chain.link(dve.tensor_scalar(tmp, tmp, -0.5, 1.5, ALU.mult, ALU.add))
    chain.link(dve.tensor_tensor(out, out, tmp, ALU.mult))


def fold_tiles(pool, fold, tiles, folded, n):
    pool.tensor_tensor(fold[:], tiles[:, 0:2, :], tiles[:, 2:4, :], ALU.add).then_inc(folded, 1)
    pool.wait_ge(folded, 2 * n + 1)
    pool.tensor_tensor(fold[:, 0, :], fold[:, 0, :], fold[:, 1, :], ALU.add).then_inc(folded, 1)


def normed_qkv_stage(nc, w_d, bqk_d, bv_d, x_d, xh_d, xl_d, qh_d, ql_d, kh_d, kl_d, v_d, alibi):
    NQK, NP = 2 * KT, 2 * KT + TT
    MEAN_AT, CENTER_AT, SQUARE_AT, VAR_AT, ROOT_AT, NORM_AT, LOW_AT = 0, 1, 1, 5, 5, 6, 9
    with Stage(nc, "qkv") as st:
        wh, wl = st.sb("wh", [P, KT, 3 * D], F32R), st.sb("wl", [P, KT, 3 * D], F32R)
        ws = WeightSplit(st, 3 * D, [(w_d[k * P:(k + 1) * P, :], wh[:, k, :], wl[:, k, :]) for k in range(KT)])
        bqk, bv = st.sb("bqk", [P, NQK]), st.sb("bv", [P, D])
        ones, eps = st.sb("ones", [P, P]), st.sb("eps", [P, 1])
        x = [st.sb(f"x{i}", [P, KT, CH]) for i in range(2)]
        xc, sq = st.sb("xc", [P, KT, CH]), st.sb("sq", [P, KT, CH])
        fold, folded = st.sb("fold", [P, 2, CH]), st.sem("folded")
        root, inv, tmp = st.sb("root", [P, CH]), st.sb("inv", [P, CH]), st.sb("tmp", [P, CH])
        xh = [st.sb(f"xh{i}", [P, KT, CH], F32R) for i in range(2)]
        xl = [st.sb(f"xl{i}", [P, KT, CH], F32R) for i in range(2)]
        full = st.sb("full", [P, 4, CH])
        hi, lo = st.sb("hi", [P, 4, CH], F32R), st.sb("lo", [P, 4, CH], F32R)
        vb = st.sb("vb", [P, TT, D])
        rounded = st.sb("rounded", [P, T], F32R)
        al_in, al_rounded, al_stored = st.sem("al_in"), st.sem("al_rounded"), st.sem("al_stored")
        acc = st.ps("acc", [P, 4, CH])
        mean, var = st.ps("mean", [P, 2, CH]), st.ps("var", [P, 2, CH])
        b_in, ones_set = st.sem("b_in"), st.sem("ones_set")
        x_in = [st.sem(f"x_in{i}") for i in range(2)]
        mean_ready, centered, squared = st.sem("mean_ready"), st.sem("centered"), st.sem("squared")
        var_ready, root_ready, newton = st.sem("var_ready"), st.sem("root_ready"), st.sem("newton")
        normed, xh_ready, xl_ready = st.sem("normed"), st.sem("xh_ready"), st.sem("xl_ready")
        made, taken = st.sem("made"), st.sem("taken")
        hi_ready, lo_ready = st.sem("hi_ready"), st.sem("lo_ready")
        xn_stored = [st.sem(f"xn_stored{i}") for i in range(2)]
        qk_stored = [st.sem(f"qk_stored{i}") for i in range(4)]
        v_stored = st.sem("v_stored")
        block = st.block()
        LINKS = 5

        @block.sync
        def _(sp):
            def load_x(c):
                if c >= 2:
                    sp.wait_ge(centered, c - 1)
                sp.dma_start(x[c % 2][:], tok(feat(x_d), c)).then_inc(x_in[c % 2], 16)

            load_x(0)
            sp.dma_start(bqk[:], bqk_d).then_inc(b_in, 16)
            sp.dma_start(bv[:], bv_d).then_inc(b_in, 16)
            ws.load_all(sp)
            load_x(1)
            for c in range(NCH):
                sp.wait_ge(xl_ready, c + 1)
                for dst, src in ((xh_d, xh), (xl_d, xl)):
                    sp.dma_start(tok(feat(dst), c), src[c % 2][:].bitcast(F32)).then_inc(xn_stored[c % 2], 16)
                if c + 2 < NCH:
                    load_x(c + 2)
                for m in range(NQK):
                    sp.wait_ge(lo_ready, c * NQK + m + 1)
                    f = slice(m % KT * P, (m % KT + 1) * P)
                    for dst, src in ((qh_d, hi), (ql_d, lo)) if m < KT else ((kh_d, hi), (kl_d, lo)):
                        sp.dma_start(dst[f, c * CH:(c + 1) * CH], src[:, m % 4, :].bitcast(F32)
                                     ).then_inc(qk_stored[m % 4], 16)
                sp.wait_ge(taken, (c + 1) * NP)
                sp.dma_start(v_d[c * CH:(c + 1) * CH, :].rearrange("(t p) d -> p t d", p=P), vb[:]).then_inc(v_stored, 16)
            for sem, n in [(xn_stored[i], NCH // 2 * 2) for i in range(2)] + [
                    (qk_stored[i], NCH * 2 * NQK // 4) for i in range(4)] + [(v_stored, NCH)]:
                sp.wait_ge(sem, n * 16)

        @block.tensor
        def _(pe):
            def mean_of(c):
                pe.wait_ge(folded, 4 * c + 2)
                pe.matmul(mean[:, c % 2, :], ones[:], fold[:, 0, :], start=True, stop=True).then_inc(mean_ready, 1)

            def var_of(c):
                pe.wait_ge(folded, 4 * c + 4)
                pe.matmul(var[:, c % 2, :], ones[:], fold[:, 0, :], start=True, stop=True).then_inc(var_ready, 1)

            pe.wait_ge(ones_set, 2)
            mean_of(0)
            var_of(0)
            ws.wait(pe)
            for c in range(NCH):
                pe.wait_ge(xl_ready, c + 1)
                for m in range(NP):
                    n = c * NP + m
                    if n >= 4:
                        pe.wait_ge(taken, n - 3)
                    for k in range(KT):
                        edge = (k == 0, k == KT - 1)
                        if m < NQK:
                            s = slice(m * P, (m + 1) * P)
                            last = three_passes(pe, acc[:, m % 4, :], wh[:, k, s], wl[:, k, s],
                                                xh[c % 2][:, k, :], xl[c % 2][:, k, :], *edge)
                        else:
                            s = slice((m - NQK) * P, (m - NQK + 1) * P)
                            last = three_passes(pe, acc[:, m % 4, :], xh[c % 2][:, k, s], xl[c % 2][:, k, s],
                                                wh[:, k, 2 * D:], wl[:, k, 2 * D:], *edge)
                    last.then_inc(made, 1)
                    if c + 1 < NCH and m == MEAN_AT:
                        mean_of(c + 1)
                    if c + 1 < NCH and m == VAR_AT:
                        var_of(c + 1)

        @block.scalar
        def _(act):
            def square(c):
                act.wait_ge(centered, c + 1)
                if c:
                    act.wait_ge(var_ready, c)
                act.activation(sq[:], xc[:], ACT.Square).then_inc(squared, 1)

            def take_root(c):
                act.wait_ge(var_ready, c + 1)
                if c:
                    act.wait_ge(normed, c)
                act.activation(root[:], var[:, c % 2, :], ACT.Sqrt, bias=eps[:, 0:1]).then_inc(root_ready, 1)

            def xn_high(c):
                act.wait_ge(normed, c + 1)
                if c >= 2:
                    act.wait_ge(made, (c - 1) * NP)
                    act.wait_ge(xn_stored[c % 2], 32)
                act.activation(xh[c % 2][:], xc[:], ACT.Copy).then_inc(xh_ready, 1)

            act.wait_ge(ones_set, 2)
            square(0)
            ws.hi(act, 0)
            take_root(0)
            ws.hi(act, 1)
            xn_high(0)
            ws.hi(act, 2)
            ws.hi(act, 3)
            for c in range(NCH):
                for m in range(NQK):
                    n = c * NQK + m
                    act.wait_ge(taken, c * NP + m + 1)
                    if n >= 4:
                        act.wait_ge(qk_stored[m % 4], n // 4 * 32)
                    act.activation(hi[:, m % 4, :], full[:, m % 4, :], ACT.Copy).then_inc(hi_ready, 1)
                    if c + 1 < NCH:
                        if m == SQUARE_AT:
                            square(c + 1)
                        if m == ROOT_AT:
                            take_root(c + 1)
                if c + 1 < NCH:
                    xn_high(c + 1)

        @block.vector
        def _(dve):
            def center(c):
                dve.wait_ge(mean_ready, c + 1)
                if c:
                    dve.wait_ge(xl_ready, c)
                dve.tensor_tensor(xc[:], x[c % 2][:], mean[:, c % 2:c % 2 + 1, :].to_broadcast([P, KT, CH]),
                                  ALU.subtract).then_inc(centered, 1)

            def normalize(c):
                dve.wait_ge(root_ready, c + 1)
                chain = Chain(dve, newton, c * LINKS)
                rsqrt_newton(dve, chain, inv[:], tmp[:], root[:], var[:, c % 2, :], LN_EPS)
                assert chain.n == LINKS
                for k in range(KT):
                    last = dve.tensor_tensor(xc[:, k, :], xc[:, k, :], inv[:], ALU.mult)
                last.then_inc(normed, 1)

            def xn_low(c):
                dve.wait_ge(xh_ready, c + 1)
                dve.tensor_tensor(xl[c % 2][:], xc[:], xh[c % 2][:].bitcast(F32), ALU.subtract).then_inc(xl_ready, 1)

            def low(n):
                dve.wait_ge(hi_ready, n + 1)
                dve.tensor_tensor(lo[:, n % 4, :], full[:, n % 4, :], hi[:, n % 4, :].bitcast(F32),
                                  ALU.subtract).then_inc(lo_ready, 1)

            dve.memset(ones[:], 1.0 / D).then_inc(ones_set, 1)
            dve.memset(eps[:], LN_EPS).then_inc(ones_set, 1)
            center(0)
            normalize(0)
            xn_low(0)
            ws.lo(dve, 2)
            ws.lo(dve, 3)
            dve.wait_ge(b_in, 32)
            for c in range(NCH):
                for m in range(NP):
                    dve.wait_ge(made, c * NP + m + 1)
                    if m < NQK:
                        n = c * NQK + m
                        if n >= 4:
                            dve.wait_ge(lo_ready, n - 3)
                        dve.tensor_scalar(full[:, m % 4, :], acc[:, m % 4, :], bqk[:, m:m + 1],
                                          float(HD) ** -0.5 if m < KT else 1.0,
                                          ALU.add, ALU.mult).then_inc(taken, 1)
                        if m:
                            low(n - 1)
                    else:
                        t = m - NQK
                        if t == 0:
                            low(c * NQK + NQK - 1)
                            if c:
                                dve.wait_ge(v_stored, c * 16)
                        dve.tensor_tensor(vb[:, t, :], acc[:, m % 4, :], bv[:], ALU.add).then_inc(taken, 1)
                    if c + 1 < NCH:
                        if m == CENTER_AT:
                            center(c + 1)
                        if m == NORM_AT:
                            normalize(c + 1)
                        if m == LOW_AT:
                            xn_low(c + 1)

        @block.gpsimd
        def _(pool):
            def fold_x(c):
                pool.wait_ge(x_in[c % 2], (c // 2 + 1) * 16)
                if c:
                    pool.wait_ge(var_ready, c)
                fold_tiles(pool, fold, x[c % 2], folded, 2 * c)

            def fold_squares(c):
                pool.wait_ge(squared, c + 1)
                pool.wait_ge(mean_ready, c + 1)
                fold_tiles(pool, fold, sq, folded, 2 * c + 1)

            fold_x(0)
            fold_squares(0)
            ws.lo(pool, 0)
            ws.lo(pool, 1)
            for c in range(1, NCH):
                fold_x(c)
                fold_squares(c)
                for j, (src, dst) in list(enumerate(alibi))[c - 1:c]:
                    rows = rounded[0:src.shape[0], :]
                    pool.dma_start(rows.bitcast(F32), src).then_inc(al_in, 16)
                    pool.wait_ge(al_in, 16 * j + 16)
                    pool.tensor_copy(rows, rows.bitcast(F32)).then_inc(al_rounded, 1)
                    pool.wait_ge(al_rounded, j + 1)
                    pool.dma_start(dst, rows.bitcast(F32)).then_inc(al_stored, 16)
                    pool.wait_ge(al_stored, 16 * j + 16)


QROWS, SROWS, KROWS = 3 * HD, 3 * HD + 4, 3 * HD + 6
MAIN = [(c, kt) for c in range(NCH) for kt in range(TT * (c + 1))]
UNITS = [(t, g) for t in range(QT) for g in range(t // TT + 1)]
NS = len(MAIN)
FIRST_UNIT_STEP, LAST_UNIT_STEP = 9, 34
UNITS_AT = [[u for u in range(NS) if FIRST_UNIT_STEP + u * (LAST_UNIT_STEP - FIRST_UNIT_STEP) // NS == s]
            for s in range(NS)]
ROW_STEP = LAST_UNIT_STEP + 1



def main_span(c, kt):
    off = max(kt - TT * c, 0) * P
    return off, min(off, CH - 2 * P)


def unit_span(t, g):
    width = CH if g < t // TT else (t % TT + 1) * P
    return width, max(width, 2 * P)


def attention_stage(nc, cst_d, aq_d, ak_d, qh_d, ql_d, kh_d, kl_d, v_d, att_d, sum_d, ahead, ternary):
    with Stage(nc, "att") as st:
        cst = st.sb("cst", [P, 3, P])
        ident = st.sb("ident", [P, P], BF16)
        neg_q, neg_k = st.sb("neg_q", [P, P], BF16), st.sb("neg_k", [P, P], BF16)
        qs = [[st.sb(f"qs{i}{h}", [KROWS, T], F32R) for h in range(2)] for i in range(2)]
        ks = [[st.sb(f"ks{i}{h}", [KROWS, T], F32R) for h in range(2)] for i in range(2)]
        vs = [st.sb(f"vs{i}", [P, QT, 2, 2 * HD]) for i in range(2)]
        probs = st.sb("probs", [P, 4, 2, CH])
        maxes = st.sb("maxes", [P, 2, QT, NCH])
        negmax = st.sb("negmax", [P, 2, QT])
        turned = st.sb("turned", [P, P])
        split = turned[:, 0:2 * 2 * QT].rearrange("p (a h t) -> p a h t", a=2, h=2)
        rows = st.sb("rows", [2 * 2 * QT, P], F32R)
        att = st.sb("att", [P, 2, CH])
        scores = st.ps("scores", [P, 2, 2, CH])
        unit = st.ps("unit", [P, 2, CH])
        outp = st.ps("outp", [P, 2, CH])
        cst_in, cst_ready = st.sem("cst_in"), st.sem("cst_ready")
        pair_in = [st.sem(f"pair_in{i}") for i in range(2)]
        v_in, row_in = ([st.sem(f"{n}{i}") for i in range(2)] for n in ("v_in", "row_in"))
        unit_made, unit_taken = st.sem("unit_made"), st.sem("unit_taken")
        max_step, rows_made, rows_ready = st.sem("max_step"), st.sem("rows_made"), st.sem("rows_ready")
        scored, exped, summed = st.sem("scored"), st.sem("exped"), st.sem("summed")
        copied, stored = st.sem("copied"), [st.sem(f"stored{i}") for i in range(2)]
        block = st.block()
        NPAIR = NH // 2
        LOADS = 2 * (2 * (3 + 1) + 3 + 1)
        MAX_LINKS = NCH + 2
        ws = WeightSplit(st, FH, ahead, 2)
        quantizer = Quantizer(st, ternary)

        def pairs(eng, body):
            with eng.Fori(0, NPAIR // 2 - 1) as r:
                for par in range(2):
                    body(r * 2 + par, par, r, True)
            body(NPAIR - 2, 0, NPAIR // 2 - 1, True)
            body(NPAIR - 1, 1, NPAIR // 2 - 1, False)

        @block.sync
        def _(sp):
            sp.dma_start(cst[:], cst_d).then_inc(cst_in, 16)

            def load_queries(p, par, t):
                for h in range(2):
                    f, sem, q = bass.ds(p * 2 * HD + h * HD, HD), pair_in[par], qs[par][h]
                    for b, q_d in enumerate((qh_d, ql_d, qh_d)):
                        sp.dma_start(q[b * HD:(b + 1) * HD, t].bitcast(F32), q_d[f, t]).then_inc(sem, 16)
                    sp.dma_start(q[QROWS:SROWS, t].bitcast(F32), aq_d[bass.ds(p * 8 + h * 4, 4), t]).then_inc(sem, 16)

            def load_keys(p, par):
                for h in range(2):
                    f, sem, k = bass.ds(p * 2 * HD + h * HD, HD), pair_in[par], ks[par][h]
                    for b, k_d in enumerate((kh_d, kh_d, kl_d)):
                        sp.dma_start(k[b * HD:(b + 1) * HD, :].bitcast(F32), k_d[f, :]).then_inc(sem, 16)
                    sp.dma_start(k[QROWS:KROWS, :].bitcast(F32), ak_d[bass.ds(p * 12 + h * 6, 6), :]).then_inc(sem, 16)
                for h in range(2):
                    sp.dma_start(vs[par][:, :, h, 0:HD], v_d[:, bass.ds(p * 2 * HD + h * HD, HD)].rearrange(
                        "(t p) d -> p t d", p=P)).then_inc(v_in[par], 16)

            early, late = slice(0, T - CH), slice(T - CH, T)

            def load(p, par):
                load_queries(p, par, early)
                load_queries(p, par, late)
                load_keys(p, par)

            def store(p, c):
                sp.wait_ge(copied, p * NCH + c + 3)
                for h in range(2):
                    o = h * 2 * HD
                    sp.dma_start(att_d[bass.ds((p * 2 + h) * HD, HD), c * CH:(c + 1) * CH], att[o:o + HD, c % 2, :]
                                 ).then_inc(stored[c % 2], 16)
                    sp.dma_start(sum_d[bass.ds(p * 2 + h, 1), c * CH:(c + 1) * CH], att[o + HD:o + HD + 1, c % 2, :]
                                 ).then_inc(stored[c % 2], 16)

            def max_rows(p, par, r):
                sp.wait_ge(rows_ready, p + 1)
                for h in range(2):
                    for part in range(2):
                        src = rows[(part * 2 + h) * QT:(part * 2 + h + 1) * QT, :]
                        dst = qs[par][h][SROWS + part:SROWS + part + 1, :].rearrange("a (t q) -> a t q", q=P)
                        sp.dma_start(dst.bitcast(F32), src.bitcast(F32)).then_inc(row_in[par], 16)

            load(0, 0)
            max_rows(0, 0, 0)
            load(1, 1)

            def body(p, par, r, more):
                again = not isinstance(p, int) or p + 2 < NPAIR
                for c in range(NCH - 2):
                    store(p, c)
                if again:
                    sp.wait_ge(scored, p * NS + NS - QT)
                    load_queries(p + 2, par, early)
                store(p, NCH - 2)
                if more:
                    max_rows(p + 1, 1 - par, r)
                if again:
                    sp.wait_ge(summed, (p + 1) * NS + 4)
                    load_queries(p + 2, par, late)
                    load_keys(p + 2, par)
                store(p, NCH - 1)

            pairs(sp, body)

        @block.tensor
        def _(pe):
            def unit_product(p, par, u, heads=(0, 1)):
                t, g = UNITS[u]
                width, cover = unit_span(t, g)
                for h in heads:
                    pe.wait_ge(unit_taken, (p * NS + u) * 2 + h + 1)
                    diag = g == t // TT
                    last = pe.matmul(unit[:, h, 0:cover], qs[par][h][0:SROWS, t * P:(t + 1) * P],
                                     ks[par][h][0:SROWS, g * CH:g * CH + cover], start=True, stop=not diag)
                    if diag:
                        last = pe.matmul(unit[:, h, width - P:width], ident[:], neg_q[:], start=False, stop=True)
                    last.then_inc(unit_made, 1)

            def turn(p):
                pe.wait_ge(max_step, (p + 1) * MAX_LINKS)
                pe.wait_ge(unit_taken, (p + 1) * NS * 2 + 2)
                pe.transpose(unit[:, 0, 0:P], turned[:], cst[:, 0, :]).then_inc(rows_made, 1)

            def sums(p, par, s):
                c, kt = MAIN[s]
                off, _ = main_span(c, kt)
                pe.wait_ge(exped, p * NS + s + 3)
                if kt == 0:
                    pe.wait_ge(copied, p * NCH + c + 1)
                for h in range(2):
                    last = pe.matmul(outp[h * 2 * HD:(h + 1) * 2 * HD, c % 2, off:CH], vs[par][:, kt, h, :],
                                     probs[:, s % 4, h, off:CH], start=kt == 0, stop=kt == TT * (c + 1) - 1,
                                     skip_group_check=True)
                last.then_inc(summed, 1)

            def body(p, par, r, more):
                for s, (c, kt) in enumerate(MAIN):
                    off, start = main_span(c, kt)
                    if s == 0:
                        pe.wait_ge(row_in[par], r * 64 + 64)
                        pe.wait_ge(v_in[par], r * 32 + 32)
                    pe.wait_ge(exped, p * NS + s + 1)
                    for h in range(2):
                        diag = kt >= TT * c
                        last = pe.matmul(scores[:, s % 2, h, start:CH], ks[par][h][:, kt * P:(kt + 1) * P],
                                         qs[par][h][:, c * CH + start:(c + 1) * CH], start=True, stop=not diag)
                        if diag:
                            last = pe.matmul(scores[:, s % 2, h, off:off + P], ident[:], neg_k[:],
                                             start=False, stop=True)
                    last.then_inc(scored, 1)
                    if more:
                        if s == FIRST_UNIT_STEP:
                            pe.wait_ge(pair_in[1 - par], (r + par) * LOADS * 16 + LOADS * 16)
                        for u in UNITS_AT[s][:1]:
                            unit_product(p + 1, 1 - par, u)
                    if s > 1:
                        sums(p, par, s - 2)
                    if more:
                        for u in UNITS_AT[s][1:]:
                            unit_product(p + 1, 1 - par, u)
                        if s == ROW_STEP:
                            turn(p + 1)
                sums(p, par, NS - 2)
                sums(p, par, NS - 1)

            pe.sem_inc(summed, 4)
            pe.wait_ge(cst_ready, 6)
            pe.wait_ge(pair_in[0], LOADS * 16)
            for u in range(NS):
                unit_product(0, 0, u)
            turn(0)
            pairs(pe, body)

        @block.scalar
        def _(act):
            act.sem_inc(exped, 2)
            act.sem_inc(copied, 2)
            for i in range(2):
                act.sem_inc(stored[i], 4 * 16)
            ws.hi_all(act)

            def copy_out(p, c):
                act.wait_ge(summed, p * NS + len([1 for m in MAIN if m[0] <= c]) + 4)
                act.wait_ge(stored[c % 2], (p * (NCH // 2) + c // 2) * 4 * 16 + 4 * 16)
                act.activation(att[:, c % 2, :], outp[:, c % 2, :], ACT.Copy).then_inc(copied, 1)

            def body(p, par, r, more):
                for s, (c, kt) in enumerate(MAIN):
                    off, _ = main_span(c, kt)
                    act.wait_ge(scored, p * NS + s + 1)
                    act.wait_ge(summed, p * NS + s + 1)
                    act.activation(probs[:, s % 4, :, off:CH], scores[:, s % 2, :, off:CH], ACT.Exp).then_inc(exped, 1)
                    if kt == 2 and c > 0:
                        copy_out(p, c - 1)
                copy_out(p, NCH - 1)
            pairs(act, body)
            for i in range(2):
                act.wait_ge(stored[i], (NPAIR * NCH // 2 + 1) * 4 * 16)

        @block.vector
        def _(dve):
            def take(p, u):
                t, g = UNITS[u]
                width, _ = unit_span(t, g)
                for h in range(2):
                    dve.wait_ge(unit_made, (p * NS + u) * 2 + h + 1)
                    dve.tensor_reduce(maxes[:, h, t, g:g + 1], unit[:, h, 0:width], AX.X, ALU.max).then_inc(unit_taken, 1)

            def finish_max(p):
                dve.wait_ge(unit_taken, (p + 1) * NS * 2 + 2)
                dve.wait_ge(rows_made, p + 1)
                chain = Chain(dve, max_step, p * MAX_LINKS)
                for g in range(NCH):
                    t = slice(g * TT, (g + 1) * TT)
                    chain.link(dve.tensor_reduce(negmax[:, :, t], maxes[:, :, t, 0:g + 1], AX.X, ALU.max, negate=True))
                chain.link(dve.tensor_copy(split[:, 0].bitcast(F32R), negmax[:]))
                chain.link(dve.tensor_tensor(split[:, 1].bitcast(F32R), negmax[:], split[:, 0], ALU.subtract))
                assert chain.n == MAX_LINKS
                dve.wait_ge(rows_made, p + 2)
                dve.tensor_copy(rows[:], unit[0:2 * 2 * QT, 0, 0:P]).then_inc(rows_ready, 1)

            def body(p, par, r, more):
                for s, (c, kt) in enumerate(MAIN):
                    if more:
                        for u in UNITS_AT[s]:
                            take(p + 1, u)
                        if s == ROW_STEP - 1:
                            finish_max(p + 1)

            dve.sem_inc(unit_taken, 2)
            dve.sem_inc(rows_made, 1)
            dve.wait_ge(cst_in, 16)
            dve.tensor_copy(ident[:], cst[:, 0, :]).then_inc(cst_ready, 1)
            dve.tensor_copy(neg_q[:], cst[:, 1, :]).then_inc(cst_ready, 1)
            dve.tensor_copy(neg_k[:], cst[:, 2, :]).then_inc(cst_ready, 1)
            dve.memset(turned[:], 0.0).then_inc(cst_ready, 1)
            for i in range(2):
                dve.memset(vs[i][:, :, :, HD:], 1.0).then_inc(cst_ready, 1)
            dve.wait_ge(cst_ready, 6)
            for u in range(NS):
                take(0, u)
            finish_max(0)
            pairs(dve, body)

        @block.gpsimd
        def _(pool):
            for j in range(len(ahead)):
                ws.load(pool, j)
                if j:
                    ws.lo(pool, j - 1)
            ws.lo(pool, len(ahead) - 1)
            quantizer.run(pool)


def attention_constants():
    i, j = np.arange(P)[:, None], np.arange(P)[None, :]
    cst = np.stack([np.eye(P), np.where(j > i, NEG, 0.0), np.where(i > j, NEG, 0.0)], axis=1).astype(np.float32)
    slope = np.float32([1.0 / 2 ** (h / 2) for h in range(NH)])
    hi = (slope.view(np.uint32) & np.uint32(0xFFFFF000)).view(np.float32)
    lo = slope - hi
    pos = np.arange(T, dtype=np.float32)
    one = np.ones(T, np.float32)
    q = np.stack([np.stack([-pos, hi[h] * one, -pos, lo[h] * one]) for h in range(NH)])
    k = np.stack([np.stack([hi[h] * one, pos, lo[h] * one, pos, one, one]) for h in range(NH)])
    return cst, q.reshape(NH * 4, T), k.reshape(NH * 6, T)


class ExpertWeights:

    def __init__(self, st, wa_d, wb_d, wo_d=None):
        self.wah, self.wal = st.sb("wah", [P, KT, FH], F32R), st.sb("wal", [P, KT, FH], F32R)
        self.wbh, self.wbl = st.sb("wbh", [P, FT, D], F32R), st.sb("wbl", [P, FT, D], F32R)
        self.pieces = [(wa_d[k * P:(k + 1) * P, :], self.wah[:, k, :], self.wal[:, k, :]) for k in range(KT)]
        self.pieces += [(wb_d[f * P:(f + 1) * P, :], self.wbh[:, f, :], self.wbl[:, f, :]) for f in range(FT)]
        if wo_d is not None:
            self.woh, self.wol = st.sb("woh", [P, KT, D], F32R), st.sb("wol", [P, KT, D], F32R)
            self.pieces += [(wo_d[k * P:(k + 1) * P, :], self.woh[:, k, :], self.wol[:, k, :]) for k in range(KT)]


def expert_stage(nc, name, expert, act_fn, w, split, wg_d, bias_d, xh_d, xl_d, resid_d, out_d,
                 att_d=None, sum_d=None, inv_d=None, zh_d=None, zl_d=None):
    proj, norm = att_d is not None, zh_d is not None
    wah, wal, wbh, wbl = w.wah, w.wal, w.wbh, w.wbl
    MEAN_AT, CENTER_AT, SQUARE_AT, VAR_AT, ROOT_AT, INVERT_AT = 1, 2, 3, 3, 5, 5
    BIAS_AT, RESID_AT, SPLIT_AT = 3, 4, 6
    with Stage(nc, name) as st:
        if proj:
            woh, wol = w.woh, w.wol
            at = [st.sb(f"at{i}", [P, KT, CH]) for i in range(2)]
            ath, atl = st.sb("ath", [P, KT, CH], F32R), st.sb("atl", [P, KT, CH], F32R)
            inv = st.sb("inv", [P, KT, CH])
            sums = st.sb("sums", [P, NH * T // P])
            sum_in, inverted, inv_out = st.sem("sum_in"), st.sem("inverted"), st.sem("inv_out")
            inv_in, at_normed = st.sem("inv_in"), st.sem("at_normed")
            by_rows = [d.rearrange("h (a b) -> (h a) b", b=NH * T // P) for d in (sum_d, inv_d)]
        if split:
            ws = WeightSplit(st, FH, w.pieces)
        if norm:
            ones, eps = st.sb("ones", [P, P]), st.sb("eps", [P, 1])
            yc, sq = st.sb("yc", [P, KT, CH]), st.sb("sq", [P, KT, CH])
            zh, zl = st.sb("zh", [P, KT, CH], F32R), st.sb("zl", [P, KT, CH], F32R)
            root, rinv, tmp = st.sb("root", [P, CH]), st.sb("rinv", [P, CH]), st.sb("tmp", [P, CH])
            fold, folded = st.sb("fold", [P, 2, CH]), st.sem("folded")
            stat = st.ps("stat", [P, CH])
            ones_set, mean_ready, centered = st.sem("ones_set"), st.sem("mean_ready"), st.sem("centered")
            squared, var_ready, root_ready = st.sem("squared"), st.sem("var_ready"), st.sem("root_ready")
            newton, normed = st.sem("newton"), st.sem("normed")
            zh_ready, zl_ready, z_stored = st.sem("zh_ready"), st.sem("zl_ready"), st.sem("z_stored")
            LINKS = 5
        wg = st.sb("wg", [P, 2, KT])
        wd = st.sb("wd", [P, KT])
        wdw = st.sb("wdw", [P, KT, P])
        wdh, wdl = st.sb("wdh", [P, KT, P], F32R), st.sb("wdl", [P, KT, P], F32R)
        bias = st.sb("bias", [P, FT + 2 * KT])
        xh = [st.sb(f"xh{i}", [P, KT, CH], F32R) for i in range(2)]
        xl = [st.sb(f"xl{i}", [P, KT, CH], F32R) for i in range(2)]
        resid = st.sb("resid", [P, KT, CH])
        mask = st.sb("mask", [P, CH])
        hid = st.sb("hid", [P, 2, CH])
        masked = st.sb("masked", [P, 2, CH])
        hh, hl = st.sb("hh", [P, 2, CH], F32R), st.sb("hl", [P, 2, CH], F32R)
        y = st.sb("y", [P, KT, CH])
        gate, up, down = st.ps("gate", [P, CH]), st.ps("up", [P, 2, CH]), st.ps("down", [P, KT, CH])
        s_in, gate_w = st.sem("s_in"), st.sem("gate_w")
        x_in = [st.sem(f"x_in{i}") for i in range(2)]
        at_in, r_in = [st.sem(f"at_in{i}") for i in range(2)], st.sem("r_in")
        gated, masks = st.sem("gated"), st.sem("masks")
        upped, activated, hmasked = st.sem("upped"), st.sem("activated"), st.sem("hmasked")
        hi_ready, lo_ready, downed = st.sem("hi_ready"), st.sem("lo_ready"), st.sem("downed")
        at_hi, at_lo, at_used = st.sem("at_hi"), st.sem("at_lo"), st.sem("at_used")
        biased, resided, added = st.sem("biased"), st.sem("resided"), st.sem("added")
        stored, y_free = st.sem("stored"), st.sem("y_free")
        passed = st.sem("passed")
        block = st.block()
        LEAD = 2 * FT

        def scale(eng, c):
            eng.wait_ge(newton, (c + 1) * LINKS)
            eng.wait_ge(squared, c + 1)
            eng.tensor_tensor(yc[:], yc[:], rinv[:].rearrange("p (a t) -> p a t", a=1).to_broadcast([P, KT, CH]),
                              ALU.mult).then_inc(normed, 1)

        def z_low(eng, c):
            eng.wait_ge(zh_ready, c + 1)
            eng.tensor_tensor(zl[:], yc[:], zh[:].bitcast(F32), ALU.subtract).then_inc(zl_ready, 1)

        def chunks(eng):
            return ((c // 2, c % 2, c) for c in range(NCH)) if norm else chunk_loop(eng)

        @block.sync
        def _(sp):
            if proj:
                sp.dma_start(sums[:], by_rows[0]).then_inc(sum_in, 16)
            sp.dma_start(wg[:], wg_d).then_inc(s_in, 16)
            sp.dma_start(bias[:], bias_d).then_inc(s_in, 16)
            if split:
                for j in range(KT):
                    ws.load(sp, j)
            for r, par, c in chunks(sp):
                sp.wait_ge(downed, c * FT + FT)
                sp.dma_start(xh[par][:].bitcast(F32), tok(feat(xh_d), c)).then_inc(x_in[par], 16)
                sp.dma_start(xl[par][:].bitcast(F32), tok(feat(xl_d), c)).then_inc(x_in[par], 16)
                if split and c == 0:
                    for j in range(KT, len(w.pieces)):
                        ws.load(sp, j)
                if proj:
                    sp.wait_ge(at_lo, c + 1)
                    sp.dma_start(at[par][:], tok(feat(att_d), c)).then_inc(at_in[par], 16)
                    sp.wait_ge(inv_out, 16)
                    sp.wait_ge(at_normed, c + 1)
                    for h in range(NH):
                        s = slice(h % HPG * HD, (h % HPG + 1) * HD)
                        sp.dma_start(inv[s, h // HPG, :], inv_d[h:h + 1, bass.ds(c * CH, CH)].to_broadcast([HD, CH])
                                     ).then_inc(inv_in, 16)
                sp.wait_ge(resided, c + 1)
                sp.dma_start(resid[:], tok(feat(resid_d), c)).then_inc(r_in, 16)

        @block.tensor
        def _(pe):
            def mean_of(c):
                pe.wait_ge(folded, 4 * c + 2)
                pe.matmul(stat[:], ones[:], fold[:, 0, :], start=True, stop=True).then_inc(mean_ready, 1)

            def var_of(c):
                pe.wait_ge(folded, 4 * c + 4)
                pe.matmul(stat[:], ones[:], fold[:, 0, :], start=True, stop=True).then_inc(var_ready, 1)

            pe.sem_inc(downed, LEAD)
            if proj:
                pe.sem_inc(at_used, 1)
            if norm:
                pe.wait_ge(ones_set, 2)
            pe.wait_ge(gate_w, 4)
            if split:
                ws.wait(pe, KT)
            for r, par, c in chunks(pe):
                def up_product(f):
                    pe.wait_ge(activated, c * FT + f + 1)
                    for k in range(KT):
                        s = slice(f * P, (f + 1) * P)
                        last = three_passes(pe, up[:, f % 2, :], wah[:, k, s], wal[:, k, s],
                                            xh[par][:, k, :], xl[par][:, k, :], k == 0, k == KT - 1)
                    last.then_inc(upped, 1)

                def down_product(f):
                    if split:
                        ws.wait(pe, KT + f + 1)
                    pe.wait_ge(lo_ready, c * FT + f + 3)
                    for m in range(KT):
                        s = slice(m * P, (m + 1) * P)
                        last = three_passes(pe, down[:, m, :], wbh[:, f, s], wbl[:, f, s], hh[:, f % 2, :],
                                            hl[:, f % 2, :], f == 0, f == FT - 1 and not proj)
                    last.then_inc(downed, 1)

                pe.wait_ge(x_in[par], r * 32 + 32)
                pe.wait_ge(masks, c + 1)
                for k in range(KT):
                    last = three_passes(pe, gate[:], wdh[:, k, :], wdl[:, k, :], xh[par][:, k, :],
                                        xl[par][:, k, :], k == 0, k == KT - 1)
                last.then_inc(gated, 1)
                up_product(0)
                up_product(1)
                pe.wait_ge(added, c + 1)
                for f in range(FT):
                    down_product(f)
                    if f + 2 < FT:
                        up_product(f + 2)
                    if norm and c and f == MEAN_AT:
                        mean_of(c - 1)
                    if norm and c and f == VAR_AT:
                        var_of(c - 1)
                if proj:
                    pe.wait_ge(at_lo, c + 3)
                    for m in range(KT):
                        s = slice(m * P, (m + 1) * P)
                        for k in range(KT):
                            last = three_passes(pe, down[:, m, :], woh[:, k, s], wol[:, k, s],
                                                ath[:, k, :], atl[:, k, :], False, k == KT - 1)
                    last.then_inc(at_used, 1)
            if norm:
                mean_of(NCH - 1)
                var_of(NCH - 1)

        @block.scalar
        def _(act):
            def square(c):
                act.wait_ge(centered, c + 1)
                act.activation(sq[:], yc[:], ACT.Square).then_inc(squared, 1)

            def take_root(c):
                act.wait_ge(var_ready, c + 1)
                act.activation(root[:], stat[:], ACT.Sqrt, bias=eps[:, 0:1]).then_inc(root_ready, 1)

            def z_high(c):
                act.wait_ge(normed, c + 1)
                if c:
                    act.wait_ge(z_stored, c * 32)
                act.activation(zh[:], yc[:], ACT.Copy).then_inc(zh_ready, 1)

            act.sem_inc(activated, 2)
            if proj:
                act.sem_inc(stored, 16)
                act.wait_ge(inverted, 1)
                act.dma_start(by_rows[1], sums[:]).then_inc(inv_out, 16)
            if split:
                for j in range(KT):
                    ws.hi(act, j)
            if norm:
                act.wait_ge(ones_set, 2)
            for r, par, c in chunks(act):
                def high(f):
                    act.wait_ge(hmasked, c * FT + f + 3)
                    act.wait_ge(downed, c * FT + f - 1 + LEAD)
                    act.activation(hh[:, f % 2, :], masked[:, f % 2, :], ACT.Copy).then_inc(hi_ready, 1)

                for f in range(FT):
                    if split and c == 0:
                        ws.hi(act, KT + f)
                    act.wait_ge(upped, c * FT + f + 1)
                    act.wait_ge(hmasked, c * FT + f + 1)
                    act.activation(hid[:, f % 2, :], up[:, f % 2, :], act_fn,
                                   bias=bias[:, f:f + 1]).then_inc(activated, 1)
                    high(f)
                    if proj and f == SPLIT_AT:
                        act.wait_ge(at_normed, c + 2)
                        act.wait_ge(at_used, c + 1)
                        act.activation(ath[:], at[par][:], ACT.Copy).then_inc(at_hi, 1)
                    if norm and c and f == SQUARE_AT:
                        square(c - 1)
                    if norm and c and f == ROOT_AT:
                        take_root(c - 1)
                if norm and c:
                    z_high(c - 1)
                if proj:
                    act.wait_ge(added, c + 2)
                    act.dma_start(tok(feat(out_d), c), y[:]).then_inc(stored, 16)
            if norm:
                square(NCH - 1)
                take_root(NCH - 1)
                z_high(NCH - 1)

        @block.vector
        def _(dve):
            def center(c):
                dve.wait_ge(mean_ready, c + 1)
                if c:
                    dve.wait_ge(zl_ready, c)
                dve.tensor_tensor(yc[:], y[:], stat[:].rearrange("p (a t) -> p a t", a=1).to_broadcast([P, KT, CH]),
                                  ALU.subtract).then_inc(centered, 1)

            def invert(c):
                dve.wait_ge(root_ready, c + 1)
                if c:
                    dve.wait_ge(normed, c)
                chain = Chain(dve, newton, c * LINKS)
                chain.link(dve.reciprocal(rinv[:], root[:]))
                return chain

            def refine(chain):
                newton_step(dve, chain, rinv[:], tmp[:], stat[:], LN_EPS)
                assert chain.n == LINKS

            dve.sem_inc(masks, 1)
            dve.sem_inc(hmasked, 2)
            dve.sem_inc(lo_ready, 2)
            dve.sem_inc(added, 1)
            dve.sem_inc(resided, 1)
            if norm:
                dve.memset(ones[:], 1.0 / D).then_inc(ones_set, 1)
                dve.memset(eps[:], LN_EPS).then_inc(ones_set, 1)
            if proj:
                dve.sem_inc(at_lo, 2)
                dve.wait_ge(sum_in, 16)
                dve.reciprocal(sums[:], sums[:]).then_inc(inverted, 1)
            dve.wait_ge(s_in, 32)
            dve.tensor_tensor(wd[:], wg[:, 0, :], wg[:, 1, :], ALU.subtract).then_inc(gate_w, 1)
            dve.wait_ge(gate_w, 1)
            dve.tensor_copy(wdw[:], wd[:].rearrange("p (k a) -> p k a", a=1).to_broadcast([P, KT, P])).then_inc(gate_w, 1)
            dve.wait_ge(gate_w, 2)
            dve.tensor_copy(wdh[:], wdw[:]).then_inc(gate_w, 1)
            dve.wait_ge(gate_w, 3)
            dve.tensor_tensor(wdl[:], wdw[:], wdh[:].bitcast(F32), ALU.subtract).then_inc(gate_w, 1)
            for r, par, c in chunks(dve):
                def low(f):
                    dve.wait_ge(hi_ready, c * FT + f + 1)
                    dve.tensor_tensor(hl[:, f % 2, :], masked[:, f % 2, :], hh[:, f % 2, :].bitcast(F32),
                                      ALU.subtract).then_inc(lo_ready, 1)

                dve.wait_ge(gated, c + 1)
                dve.wait_ge(biased, c * KT + KT)
                dve.tensor_scalar(mask[:], gate[:], 0.0, None,
                                  ALU.is_ge if expert == 0 else ALU.is_lt).then_inc(masks, 1)
                dve.wait_ge(masks, c + 2)
                for f in range(FT):
                    dve.wait_ge(activated, c * FT + f + 3)
                    dve.wait_ge(lo_ready, c * FT + f + 1)
                    dve.tensor_tensor(masked[:, f % 2, :], hid[:, f % 2, :], mask[:], ALU.mult).then_inc(hmasked, 1)
                    low(f)
                    if proj and f == SPLIT_AT:
                        dve.wait_ge(at_hi, c + 1)
                        dve.tensor_tensor(atl[:], at[par][:], ath[:].bitcast(F32), ALU.subtract).then_inc(at_lo, 1)
                    if norm and c and f == CENTER_AT:
                        center(c - 1)
                    if f == BIAS_AT:
                        if proj:
                            dve.wait_ge(stored, c * 16 + 16)
                        else:
                            dve.wait_ge(y_free, c + 1)
                        if norm and c:
                            dve.wait_ge(centered, c)
                        for m in range(KT):
                            dve.tensor_scalar(y[:, m, :], mask[:], bias[:, FT + m:FT + m + 1],
                                              bias[:, FT + KT + m:FT + KT + m + 1], ALU.mult, ALU.add).then_inc(biased, 1)
                    if f == RESID_AT:
                        dve.wait_ge(r_in, c * 16 + 16)
                        dve.wait_ge(biased, c * KT + 2 * KT)
                        dve.tensor_tensor(y[:], y[:], resid[:], ALU.add).then_inc(resided, 1)
                    if norm and c and f == INVERT_AT:
                        chain = invert(c - 1)
                    if norm and c and f == INVERT_AT + 1:
                        refine(chain)
                dve.wait_ge(resided, c + 2)
                dve.wait_ge(downed, c * FT + FT + LEAD)
                if proj:
                    dve.wait_ge(at_used, c + 2)
                dve.tensor_tensor(y[:], y[:], down[:], ALU.add).then_inc(added, 1)
            if norm:
                center(NCH - 1)
                refine(invert(NCH - 1))
                scale(dve, NCH - 1)
                dve.wait_ge(z_stored, (NCH - 1) * 32)
                z_low(dve, NCH - 1)

        @block.gpsimd
        def _(pool):
            def fold_y(c):
                if c:
                    pool.wait_ge(var_ready, c)
                fold_tiles(pool, fold, y, folded, 2 * c)

            def fold_squares(c):
                pool.wait_ge(squared, c + 1)
                pool.wait_ge(mean_ready, c + 1)
                fold_tiles(pool, fold, sq, folded, 2 * c + 1)

            def z_rest(c):
                scale(pool, c)
                z_low(pool, c)
                z_store(c)

            def z_store(c):
                pool.wait_ge(zl_ready, c + 1)
                pool.dma_start(tok(feat(zh_d), c), zh[:].bitcast(F32)).then_inc(z_stored, 16)
                pool.dma_start(tok(feat(zl_d), c), zl[:].bitcast(F32)).then_inc(z_stored, 16)

            pool.sem_inc(biased, KT)
            if proj:
                pool.sem_inc(at_normed, 1)
                for r, par, c in chunks(pool):
                    wait_alone(pool, at_in[par], r * 16 + 16, passed)
                    wait_alone(pool, inv_in, (c + 1) * NH * 16, passed)
                    pool.tensor_tensor(at[par][:], at[par][:], inv[:], ALU.mult).then_inc(at_normed, 1)
                pool.wait_ge(stored, NCH * 16 + 16)
                return
            pool.sem_inc(y_free, 1)
            if split:
                ws.lo_all(pool)
            for r, par, c in chunks(pool):
                if norm and c:
                    fold_squares(c - 1)
                    z_rest(c - 1)
                wait_alone(pool, added, c + 2, passed)
                if norm:
                    fold_y(c)
                pool.dma_start(tok(feat(out_d), c), y[:]).then_inc(stored, 16)
                pool.wait_ge(stored, c * 16 + 16)
                if norm and c:
                    pool.wait_ge(z_stored, c * 32)
                pool.sem_inc(y_free, 1)
            if norm:
                fold_squares(NCH - 1)
                z_store(NCH - 1)
                pool.wait_ge(z_stored, NCH * 32)


def glu_stage(nc, w1_d, w2_d, w3_d, xh_d, xl_d, resid_d, out_d):
    LOAD = 3
    with Stage(nc, "glu") as st:
        w1, w2 = st.sb("w1", [P, KT, GH], F32R), st.sb("w2", [P, KT, GH], F32R)
        w3 = st.sb("w3", [P, GT, D], F32R)
        xh = [st.sb(f"xh{i}", [P, KT, CH], F32R) for i in range(2)]
        xl = [st.sb(f"xl{i}", [P, KT, CH], F32R) for i in range(2)]
        resid, y = st.sb("resid", [P, KT, CH]), st.sb("y", [P, KT, CH])
        sig, hid = st.sb("sig", [P, 2, CH]), st.sb("hid", [P, 2, CH])
        hh, hl = st.sb("hh", [P, 2, CH], F32R), st.sb("hl", [P, 2, CH], F32R)
        u1, u2, down = st.ps("u1", [P, 2, CH]), st.ps("u2", [P, 2, CH]), st.ps("down", [P, KT, CH])
        edges = [0, 2] + list(range(2 + LOAD, GT, LOAD)) + [GT]
        loads = [range(a, b) for a, b in zip(edges[:-1], edges[1:])]
        load_of = {f: i for i, fs in enumerate(loads) for f in fs}
        up_in, down_in = [st.sem(f"up_in{i}") for i in range(len(loads))], [st.sem(f"down_in{i}") for i in range(len(loads))]
        x_in, r_in = [st.sem(f"x_in{i}") for i in range(2)], st.sem("r_in")
        upped, sig_ready, hid_ready = st.sem("upped"), st.sem("sig_ready"), st.sem("hid_ready")
        hi_ready, lo_ready, downed = st.sem("hi_ready"), st.sem("lo_ready"), st.sem("downed")
        added, y_ready, stored, y_free = st.sem("added"), st.sem("y_ready"), st.sem("stored"), st.sem("y_free")
        passed = st.sem("passed")
        block = st.block()
        LEAD = 2 * GT

        def load_weights(eng, i):
            fs = slice(loads[i][0] * P, (loads[i][-1] + 1) * P)
            for w, w_d in ((w1, w1_d), (w2, w2_d)):
                eng.dma_start(w[:, :, fs].bitcast(F32), w_d[:, fs].rearrange("(k p) n -> p k n", p=P)).then_inc(up_in[i], 16)
            eng.dma_start(w3[:, loads[i][0]:loads[i][-1] + 1, :].bitcast(F32),
                          w3_d[fs, :].rearrange("(f p) n -> p f n", p=P)).then_inc(down_in[i], 16)

        @block.sync
        def _(sp):
            load_weights(sp, 0)
            for r, par, c in chunk_loop(sp):
                sp.wait_ge(downed, c * GT + GT)
                sp.dma_start(xh[par][:].bitcast(F32), tok(feat(xh_d), c)).then_inc(x_in[par], 16)
                sp.dma_start(xl[par][:].bitcast(F32), tok(feat(xl_d), c)).then_inc(x_in[par], 16)
                sp.wait_ge(y_ready, c + 1)
                sp.dma_start(resid[:], tok(feat(resid_d), c)).then_inc(r_in, 16)

        @block.tensor
        def _(pe):
            pe.sem_inc(downed, LEAD)
            for r, par, c in chunk_loop(pe):
                def up_product(f):
                    n = par * GT + f
                    s = slice(f * P, (f + 1) * P)
                    pe.wait_ge(up_in[load_of[f]], 32)
                    pe.wait_ge(hid_ready, c * GT + f + 1)
                    for w, u in ((w1, u1), (w2, u2)):
                        for k in range(KT):
                            pe.matmul(u[:, n % 2, :], w[:, k, s], xh[par][:, k, :], start=k == 0, stop=False)
                            last = pe.matmul(u[:, n % 2, :], w[:, k, s], xl[par][:, k, :], start=False, stop=k == KT - 1)
                    last.then_inc(upped, 1)

                def down_product(f):
                    n = par * GT + f
                    pe.wait_ge(down_in[load_of[f]], 16)
                    pe.wait_ge(lo_ready, c * GT + f + 3)
                    for m in range(KT):
                        w = w3[:, f, m * P:(m + 1) * P]
                        pe.matmul(down[:, m, :], w, hh[:, n % 2, :], start=f == 0, stop=False)
                        last = pe.matmul(down[:, m, :], w, hl[:, n % 2, :], start=False, stop=f == GT - 1)
                    last.then_inc(downed, 1)

                pe.wait_ge(x_in[par], r * 32 + 32)
                up_product(0)
                up_product(1)
                pe.wait_ge(added, c + 1)
                for f in range(GT):
                    down_product(f)
                    if f + 2 < GT:
                        up_product(f + 2)

        @block.scalar
        def _(act):
            act.wait_ge(x_in[0], 32)
            for i in range(1, len(loads)):
                load_weights(act, i)
            for r, par, c in chunk_loop(act):
                def high(f):
                    n = par * GT + f
                    act.wait_ge(hid_ready, c * GT + f + 3)
                    act.wait_ge(downed, c * GT + f - 1 + LEAD)
                    act.activation(hh[:, n % 2, :], hid[:, n % 2, :], ACT.Copy).then_inc(hi_ready, 1)

                for f in range(GT):
                    n = par * GT + f
                    act.wait_ge(upped, c * GT + f + 1)
                    act.wait_ge(hid_ready, c * GT + f + 1)
                    act.activation(sig[:, n % 2, :], u1[:, n % 2, :], ACT.Sigmoid).then_inc(sig_ready, 1)
                    high(f)

        @block.vector
        def _(dve):
            dve.sem_inc(hid_ready, 2)
            dve.sem_inc(lo_ready, 2)
            dve.sem_inc(added, 1)
            dve.sem_inc(y_ready, 1)
            for r, par, c in chunk_loop(dve):
                def low(f):
                    n = par * GT + f
                    dve.wait_ge(hi_ready, c * GT + f + 1)
                    dve.tensor_tensor(hl[:, n % 2, :], hid[:, n % 2, :], hh[:, n % 2, :].bitcast(F32),
                                      ALU.subtract).then_inc(lo_ready, 1)

                for f in range(GT):
                    n = par * GT + f
                    dve.wait_ge(sig_ready, c * GT + f + 1)
                    dve.wait_ge(lo_ready, c * GT + f + 1)
                    dve.tensor_tensor(hid[:, n % 2, :], sig[:, n % 2, :], u2[:, n % 2, :], ALU.mult).then_inc(hid_ready, 1)
                    low(f)
                dve.wait_ge(y_free, c + 1)
                dve.wait_ge(r_in, c * 16 + 16)
                dve.wait_ge(downed, c * GT + GT + LEAD)
                dve.tensor_tensor(y[:], resid[:], down[:], ALU.add).then_inc(added, 1)
                dve.wait_ge(added, c + 2)
                dve.sem_inc(y_ready, 1)

        @block.gpsimd
        def _(pool):
            pool.sem_inc(y_free, 1)
            for r, par, c in chunk_loop(pool):
                wait_alone(pool, added, c + 2, passed)
                pool.dma_start(tok(feat(out_d), c), y[:]).then_inc(stored, 16)
                pool.wait_ge(stored, c * 16 + 16)
                pool.sem_inc(y_free, 1)


NI = TT * KT
BANKS = 3


class Ring:
    READER = {"q": "act", "k": "act", "v": "act", "gk": "act", "gate": "act",
              "turn": "dve", "score": "dve", "spread": "dve", "out": "dve"}

    def __init__(self):
        order = []
        for c in range(NCH + 1):
            for kind, count, late in (("q", KT, 0), ("k", KT, 0), ("spread", KT, 1), ("v", TT, 0), ("out", KT, 1),
                                      ("gk", 1, 0), ("gate", KT, 0), ("turn", KT, 0), ("score", NI, 0)):
                if 0 <= c - late < NCH:
                    order += [(kind, c - late, n) for n in range(count)]
        self.order = order
        self.at = {product: i for i, product in enumerate(order)}

    def made(self, kind, c, n=0):
        return self.at[kind, c, n] + 1

    def taken(self, kind, c, n=0):
        e = self.READER[kind]
        return e, sum(self.READER[p[0]] == e for p in self.order[:self.at[kind, c, n] + 1])

    def freed(self, kind, c, n=0):
        i = self.at[kind, c, n] - BANKS
        return self.order[i] if i >= 0 else None


def lightning_stage(nc, cst_d, w_d, wg1_d, wg2_d, decay_p_d, decay_f_d, norm_w_d, xh_d, xl_d, resid_d, out_d):
    with Stage(nc, "lin") as st:
        NC = 4 * P + HD + KT * P + P + 1
        cst = st.sb("cst", [P, NC])
        at = np.cumsum([0, P, P, P, P, HD, KT * P, P, 1])
        dist, causal, cpos, diag, msel, spread, ident, kpos = (cst[:, a:b] for a, b in zip(at[:-1], at[1:]))
        names = ("q", "k", "v", "o")
        wh = {n: st.sb(f"w{n}h", [P, KT, D], F32R) for n in names}
        wl = {n: st.sb(f"w{n}l", [P, KT, D], F32R) for n in names}
        g1h, g1l = st.sb("g1h", [P, KT, P], F32R), st.sb("g1l", [P, KT, P], F32R)
        g2 = st.sb("g2", [P, D])
        ld_p, ld_f, nw = st.sb("ld_p", [P, KT]), st.sb("ld_f", [P, NH]), st.sb("nw", [P, KT])
        eps = st.sb("eps", [P, 1])
        pair_decay = st.sb("pair_decay", [P, NH, P])
        q_decay = st.sb("q_decay", [P, KT, P])
        k_decay16, k_decay = st.sb("k_decay16", [P, NH]), st.sb("k_decay", [P, D])
        c_decay = st.sb("c_decay", [P, KT])
        xh, xl = st.sb("xh", [P, KT, CH], F32R), st.sb("xl", [P, KT, CH], F32R)
        qt, qd = st.sb("qt", [P, KT, CH]), st.sb("qd", [P, KT, CH])
        qblk = st.sb("qblk", [P, 2, KT, HPG, P])
        kt_, kd = st.sb("kt", [P, KT, CH]), st.sb("kd", [P, KT, TT, P])
        v = st.sb("v", [P, TT, D])
        gk, sig = st.sb("gk", [P, CH]), st.sb("sig", [P, KT, CH])
        dec = st.sb("dec", [P, 3, HPG, P])
        state, fresh = st.sb("state", [P, KT, P]), st.sb("fresh", [P, P])
        og, sq = sig, qd
        ogh, ogl = st.sb("ogh", [P, KT, CH], F32R), st.sb("ogl", [P, KT, CH], F32R)
        root, inv, tmp = gk, st.sb("inv", [P, CH]), st.sb("tmp", [P, CH])
        y = st.sb("y", [P, KT, CH])
        order = ("q", "k", "v", "g1", "o")
        pieces = {n: [(w_d[n][k * P:(k + 1) * P, :], wh[n][:, k, :], wl[n][:, k, :]) for k in range(KT)] for n in names}
        pieces["g1"] = [(wg1_d[k * P:(k + 1) * P, :], g1h[:, k, 0:HD], g1l[:, k, 0:HD]) for k in range(KT)]
        ws = WeightSplit(st, D, [p for n in order for p in pieces[n]],
                         stage=[y[:, m, :] for m in range(KT)] + [
                             kd[:, g].rearrange("p t f -> p (t f)") for g in range(KT)])
        ring, upd, o = st.ps("ring", [P, BANKS, CH]), st.ps("upd", [P, CH]), st.ps("o", [P, KT, CH])
        mean_sq = upd
        s_in, zeroed, expd, masked = st.sem("s_in"), st.sem("zeroed"), st.sem("expd"), st.sem("masked")
        blk_zeroed, g2_in = st.sem("blk_zeroed"), st.sem("g2_in")
        x_in, r_in = st.sem("x_in"), st.sem("r_in")
        made, taken = st.sem("made"), {e: st.sem(f"taken_{e}") for e in ("act", "dve")}
        qd_ready, qblk_ready = st.sem("qd_ready"), st.sem("qblk_ready")
        o_made, updated, fresh_ready, state_ready = (st.sem(n) for n in ("o_made", "updated", "fresh_ready", "state_ready"))
        gated, squared, ms_made = st.sem("gated"), st.sem("squared"), st.sem("ms_made")
        root_ready, newton = st.sem("root_ready"), st.sem("newton")
        normed, hi_ready, lo_ready = st.sem("normed"), st.sem("hi_ready"), st.sem("lo_ready")
        stored = st.sem("stored")
        block = st.block()
        LINKS = 5
        rg = Ring()

        def bank(kind, c, n=0):
            return ring[:, rg.at[kind, c, n] % BANKS, :]

        def wait_taken(eng, kind, c, n=0):
            e, count = rg.taken(kind, c, n)
            eng.wait_ge(taken[e], count)

        def arrived(eng, kind, c, n=0):
            eng.wait_ge(made, rg.made(kind, c, n))
            return bank(kind, c, n)

        @block.sync
        def _(sp):
            for dst, src in ((cst, cst_d), (ld_p, decay_p_d), (ld_f, decay_f_d), (nw, norm_w_d)):
                sp.dma_start(dst[:], src).then_inc(s_in, 16)
            for j in range(KT):
                ws.load(sp, j)
            sp.wait_ge(zeroed, 1)
            sp.dma_start(g2[0:HD, :], wg2_d).then_inc(g2_in, 16)
            for c in range(NCH):
                if c:
                    sp.wait_ge(made, rg.made("gk", c - 1))
                sp.dma_start(xh[:].bitcast(F32), tok(feat(xh_d), c)).then_inc(x_in, 16)
                sp.dma_start(xl[:].bitcast(F32), tok(feat(xl_d), c)).then_inc(x_in, 16)
                if c == 0:
                    for j in range(KT, len(ws.pieces)):
                        ws.load(sp, j)
                    ws.wait(sp)
                else:
                    wait_taken(sp, "out", c - 1, KT - 1)
                    sp.dma_start(tok(feat(out_d), c - 1), y[:]).then_inc(stored, 16)
                    sp.wait_ge(stored, c * 16)
                sp.dma_start(y[:], tok(feat(resid_d), c)).then_inc(r_in, 16)
            wait_taken(sp, "out", NCH - 1, KT - 1)
            sp.dma_start(tok(feat(out_d), NCH - 1), y[:]).then_inc(stored, 16)
            sp.wait_ge(stored, NCH * 16)

        @block.tensor
        def _(pe):
            def slot(kind, c, n=0):
                freed = rg.freed(kind, c, n)
                if freed:
                    wait_taken(pe, *freed)
                return bank(kind, c, n)

            def projected(kind, c, n, w, x_first=False):
                out, s = slot(kind, c, n), slice(n * P, (n + 1) * P)
                for k in range(KT):
                    edge = (k == 0, k == KT - 1)
                    if x_first:
                        last = three_passes(pe, out, xh[:, k, s], xl[:, k, s], wh[w][:, k, :], wl[w][:, k, :], *edge)
                    else:
                        last = three_passes(pe, out, wh[w][:, k, s], wl[w][:, k, s], xh[:, k, :], xl[:, k, :], *edge)
                last.then_inc(made, 1)

            def mean_squares(c):
                pe.wait_ge(squared, c + 1)
                pe.wait_ge(fresh_ready, (c + 1) * NI)
                for g in range(KT):
                    last = pe.matmul(mean_sq[g * HD:(g + 1) * HD, :], msel, sq[:, g, :], start=True, stop=True,
                                     skip_group_check=True)
                last.then_inc(ms_made, 1)

            def spread_inverses(c):
                pe.wait_ge(newton, (c + 1) * LINKS)
                for g in range(KT):
                    pe.matmul(slot("spread", c, g), spread[:, g * P:(g + 1) * P], inv[:], start=True,
                              stop=True).then_inc(made, 1)

            def output(c):
                ws.wait(pe)
                pe.wait_ge(lo_ready, (c + 1) * KT)
                for m in range(KT):
                    out, s = slot("out", c, m), slice(m * P, (m + 1) * P)
                    for k in range(KT):
                        last = three_passes(pe, out, wh["o"][:, k, s], wl["o"][:, k, s], ogh[:, k, :], ogl[:, k, :],
                                            k == 0, k == KT - 1)
                    last.then_inc(made, 1)

            def score(c, i):
                t, g = divmod(i, KT)
                pe.wait_ge(qblk_ready, c * NI + i + 1)
                pe.matmul(slot("score", c, i), kt_[:, g, t * P:(t + 1) * P],
                          qblk[:, t % 2, g].rearrange("p h c -> p (h c)"), start=True, stop=True).then_inc(made, 1)

            def attend(c, i):
                t, g = divmod(i, KT)
                s = slice(t * P, (t + 1) * P)
                if c * NI + i >= KT:
                    pe.wait_ge(state_ready, c * NI + i + 1 - KT)
                wait_taken(pe, "score", c, i)
                if i == 0:
                    pe.wait_ge(qd_ready, (c + 1) * KT)
                    if c:
                        pe.wait_ge(gated, c)
                        pe.wait_ge(newton, c * LINKS)
                    wait_taken(pe, "v", c, TT - 1)
                pe.matmul(o[:, g, s], state[:, g, :], qd[:, g, s], start=True, stop=False, skip_group_check=True)
                for h in range(HPG):
                    f = (g * HPG + h) * HD
                    last = pe.matmul(o[h * HD:(h + 1) * HD, g, s], v[:, t, f:f + HD], dec[:, i % 3, h, :],
                                     start=False, stop=True, skip_group_check=True)
                last.then_inc(o_made, 1)
                if t == 0:
                    wait_taken(pe, "turn", c, g)
                if c * NI + i:
                    pe.wait_ge(fresh_ready, c * NI + i)
                pe.matmul(upd[:, 0:P], kd[:, g, t, :], v[:, t, g * P:(g + 1) * P], start=True,
                          stop=True).then_inc(updated, 1)

            pe.wait_ge(s_in, 4 * 16)
            pe.wait_ge(g2_in, 16)
            pe.wait_ge(zeroed, 5)
            for c in range(NCH):
                pe.wait_ge(x_in, c * 32 + 32)
                ws.wait(pe, KT)
                for m in range(KT):
                    projected("q", c, m, "q")
                if c:
                    mean_squares(c - 1)
                ws.wait(pe, 2 * KT)
                for m in range(KT):
                    projected("k", c, m, "k")
                if c:
                    spread_inverses(c - 1)
                ws.wait(pe, 3 * KT)
                for t in range(TT):
                    projected("v", c, t, "v", True)
                if c:
                    output(c - 1)
                out = slot("gk", c)
                ws.wait(pe, 4 * KT)
                for k in range(KT):
                    last = three_passes(pe, out, g1h[:, k, :], g1l[:, k, :], xh[:, k, :], xl[:, k, :], k == 0, k == KT - 1)
                last.then_inc(made, 1)
                for g in range(KT):
                    out = slot("gate", c, g)
                    if g == 0:
                        wait_taken(pe, "gk", c)
                    pe.matmul(out, g2[:, g * P:(g + 1) * P], gk[:], start=True, stop=True).then_inc(made, 1)
                for g in range(KT):
                    out = slot("turn", c, g)
                    wait_taken(pe, "k", c, g)
                    for t in range(TT):
                        last = pe.transpose(out[:, t * P:(t + 1) * P], kt_[:, g, t * P:(t + 1) * P], ident)
                    last.then_inc(made, 1)
                for i in range(NI):
                    score(c, i)
                    if i >= 2:
                        attend(c, i - 2)
                attend(c, NI - 2)
                attend(c, NI - 1)
            mean_squares(NCH - 1)
            spread_inverses(NCH - 1)
            output(NCH - 1)

        @block.scalar
        def _(act):
            def take(dst, fn, kind, c, n=0):
                act.activation(dst, arrived(act, kind, c, n), fn).then_inc(taken["act"], 1)

            def square(c):
                act.wait_ge(gated, c + 1)
                act.activation(sq[:], og[:], ACT.Square).then_inc(squared, 1)

            def take_root(c):
                act.wait_ge(ms_made, c + 1)
                act.activation(root[:], mean_sq[:], ACT.Sqrt, bias=eps[:, 0:1]).then_inc(root_ready, 1)

            def high(c):
                if c:
                    act.wait_ge(made, rg.made("out", c - 1, KT - 1))
                for g in range(KT):
                    act.wait_ge(normed, c * KT + g + 1)
                    act.activation(ogh[:, g, :], og[:, g, :], ACT.Copy).then_inc(hi_ready, 1)

            def split(names):
                for j, n in enumerate(order):
                    if n in names:
                        for k in range(KT):
                            ws.hi(act, j * KT + k)

            act.wait_ge(s_in, 4 * 16)
            for h in range(NH):
                act.activation(pair_decay[:, h, :], dist, ACT.Exp, scale=ld_f[:, h:h + 1]).then_inc(expd, 1)
            for g in range(KT):
                act.activation(q_decay[:, g, :], cpos, ACT.Exp, scale=ld_p[:, g:g + 1]).then_inc(expd, 1)
            act.activation(k_decay16[:], ld_f[:], ACT.Exp, scale=kpos).then_inc(expd, 1)
            act.activation(c_decay[:], ld_p[:], ACT.Exp, scale=float(P)).then_inc(expd, 1)
            act.wait_ge(zeroed, 5)
            split(("q", "k"))
            for c in range(NCH):
                if c:
                    square(c - 1)
                    act.wait_ge(qblk_ready, c * NI)
                    act.wait_ge(qd_ready, c * KT)
                for g in range(KT):
                    take(qt[:, g, :], ACT.Silu, "q", c, g)
                if c == 0:
                    split(("v", "g1"))
                else:
                    take_root(c - 1)
                    act.wait_ge(made, rg.made("score", c - 1, NI - 1))
                for g in range(KT):
                    take(kt_[:, g, :], ACT.Silu, "k", c, g)
                if c == 0:
                    split(("o",))
                else:
                    high(c - 1)
                    act.wait_ge(updated, c * NI)
                for t in range(TT):
                    take(v[:, t, :], ACT.Silu, "v", c, t)
                if c:
                    act.wait_ge(newton, c * LINKS)
                take(gk[:], ACT.Copy, "gk", c)
                if c:
                    act.wait_ge(lo_ready, c * KT)
                for g in range(KT):
                    take(sig[:, g, :], ACT.Sigmoid, "gate", c, g)
            square(NCH - 1)
            take_root(NCH - 1)
            high(NCH - 1)

        @block.vector
        def _(dve):
            def gated_output(c):
                wait_taken(dve, "gate", c, KT - 1)
                dve.wait_ge(o_made, (c + 1) * NI)
                dve.tensor_tensor(og[:], o[:], sig[:], ALU.mult).then_inc(gated, 1)

            def invert(c):
                dve.wait_ge(root_ready, c + 1)
                if c:
                    dve.wait_ge(made, rg.made("spread", c - 1, KT - 1))
                chain = Chain(dve, newton, c * LINKS)
                rsqrt_newton(dve, chain, inv[:], tmp[:], root[:], mean_sq[:], LN_EPS)
                assert chain.n == LINKS

            def normalize(c):
                for g in range(KT):
                    dve.scalar_tensor_tensor(out=og[:, g, :], in0=og[:, g, :], scalar=nw[:, g:g + 1],
                                             in1=arrived(dve, "spread", c, g), op0=ALU.mult, op1=ALU.mult
                                             ).then_inc(normed, 1)
                    dve.wait_ge(normed, c * KT + g + 1)
                    dve.sem_inc(taken["dve"], 1)
                for g in range(KT):
                    dve.wait_ge(hi_ready, c * KT + g + 1)
                    dve.tensor_tensor(ogl[:, g, :], og[:, g, :], ogh[:, g, :].bitcast(F32),
                                      ALU.subtract).then_inc(lo_ready, 1)

            def add_output(c):
                dve.wait_ge(r_in, c * 16 + 16)
                for m in range(KT):
                    dve.tensor_tensor(y[:, m, :], y[:, m, :], arrived(dve, "out", c, m), ALU.add
                                      ).then_inc(taken["dve"], 1)

            def decay(c, i):
                t, g = divmod(i, KT)
                if c * NI + i >= 3:
                    dve.wait_ge(o_made, c * NI + i - 2)
                dve.tensor_tensor(dec[:, i % 3], arrived(dve, "score", c, i).rearrange("p (h c) -> p h c", c=P),
                                  pair_decay[:, g * HPG:(g + 1) * HPG, :], ALU.mult).then_inc(taken["dve"], 1)

            def advance(c, i):
                t, g = divmod(i, KT)
                n = c * NI + i
                dve.wait_ge(updated, n + 1)
                if n:
                    dve.wait_ge(state_ready, n)
                dve.tensor_tensor(fresh[:], upd[:, 0:P], diag, ALU.mult).then_inc(fresh_ready, 1)
                dve.wait_ge(fresh_ready, n + 1)
                dve.scalar_tensor_tensor(out=state[:, g, :], in0=state[:, g, :], scalar=c_decay[:, g:g + 1],
                                         in1=fresh[:], op0=ALU.mult, op1=ALU.add).then_inc(state_ready, 1)

            dve.memset(g2[:], 0.0).then_inc(zeroed, 1)
            dve.memset(g1h[:].bitcast(F32), 0.0).then_inc(zeroed, 1)
            dve.memset(g1l[:].bitcast(F32), 0.0).then_inc(zeroed, 1)
            dve.memset(state[:], 0.0).then_inc(zeroed, 1)
            dve.memset(eps[:], LN_EPS).then_inc(zeroed, 1)
            dve.wait_ge(expd, NH + KT + 2)
            for g in range(KT):
                s = slice(g * HPG, (g + 1) * HPG)
                dve.tensor_tensor(pair_decay[:, s, :], pair_decay[:, s, :],
                                  causal.rearrange("p (a c) -> p a c", a=1).to_broadcast([P, HPG, P]),
                                  ALU.mult).then_inc(masked, 1)
            dve.tensor_copy(k_decay[:].rearrange("p (h d) -> p h d", d=HD),
                            k_decay16[:].rearrange("p (h a) -> p h a", a=1).to_broadcast([P, NH, HD])).then_inc(masked, 1)
            dve.wait_ge(masked, KT + 1)
            for c in range(NCH):
                if c:
                    invert(c - 1)
                    dve.wait_ge(ms_made, c)
                for g in range(KT):
                    wait_taken(dve, "q", c, g)
                    dve.tensor_tensor(qd[:, g, :].rearrange("p (t c) -> p t c", c=P),
                                      qt[:, g, :].rearrange("p (t c) -> p t c", c=P),
                                      q_decay[:, g:g + 1, :].to_broadcast([P, TT, P]), ALU.mult).then_inc(qd_ready, 1)
                if c:
                    normalize(c - 1)
                    add_output(c - 1)
                else:
                    ws.wait(dve)
                for g in range(KT):
                    if c and g == 0:
                        dve.wait_ge(updated, c * NI)
                    dve.tensor_tensor(kd[:, g, :, :], arrived(dve, "turn", c, g).rearrange("p (t f) -> p t f", f=P),
                                      k_decay[:, g * P:(g + 1) * P].rearrange("p (a f) -> p a f", a=1).to_broadcast([P, TT, P]),
                                      ALU.mult).then_inc(taken["dve"], 1)
                for i in range(NI):
                    decay(c, i)
                    if i >= 2:
                        advance(c, i - 2)
                advance(c, NI - 2)
                advance(c, NI - 1)
                gated_output(c)
            invert(NCH - 1)
            normalize(NCH - 1)
            add_output(NCH - 1)

        @block.gpsimd
        def _(pool):
            pool.wait_ge(zeroed, 5)
            for j in range(2 * KT):
                ws.lo(pool, j)
            pool.memset(qblk[:], 0.0).then_inc(blk_zeroed, 1)
            for j in range(2 * KT, len(ws.pieces)):
                ws.lo(pool, j)
            pool.wait_ge(blk_zeroed, 1)
            ws.wait(pool)
            for c in range(NCH):
                for i in range(NI):
                    t, g = divmod(i, KT)
                    if t == 0:
                        wait_taken(pool, "q", c, g)
                    if c * NI + i >= 2 * KT:
                        pool.wait_ge(made, rg.made("score", *divmod(c * NI + i - 2 * KT, NI)))
                    for h in range(HPG):
                        s = slice(h * HD, (h + 1) * HD)
                        last = pool.tensor_copy(qblk[s, t % 2, g, h, :], qt[s, g, t * P:(t + 1) * P])
                    last.then_inc(qblk_ready, 1)


def lightning_constants():
    s, c = np.arange(P)[:, None], np.arange(P)[None, :]
    p = np.arange(P)[:, None]
    parts = [np.maximum(c - s, 0), c >= s, np.broadcast_to(c + 1, (P, P)), p // HD == c // HD,
             (p // HD == np.arange(HD)[None, :] % HPG) / HD]
    parts += [p == g * HD + c // HD for g in range(KT)]
    parts += [p == c, P - 1 - p]
    return np.concatenate([np.asarray(a, np.float32) for a in parts], axis=1)


def build(nc, i, out):
    def dram(name, shape):
        return nc.dram_tensor(name, shape, F32).ap()

    xh_d, xl_d = dram("xn_hi", [D, T]), dram("xn_lo", [D, T])
    qh_d, ql_d, kh_d, kl_d = (dram(n, [D, T]) for n in ("q_hi", "q_lo", "k_hi", "k_lo"))
    v_d, att_d = dram("v", [T, D]), dram("att", [D, T])
    sum_d, inv_d = dram("softmax_sums", [NH, T]), dram("softmax_inverses", [NH, T])
    ternary = [(i[n], dram(f"{n}_ternary", list(i[n].shape)), dram(f"{n}_sums", [P])) for n in ("w1", "w2", "w3")]
    y0_d, x1_d, y1_d = dram("y0", [D, T]), dram("x1", [D, T]), dram("y1", [D, T])
    zh_d, zl_d = dram("zn_hi", [D, T]), dram("zn_lo", [D, T])

    aq_d, ak_d = dram("alibi_q_rounded", [NH * 4, T]), dram("alibi_k_rounded", [NH * 6, T])
    normed_qkv_stage(nc, i["Wqkv"], i["bqk"], i["bv"], i["x"], xh_d, xl_d, qh_d, ql_d, kh_d, kl_d, v_d,
                     ((i["alibi_q"], aq_d), (i["alibi_k"], ak_d)))
    with Stage(nc, "exp0w") as st:
        w = ExpertWeights(st, i["W0a"], i["W0b"], i["L0_Wo"])
        attention_stage(nc, i["att_cst"], aq_d, ak_d, qh_d, ql_d, kh_d, kl_d, v_d, att_d, sum_d,
                        w.pieces, ternary)
        expert_stage(nc, "exp0", 0, ACT.Gelu, w, False, i["Wg"], i["bias0"], xh_d, xl_d, i["x"], y0_d,
                     att_d, sum_d, inv_d)
    with Stage(nc, "exp1w") as st:
        w = ExpertWeights(st, i["W1a"], i["W1b"])
        expert_stage(nc, "exp1", 1, ACT.Relu, w, True, i["Wg"], i["bias1"], xh_d, xl_d, y0_d, x1_d,
                     zh_d=zh_d, zl_d=zl_d)
    lightning_stage(nc, i["lin_cst"], {n: i[f"W{n}"] for n in "qkvo"}, i["Wg1"], i["Wg2"], i["decay_p"], i["decay_f"],
                    i["norm_w"], zh_d, zl_d, x1_d, y1_d)
    glu_stage(nc, *(q for _, q, _ in ternary), zh_d, zl_d, y1_d, out)


def kernel(**inputs):
    import numpy as _np
    import concourse.bacc as _bacc
    from concourse import mybir as _mybir
    from concourse.bass_utils import run_bass_kernel_spmd as _run

    a = {n: _np.asarray(v) for n, v in inputs.items()}

    def by_partition(v):
        return v.reshape(-1, P).T

    att_cst, alibi_q, alibi_k = attention_constants()
    bqkv, ld = a["L0_attn_bqkv"], a["L1_attn_log_decay"]
    none = _np.zeros(D, _np.float32)
    arrays = {
        "x": a["L0_attn_x"][0].T, "Wqkv": a["L0_attn_Wqkv"], "bqk": by_partition(bqkv[:2 * D]),
        "bv": _np.broadcast_to(bqkv[2 * D:], (P, D)), "L0_Wo": a["L0_attn_Wo"],
        "Wg": a["L0_ffn_Wg"].reshape(2, KT, P).transpose(2, 0, 1),
        "W0a": a["L0_ffn_W0a"].T, "W0b": a["L0_ffn_W0b"].T, "W1a": a["L0_ffn_W1a"].T, "W1b": a["L0_ffn_W1b"].T,
        "bias0": _np.concatenate([by_partition(a[n]) for n in ("L0_ffn_b0a", "L0_ffn_b0b", "L0_attn_bo")], 1),
        "bias1": _np.concatenate([by_partition(v) for v in (a["L0_ffn_b1a"], a["L0_ffn_b1b"], none)], 1),
        "Wq": a["L1_attn_Wq"], "Wk": a["L1_attn_Wk"], "Wv": a["L1_attn_Wv"], "Wo": a["L1_attn_Wo"],
        "Wg1": a["L1_attn_Wg1"], "Wg2": a["L1_attn_Wg2"], "norm_w": by_partition(a["L1_attn_norm_w"]),
        "decay_p": _np.repeat(ld.reshape(KT, HPG).T, HD, axis=0), "decay_f": _np.broadcast_to(ld, (P, NH)),
        "w1": a["L1_ffn_w1"].T, "w2": a["L1_ffn_w2"].T, "w3": a["L1_ffn_w3"].T,
        "att_cst": att_cst, "alibi_q": alibi_q, "alibi_k": alibi_k, "lin_cst": lightning_constants(),
    }
    nc = _bacc.Bacc("TRN2", target_bir_lowering=False, num_devices=1)
    given, aps = {}, {}
    for name, v in arrays.items():
        given[f"in_{name}"] = _np.ascontiguousarray(v)
        aps[name] = nc.dram_tensor(f"in_{name}", v.shape, _mybir.dt.from_np(v.dtype), kind="ExternalInput").ap()
    out = nc.dram_tensor("out", (D, T), F32, kind="ExternalOutput").ap()
    build(nc, aps, out)
    r = _run(nc, [given], core_ids=[0])
    return r.results[0]["out"].T.reshape(1, T, D)
```
